# Optimizing a Trainium2 kernel written in Bass

```python
import numpy as np
import jax
import jax.numpy as jnp

def _softmax(x, axis=-1):
    return jax.nn.softmax(x, axis=axis)

def _gelu(x):
    return jax.nn.gelu(x, approximate=True)

def _silu(x):
    return jax.nn.silu(x)

def _sigmoid(x):
    return jax.nn.sigmoid(x)

def _layernorm(x, axis=-1, eps=1e-05):
    m = jnp.mean(x, axis=axis, keepdims=True)
    v = jnp.var(x, axis=axis, keepdims=True)
    return (x - m) / jnp.sqrt(v + eps)

def _scatter_add(tgt, idx, src, axis=0):
    return tgt.at[idx].add(src)

def _segment_sum(src, seg, n):
    return jax.ops.segment_sum(src, seg, n)
kernel_name = 'mk_early_fusion_d1_tok_img768_r4_9bbbba'

def setup_inputs(seed: int=0):
    np.random.seed(seed)
    _w = jnp.asarray

    def _rec_inputs():
        import jax
        import jax.numpy as jnp
        _rk = jax.random.key(seed)
        x = -9.30917e-05 + 1.0002 * jax.random.normal(jax.random.fold_in(_rk, 1), (32, 3, 224, 224), jnp.float32)
        txt = -0.000192023 + 1.00029 * jax.random.normal(jax.random.fold_in(_rk, 2), (32, 77, 192), jnp.float32)
        return (x, txt)
    x, txt = _rec_inputs()

    def _L0_tok_setup():
        import jax, jax.numpy as jnp
        import numpy as np
        PATCH = 16
        EPS = 1e-05

        def _shift(x, pad_spec):
            l, r, t, b = pad_spec
            H, W = (x.shape[2], x.shape[3])
            xp = jnp.pad(x, ((0, 0), (0, 0), (max(t, 0), max(b, 0)), (max(l, 0), max(r, 0))))
            h0 = -t if t < 0 else 0
            w0 = -l if l < 0 else 0
            return xp[:, :, h0:h0 + H, w0:w0 + W]
        key = jax.random.key(seed)
        k1, k2 = jax.random.split(key)
        B, C, H, Wd = (32, 3, 224, 224)
        patch_dim = PATCH * PATCH * 5 * C
        dim = 192
        x = jax.random.normal(k1, (B, C, H, Wd), dtype=jnp.float32)
        ln_gamma = jnp.ones((patch_dim,), dtype=jnp.float32)
        ln_beta = jnp.zeros((patch_dim,), dtype=jnp.float32)
        W = jax.random.normal(k2, (patch_dim, dim), dtype=jnp.float32) * patch_dim ** (-0.5)
        b = jnp.zeros((dim,), dtype=jnp.float32)
        return {'x': x, 'ln_gamma': ln_gamma, 'ln_beta': ln_beta, 'W': W, 'b': b}
    _L0_tok_all = _L0_tok_setup()
    _L0_tok_in = {k: v for k, v in _L0_tok_all.items() if k in ('ln_gamma', 'ln_beta', 'W', 'b')}
    del _L0_tok_all

    def _L0_attn_setup():
        import jax, jax.numpy as jnp
        import numpy as np
        D_MODEL = 192
        N_HEAD = 8
        D_QKV = 96
        D_FF = 768
        MAX_REL = 100
        NUM_EMB = 2 * MAX_REL - 1
        T, B = (256, 4)

        def _layer_norm(x, g, b):
            m = jnp.mean(x, axis=-1, keepdims=True)
            v = jnp.var(x, axis=-1, keepdims=True)
            return g * (x - m) * jax.lax.rsqrt(v + 1e-05) + b

        def _rel_pos_logits(qp, rel_emb):
            length = qp.shape[0]
            emb = jax.lax.stop_gradient(rel_emb)
            pad_len = max(length - MAX_REL, 0)
            start = max(MAX_REL - length, 0)
            emb = jnp.pad(emb, ((0, 0), (pad_len, pad_len), (0, 0), (0, 0)))
            used = jax.lax.dynamic_slice_in_dim(emb, start, 2 * length - 1, axis=1)[..., 0]
            q = qp.reshape(length, -1, N_HEAD, D_QKV)
            logits = jnp.einsum('lbhd,hmd->lbhm', q, used)
            logits = logits.reshape(length, -1, 2 * length - 1)
            if length > MAX_REL:
                p = length - MAX_REL
                logits = logits.at[:, :, :p].add(-100000000.0)
                logits = logits.at[:, :, -p:].add(-100000000.0)
            bh = logits.shape[1]
            x = jnp.pad(logits, ((0, 0), (0, 0), (0, 1)))
            x = jnp.transpose(x, (1, 0, 2)).reshape(bh, length * 2 * length)
            x = jnp.pad(x, ((0, 0), (0, length - 1)))
            x = x.reshape(bh, length + 1, 2 * length - 1)
            return x[:, :length, length - 1:]
        key = jax.random.key(seed)
        ks = jax.random.split(key, 8)

        def n(k, shape, scale=1.0):
            return jax.random.normal(k, shape, dtype=jnp.float32) * scale
        return dict(src=n(ks[0], (T, B, D_MODEL)), w_q=n(ks[1], (N_HEAD, D_MODEL, D_QKV), 0.05), w_k=n(ks[2], (N_HEAD, D_MODEL, D_QKV), 0.05), w_v=n(ks[3], (N_HEAD, D_MODEL, D_QKV), 0.05), w_o=n(ks[4], (N_HEAD, D_QKV, D_MODEL), 0.05), rel_emb=n(ks[5], (N_HEAD, NUM_EMB, D_QKV, 1), D_QKV ** (-0.5)), lin1_w=n(ks[6], (D_FF, D_MODEL), 0.02), lin1_b=jnp.zeros((D_FF,), jnp.float32), lin2_w=n(ks[7], (D_MODEL, D_FF), 0.02), lin2_b=jnp.zeros((D_MODEL,), jnp.float32), ln1_g=jnp.ones((D_MODEL,), jnp.float32), ln1_b=jnp.zeros((D_MODEL,), jnp.float32), ln2_g=jnp.ones((D_MODEL,), jnp.float32), ln2_b=jnp.zeros((D_MODEL,), jnp.float32))
    _L0_attn_all = _L0_attn_setup()
    _L0_attn_in = {k: v for k, v in _L0_attn_all.items() if k in ('w_q', 'w_k', 'w_v', 'w_o', 'rel_emb', 'lin1_w', 'lin1_b', 'lin2_w', 'lin2_b', 'ln1_g', 'ln1_b', 'ln2_g', 'ln2_b')}
    del _L0_attn_all

    def _L0_ffn_setup():
        import jax, jax.numpy as jnp
        import numpy as np
        B, S, D = (2, 256, 192)
        I = 96
        E = 8
        G = 4
        TOPK_GROUPS = 2
        K = 2
        ROUTE_SCALE = 1.0
        ALPHA, LIMIT = (1.702, 7.0)

        def swiglu(h):
            xg = jnp.minimum(h[..., ::2], LIMIT)
            xl = jnp.clip(h[..., 1::2], -LIMIT, LIMIT)
            return xg * jax.nn.sigmoid(ALPHA * xg) * (xl + 1.0)

        def gate(x, gate_w, gate_b):
            scores = jax.nn.softmax(jnp.einsum('td,ed->te', x, gate_w).astype(jnp.float32), axis=-1)
            original_scores = scores
            s = scores + gate_b
            T = x.shape[0]
            sg = s.reshape(T, G, E // G)
            group_scores = jnp.sum(jax.lax.top_k(sg, 2)[0], axis=-1)
            _, gidx = jax.lax.top_k(group_scores, TOPK_GROUPS)
            keep = jnp.any(jax.nn.one_hot(gidx, G, dtype=jnp.bool_), axis=1)
            sg = jnp.where(keep[:, :, None], sg, -jnp.inf)
            s = sg.reshape(T, E)
            _, idx = jax.lax.top_k(s, K)
            w = jnp.take_along_axis(original_scores, idx, axis=1) * ROUTE_SCALE
            return (w.astype(x.dtype), idx)

        def expert_ffn(x, W1, B1, W3, B3, W2, B2):
            h1 = jnp.einsum('td,edh->teh', x, W1) + B1
            h3 = jnp.einsum('td,edh->teh', x, W3) + B3
            g = swiglu(h1 * h3)
            return jnp.einsum('tei,eid->ted', g, W2) + B2

        def shared_ffn(x, Ws1, Bs1, Ws3, Bs3, Ws2, Bs2):
            h = (x @ Ws1 + Bs1) * (x @ Ws3 + Bs3)
            return swiglu(h) @ Ws2 + Bs2
        key = jax.random.key(seed)
        ks = jax.random.split(key, 16)
        sc = 0.02
        inp = {'x': jax.random.normal(ks[0], (B, S, D), jnp.float32), 'gate_w': jax.random.normal(ks[1], (E, D), jnp.float32) * sc, 'gate_b': jax.random.normal(ks[2], (E,), jnp.float32) * sc, 'W1': jax.random.normal(ks[3], (E, D, 2 * I), jnp.float32) * sc, 'B1': jax.random.normal(ks[4], (E, 2 * I), jnp.float32) * sc, 'W3': jax.random.normal(ks[5], (E, D, 2 * I), jnp.float32) * sc, 'B3': jax.random.normal(ks[6], (E, 2 * I), jnp.float32) * sc, 'W2': jax.random.normal(ks[7], (E, I, D), jnp.float32) * sc, 'B2': jax.random.normal(ks[8], (E, D), jnp.float32) * sc, 'Ws1': jax.random.normal(ks[9], (D, 2 * I), jnp.float32) * sc, 'Bs1': jax.random.normal(ks[10], (2 * I,), jnp.float32) * sc, 'Ws3': jax.random.normal(ks[11], (D, 2 * I), jnp.float32) * sc, 'Bs3': jax.random.normal(ks[12], (2 * I,), jnp.float32) * sc, 'Ws2': jax.random.normal(ks[13], (I, D), jnp.float32) * sc, 'Bs2': jax.random.normal(ks[14], (D,), jnp.float32) * sc}
        return inp
    _L0_ffn_all = _L0_ffn_setup()
    _L0_ffn_in = {k: v for k, v in _L0_ffn_all.items() if k in ('gate_w', 'gate_b', 'W1', 'B1', 'W3', 'B3', 'W2', 'B2', 'Ws1', 'Bs1', 'Ws3', 'Bs3', 'Ws2', 'Bs2')}
    del _L0_ffn_all
    return {'x': x, 'txt': txt, 'L0_tok_ln_gamma': _L0_tok_in['ln_gamma'], 'L0_tok_ln_beta': _L0_tok_in['ln_beta'], 'L0_tok_W': _L0_tok_in['W'], 'L0_tok_b': _L0_tok_in['b'], 'L0_attn_w_q': _L0_attn_in['w_q'], 'L0_attn_w_k': _L0_attn_in['w_k'], 'L0_attn_w_v': _L0_attn_in['w_v'], 'L0_attn_w_o': _L0_attn_in['w_o'], 'L0_attn_rel_emb': _L0_attn_in['rel_emb'], 'L0_attn_lin1_w': _L0_attn_in['lin1_w'], 'L0_attn_lin1_b': _L0_attn_in['lin1_b'], 'L0_attn_lin2_w': _L0_attn_in['lin2_w'], 'L0_attn_lin2_b': _L0_attn_in['lin2_b'], 'L0_attn_ln1_g': _L0_attn_in['ln1_g'], 'L0_attn_ln1_b': _L0_attn_in['ln1_b'], 'L0_attn_ln2_g': _L0_attn_in['ln2_g'], 'L0_attn_ln2_b': _L0_attn_in['ln2_b'], 'L0_ffn_gate_w': _L0_ffn_in['gate_w'], 'L0_ffn_gate_b': _L0_ffn_in['gate_b'], 'L0_ffn_W1': _L0_ffn_in['W1'], 'L0_ffn_B1': _L0_ffn_in['B1'], 'L0_ffn_W3': _L0_ffn_in['W3'], 'L0_ffn_B3': _L0_ffn_in['B3'], 'L0_ffn_W2': _L0_ffn_in['W2'], 'L0_ffn_B2': _L0_ffn_in['B2'], 'L0_ffn_Ws1': _L0_ffn_in['Ws1'], 'L0_ffn_Bs1': _L0_ffn_in['Bs1'], 'L0_ffn_Ws3': _L0_ffn_in['Ws3'], 'L0_ffn_Bs3': _L0_ffn_in['Bs3'], 'L0_ffn_Ws2': _L0_ffn_in['Ws2'], 'L0_ffn_Bs2': _L0_ffn_in['Bs2']}

def reference(x, txt, L0_tok_ln_gamma, L0_tok_ln_beta, L0_tok_W, L0_tok_b, L0_attn_w_q, L0_attn_w_k, L0_attn_w_v, L0_attn_w_o, L0_attn_rel_emb, L0_attn_lin1_w, L0_attn_lin1_b, L0_attn_lin2_w, L0_attn_lin2_b, L0_attn_ln1_g, L0_attn_ln1_b, L0_attn_ln2_g, L0_attn_ln2_b, L0_ffn_gate_w, L0_ffn_gate_b, L0_ffn_W1, L0_ffn_B1, L0_ffn_W3, L0_ffn_B3, L0_ffn_W2, L0_ffn_B2, L0_ffn_Ws1, L0_ffn_Bs1, L0_ffn_Ws3, L0_ffn_Bs3, L0_ffn_Ws2, L0_ffn_Bs2):
    import jax
    import jax.numpy as jnp

    def _L0_tok_ref(x, ln_gamma, ln_beta, W, b):
        import jax, jax.numpy as jnp
        import numpy as np
        PATCH = 16
        EPS = 1e-05

        def _shift(x, pad_spec):
            l, r, t, b = pad_spec
            H, W = (x.shape[2], x.shape[3])
            xp = jnp.pad(x, ((0, 0), (0, 0), (max(t, 0), max(b, 0)), (max(l, 0), max(r, 0))))
            h0 = -t if t < 0 else 0
            w0 = -l if l < 0 else 0
            return xp[:, :, h0:h0 + H, w0:w0 + W]
        shifts = [(1, -1, 0, 0), (-1, 1, 0, 0), (0, 0, 1, -1), (0, 0, -1, 1)]
        xs = jnp.concatenate([x] + [_shift(x, s) for s in shifts], axis=1)
        B, C5, H, Wd = xs.shape
        h, w = (H // PATCH, Wd // PATCH)
        t = xs.reshape(B, C5, h, PATCH, w, PATCH)
        t = t.transpose(0, 2, 4, 3, 5, 1)
        t = t.reshape(B, h * w, PATCH * PATCH * C5)
        mu = jnp.mean(t, axis=-1, keepdims=True)
        var = jnp.var(t, axis=-1, keepdims=True)
        tn = (t - mu) * jax.lax.rsqrt(var + EPS) * ln_gamma + ln_beta
        return jnp.einsum('bnp,pd->bnd', tn, W) + b

    def _L0_attn_ref(src, w_q, w_k, w_v, w_o, rel_emb, lin1_w, lin1_b, lin2_w, lin2_b, ln1_g, ln1_b, ln2_g, ln2_b):
        import jax, jax.numpy as jnp
        import numpy as np
        D_MODEL = 192
        N_HEAD = 8
        D_QKV = 96
        D_FF = 768
        MAX_REL = 100
        NUM_EMB = 2 * MAX_REL - 1
        T, B = (256, 4)

        def _layer_norm(x, g, b):
            m = jnp.mean(x, axis=-1, keepdims=True)
            v = jnp.var(x, axis=-1, keepdims=True)
            return g * (x - m) * jax.lax.rsqrt(v + 1e-05) + b

        def _rel_pos_logits(qp, rel_emb):
            length = qp.shape[0]
            emb = jax.lax.stop_gradient(rel_emb)
            pad_len = max(length - MAX_REL, 0)
            start = max(MAX_REL - length, 0)
            emb = jnp.pad(emb, ((0, 0), (pad_len, pad_len), (0, 0), (0, 0)))
            used = jax.lax.dynamic_slice_in_dim(emb, start, 2 * length - 1, axis=1)[..., 0]
            q = qp.reshape(length, -1, N_HEAD, D_QKV)
            logits = jnp.einsum('lbhd,hmd->lbhm', q, used)
            logits = logits.reshape(length, -1, 2 * length - 1)
            if length > MAX_REL:
                p = length - MAX_REL
                logits = logits.at[:, :, :p].add(-100000000.0)
                logits = logits.at[:, :, -p:].add(-100000000.0)
            bh = logits.shape[1]
            x = jnp.pad(logits, ((0, 0), (0, 0), (0, 1)))
            x = jnp.transpose(x, (1, 0, 2)).reshape(bh, length * 2 * length)
            x = jnp.pad(x, ((0, 0), (0, length - 1)))
            x = x.reshape(bh, length + 1, 2 * length - 1)
            return x[:, :length, length - 1:]
        Tq, Bq, _ = src.shape
        q = jnp.einsum('tbf,hfa->bhta', src, w_q)
        k = jnp.einsum('tbf,hfa->bhta', src, w_k)
        v = jnp.einsum('tbf,hfa->bhta', src, w_v)
        logits = jnp.einsum('bhqa,bhka->bhqk', q, k) / D_QKV ** 0.5
        qp = jnp.transpose(q, (2, 0, 1, 3)).reshape(Tq, Bq * N_HEAD, D_QKV)
        pos = _rel_pos_logits(qp, rel_emb).reshape(Bq, N_HEAD, Tq, Tq)
        logits = logits + pos
        probs = jax.nn.softmax(logits, axis=-1)
        o = jnp.einsum('bhqk,bhka->bhqa', probs, v)
        attn_out = jnp.einsum('bhta,haf->tbf', o, w_o)
        x = _layer_norm(src + attn_out, ln1_g, ln1_b)
        h = jax.nn.relu(x @ lin1_w.T + lin1_b)
        ff = h @ lin2_w.T + lin2_b
        return _layer_norm(x + ff, ln2_g, ln2_b)

    def _L0_ffn_ref(x, gate_w, gate_b, W1, B1, W3, B3, W2, B2, Ws1, Bs1, Ws3, Bs3, Ws2, Bs2):
        import jax, jax.numpy as jnp
        import numpy as np
        B, S, D = (2, 256, 192)
        I = 96
        E = 8
        G = 4
        TOPK_GROUPS = 2
        K = 2
        ROUTE_SCALE = 1.0
        ALPHA, LIMIT = (1.702, 7.0)

        def swiglu(h):
            xg = jnp.minimum(h[..., ::2], LIMIT)
            xl = jnp.clip(h[..., 1::2], -LIMIT, LIMIT)
            return xg * jax.nn.sigmoid(ALPHA * xg) * (xl + 1.0)

        def gate(x, gate_w, gate_b):
            scores = jax.nn.softmax(jnp.einsum('td,ed->te', x, gate_w).astype(jnp.float32), axis=-1)
            original_scores = scores
            s = scores + gate_b
            T = x.shape[0]
            sg = s.reshape(T, G, E // G)
            group_scores = jnp.sum(jax.lax.top_k(sg, 2)[0], axis=-1)
            _, gidx = jax.lax.top_k(group_scores, TOPK_GROUPS)
            keep = jnp.any(jax.nn.one_hot(gidx, G, dtype=jnp.bool_), axis=1)
            sg = jnp.where(keep[:, :, None], sg, -jnp.inf)
            s = sg.reshape(T, E)
            _, idx = jax.lax.top_k(s, K)
            w = jnp.take_along_axis(original_scores, idx, axis=1) * ROUTE_SCALE
            return (w.astype(x.dtype), idx)

        def expert_ffn(x, W1, B1, W3, B3, W2, B2):
            h1 = jnp.einsum('td,edh->teh', x, W1) + B1
            h3 = jnp.einsum('td,edh->teh', x, W3) + B3
            g = swiglu(h1 * h3)
            return jnp.einsum('tei,eid->ted', g, W2) + B2

        def shared_ffn(x, Ws1, Bs1, Ws3, Bs3, Ws2, Bs2):
            h = (x @ Ws1 + Bs1) * (x @ Ws3 + Bs3)
            return swiglu(h) @ Ws2 + Bs2
        inp_shape = x.shape
        xt = x.reshape(-1, D)
        w, idx = gate(xt, gate_w, gate_b)
        combine = jnp.einsum('tk,tke->te', w, jax.nn.one_hot(idx, E, dtype=w.dtype))
        per_expert = expert_ffn(xt, W1, B1, W3, B3, W2, B2)
        routed = jnp.einsum('ted,te->td', per_expert, combine)
        out = routed + shared_ffn(xt, Ws1, Bs1, Ws3, Bs3, Ws2, Bs2)
        return out.reshape(inp_shape)
    h = _L0_tok_ref(x, L0_tok_ln_gamma, L0_tok_ln_beta, L0_tok_W, L0_tok_b)
    h = jnp.concatenate([h, txt], axis=1)
    h = h + _L0_attn_ref(_layernorm(h, axis=-1), L0_attn_w_q, L0_attn_w_k, L0_attn_w_v, L0_attn_w_o, L0_attn_rel_emb, L0_attn_lin1_w, L0_attn_lin1_b, L0_attn_lin2_w, L0_attn_lin2_b, L0_attn_ln1_g, L0_attn_ln1_b, L0_attn_ln2_g, L0_attn_ln2_b)
    h = h + _L0_ffn_ref(_layernorm(h, axis=-1), L0_ffn_gate_w, L0_ffn_gate_b, L0_ffn_W1, L0_ffn_B1, L0_ffn_W3, L0_ffn_B3, L0_ffn_W2, L0_ffn_B2, L0_ffn_Ws1, L0_ffn_Bs1, L0_ffn_Ws3, L0_ffn_Bs3, L0_ffn_Ws2, L0_ffn_Bs2)
    return h

_drawn_inputs = setup_inputs


def setup_inputs(seed=0):
    import zlib

    import numpy as np

    out = dict(_drawn_inputs(seed))
    spreads = {'L0_tok_ln_gamma': (1.0, 0.2),
     'L0_tok_ln_beta': (0.0, 0.1),
     'L0_tok_b': (0.0, 0.1),
     'L0_attn_lin1_b': (0.0, 0.41),
     'L0_attn_lin2_b': (0.0, 0.1),
     'L0_attn_ln1_g': (1.0, 0.2),
     'L0_attn_ln1_b': (0.0, 0.1),
     'L0_attn_ln2_g': (1.0, 0.2),
     'L0_attn_ln2_b': (0.0, 0.1)}
    factors = {'L0_ffn_gate_w': 8.0,
     'L0_ffn_gate_b': 8.0,
     'L0_ffn_W1': 8.0,
     'L0_ffn_B1': 8.0,
     'L0_ffn_W3': 8.0,
     'L0_ffn_B3': 8.0,
     'L0_ffn_W2': 8.0,
     'L0_ffn_B2': 64.0,
     'L0_ffn_Ws1': 8.0,
     'L0_ffn_Bs1': 8.0,
     'L0_ffn_Ws3': 8.0,
     'L0_ffn_Bs3': 8.0,
     'L0_ffn_Ws2': 8.0,
     'L0_ffn_Bs2': 48.4}
    for name, (base, spread) in spreads.items():
        noise = np.random.default_rng([zlib.crc32(name.encode()), seed]).standard_normal(out[name].shape)
        drawn = base * np.exp(spread * noise) if base else spread * noise
        out[name] = jnp.asarray(drawn.astype(out[name].dtype))
    for name, factor in factors.items():
        out[name] = (out[name] * factor).astype(out[name].dtype)
    return out
```

```python
from contextlib import ExitStack

import concourse.bass as bass
from concourse import mybir

F32 = mybir.dt.float32
F32R = mybir.dt.float32r
ALU = mybir.AluOpType
ACT = mybir.ActivationFunctionType
AX = mybir.AxisListType

SEQ, NPATCH, NTXT, D = 32, 196, 77, 192
NTOK = NPATCH + NTXT
HEADS, DQ, DFF = 8, 96, 768
EXPERTS, INNER, GROUPS = 8, 96, 4
EPS = 1e-5
IMG, PATCH, GRID = 224, 16, 14
ROW = IMG + 2
WIN = 54
HALF = 9
KWIN = 64 + WIN
NMEAN = 5 * 3 * PATCH * PATCH
TILES = 3
STEP_TOK = 4 * TILES
STEPS = -(-NTOK // STEP_TOK)
PADTOK = STEPS * STEP_TOK
ROWS = TILES * 128
REL = 2 * SEQ - 1
EW = 4 * INNER
NEXP = EXPERTS + 1
W13 = NEXP * EW
BIG = 1e30


def wait(eng, sem, value):
    if not isinstance(value, int) or value > 0:
        eng.wait_ge(sem, value)


def stand(eng, passed):
    eng.sem_inc(passed, 1)


def wait_alone(eng, sem, value, passed):
    wait(eng, sem, value)
    if not isinstance(value, int):
        stand(eng, passed)


class Chain:

    def __init__(self, eng, sem, per):
        self.eng, self.sem, self.per, self.k, self.base = eng, sem, per, 0, 0

    def start(self, step):
        self.base, self.k = step * self.per, 0

    def link(self, ins):
        self.k += 1
        ins.then_inc(self.sem, 1)
        self.eng.wait_ge(self.sem, self.base + self.k)

    def end(self):
        assert self.k == self.per, (self.k, self.per)


def names(ctx, nc):
    return (lambda n, s, d=F32: ctx.enter_context(nc.sbuf_tensor(n, s, d)),
            lambda n, s, d=F32: ctx.enter_context(nc.psum_tensor(n, s, d)),
            lambda n: ctx.enter_context(nc.semaphore(n)))


def embed_phase(nc, T, hs):
    NT, NW = NPATCH // 4, 5 * HALF
    EDGES = (0, 1, 7, 8)
    with ExitStack() as ctx:
        sb, ps, sem = names(ctx, nc)
        shifts = sb("shifts", [KWIN, 5, HALF, D + 2])
        wk = sb("wk", [KWIN, HALF, D + 1])
        cnt = sb("cnt", [KWIN, HALF])
        cntsq = sb("cntsq", [KWIN, 5])
        ones = sb("ones", [128, 128])
        xb = sb("xb", [KWIN, 2, 128, HALF])
        sq = sb("sq", [KWIN, 2, 128, HALF])
        rows = sb("rows", [KWIN, 2, 128])
        zero = sb("zero", [128, D])
        c0row = sb("c0row", [1, 2, D])
        c0 = sb("c0", [128, D])
        c1 = sb("c1", [128, D])
        mhalf = sb("mhalf", [128, 1])
        st = sb("st", [128, 4])
        rstd = sb("rstd", [128, 1])
        tmp = sb("tmp", [128, D])
        ho = sb("ho", [128, 2, D])
        acc = ps("acc", [128, 2, 512])
        pc = ps("pc", [128, 2, 512])
        w_in, txt_in, x_zero, x_sq, win_done = [sem("e_" + n) for n in (
            "w_in", "txt_in", "x_zero", "x_sq", "win_done")]
        row_done, emb_done, mean_done, rstd_done, h_done = [sem("e_" + n) for n in (
            "row_done", "emb_done", "mean_done", "rstd_done", "h_done")]
        x_in = [sem(f"e_x_in{u}") for u in range(2)]
        h_out = [sem(f"e_h_out{u}") for u in range(2)]
        cst, cst_sb, beta_done, beta_sb, steps, psteps = [sem("e_" + n) for n in (
            "cst", "cst_sb", "beta_done", "beta_sb", "steps", "psteps")]
        block = ctx.enter_context(nc.Block())

        def tiles(eng, body):
            for n in range(3):
                body(n, n % 2, n // 2)
            with eng.Fori(1, NT // 2) as i:
                body(i * 2 + 1, 1, i)
                body(i * 2 + 2, 0, i + 1)

        @block.sync
        def _(sp):
            sp.dma_start(shifts[:, :, :, :], T["shift_w"].rearrange("s p k d -> p s k d")).then_inc(w_in, 16)
            sp.dma_start(cnt[:, :], T["count_w"]).then_inc(w_in, 16)
            sp.dma_start(cntsq[:, :], T["count_sq"]).then_inc(w_in, 16)
            sp.dma_start(c0row[:, 1, :], T["tok_b"]).then_inc(w_in, 16)
            sp.dma_start(hs[NPATCH:NTOK].rearrange("b t d -> t b d"), T["txt"]).then_inc(txt_in, 16)
            sp.wait_ge(x_zero, 1)
            sp.dma_start(hs[NTOK:PADTOK].rearrange("b t d -> (b t) d"),
                         zero[0:(PADTOK - NTOK) * SEQ, :]).then_inc(txt_in, 16)
            sp.wait_ge(x_zero, 2)

            def body(n, u, v):
                wait(sp, emb_done, n - 1)
                wait(sp, x_sq, n - 1)
                src = T["xw"][bass.ds(n, 1)]
                for h in range(2):
                    sp.dma_start(xb[64 * h:64 * h + WIN, u, :, :], src[:, h * WIN:(h + 1) * WIN].rearrange(
                        "o p (r k) -> (o p) r k", k=HALF)).then_inc(x_in[u], 16)

            tiles(sp, body)

        @block.scalar
        def _(act):
            act.wait_ge(beta_done, 1)
            act.activation(c0row[:, 0, :], pc[0:1, 0, 0:D], ACT.Copy).then_inc(beta_sb, 1)

            def body(n, u, v):
                act.wait_ge(x_in[u], (v + 1) * 32)
                wait(act, emb_done, n - 1)
                act.activation(sq[:, u, :, :], xb[:, u, :, :], ACT.Square).then_inc(x_sq, 1)
                if isinstance(n, int) and n == 0:
                    return
                store(n - 1, 1 - u)

            def store(n, u):
                act.wait_ge(h_done, n + 1)
                act.dma_start(hs[bass.ds(n * 4, 4)].rearrange("b t d -> (b t) d"), ho[:, u, :]).then_inc(h_out[u], 16)

            tiles(act, body)
            store(NT - 1, 0)
            act.wait_ge(h_out[0], 16 * (NT // 2 + 1))
            act.wait_ge(h_out[1], 16 * (NT // 2))
            act.wait_ge(txt_in, 32)

        @block.gpsimd
        def _(pool):
            pool.memset(mhalf[:, :], -0.5).then_inc(psteps, 1)
            pool.wait_ge(psteps, 1)

            def body(n, u, v):
                pool.wait_ge(mean_done, n + 1)
                pool.tensor_tensor(rstd[:, :], st[:, 3:4], mhalf[:, :], ALU.pow).then_inc(rstd_done, 1)

            tiles(pool, body)

        @block.vector
        def _(dve):
            dve.memset(zero[:, :], 0.0).then_inc(x_zero, 1)
            dve.memset(ones[:, :], 1.0)
            dve.memset(xb[32:64, :, :, :], 0.0).then_inc(x_zero, 1)
            dve.wait_ge(w_in, 64)
            dve.tensor_copy(wk[:, :, D], cnt[:, :])
            done = 0
            for s in range(5):
                if s:
                    dve.wait_ge(steps, done)
                for k in range(HALF):
                    w, g = shifts[:, s, k, 0:D], shifts[:, s, k, D:D + 1]
                    if s == 0:
                        ins = dve.tensor_scalar(wk[:, k, 0:D], w, g, None, ALU.mult)
                    else:
                        ins = dve.scalar_tensor_tensor(wk[:, k, 0:D], w, g, wk[:, k, 0:D], ALU.mult, ALU.add)
                    ins.then_inc(steps, 1)
                    done += 1
            dve.wait_ge(steps, done)
            dve.wait_ge(beta_sb, 1)
            dve.tensor_tensor(c0row[:, 0, :], c0row[:, 0, :], c0row[:, 1, :], ALU.add).then_inc(win_done, 1)
            dve.wait_ge(cst, 1)
            dve.tensor_copy(c0[:, :], pc[:, 0, 0:D])
            dve.tensor_copy(c1[:, :], pc[:, 1, 0:D]).then_inc(cst_sb, 1)
            dve.wait_ge(cst_sb, 1)
            K = 5

            def body(n, u, v):
                dve.wait_ge(x_sq, n + 1)
                wait(dve, emb_done, n - 1)
                dve.tensor_reduce(rows[:, u, :], sq[:, u, :, :], AX.X, ALU.add).then_inc(row_done, 1)
                dve.wait_ge(emb_done, n + 1)
                b = done + n * K
                dve.tensor_scalar(st[:, 0:1], acc[:, u, D:D + 1], -1.0 / NMEAN, None, ALU.mult).then_inc(steps, 1)
                dve.tensor_scalar(st[:, 1:2], acc[:, u, D + 1:D + 2], 1.0 / NMEAN, None, ALU.mult).then_inc(steps, 1)
                dve.wait_ge(steps, b + 2)
                dve.tensor_tensor(st[:, 2:3], st[:, 0:1], st[:, 0:1], ALU.mult).then_inc(steps, 1)
                dve.wait_ge(steps, b + 3)
                dve.tensor_tensor(st[:, 2:3], st[:, 1:2], st[:, 2:3], ALU.subtract).then_inc(steps, 1)
                dve.wait_ge(steps, b + 4)
                wait(dve, rstd_done, n)
                dve.tensor_scalar(st[:, 3:4], st[:, 2:3], 0.0, EPS, ALU.max, ALU.add).then_inc(mean_done, 1)
                dve.scalar_tensor_tensor(tmp[:, :], c1[:, :], st[:, 0:1], acc[:, u, 0:D], ALU.mult,
                                         ALU.add).then_inc(steps, 1)
                dve.wait_ge(steps, b + 5)
                dve.wait_ge(rstd_done, n + 1)
                wait(dve, h_out[u], v * 16)
                dve.scalar_tensor_tensor(ho[:, u, :], tmp[:, :], rstd[:, :], c0[:, :], ALU.mult,
                                         ALU.add).then_inc(h_done, 1)

            tiles(dve, body)

        @block.tensor
        def _(pe):
            pe.wait_ge(w_in, 64)
            for s in range(5):
                for k in range(HALF):
                    m = pe.matmul(pc[0:1, 0, 0:D], shifts[:, s, k, D + 1:D + 2], shifts[:, s, k, 0:D],
                                  start=(s + k == 0), stop=(s * HALF + k == NW - 1))
            m.then_inc(beta_done, 1)
            pe.wait_ge(win_done, 1)
            pe.matmul(pc[:, 0, 0:D], ones[0:1, :], c0row[:, 0, :], start=True, stop=True)
            for k in range(HALF):
                m = pe.matmul(pc[:, 1, 0:D], ones[0:KWIN, :], wk[:, k, 0:D], start=(k == 0), stop=(k == HALF - 1))
            m.then_inc(cst, 1)

            def body(n, u, v):
                pe.wait_ge(x_in[u], (v + 1) * 32)
                wait(pe, h_done, n - 1)
                for k in range(HALF):
                    pe.matmul(acc[:, u, 0:D + 1], xb[:, u, :, k], wk[:, k, :], start=(k == 0), stop=(k == HALF - 1))
                pe.wait_ge(row_done, n + 1)
                m = pe.matmul(acc[:, u, D + 1:D + 2], rows[:, u, :], cntsq[:, 0:1], start=True, stop=False)
                for e, k in enumerate(EDGES):
                    m = pe.matmul(acc[:, u, D + 1:D + 2], sq[:, u, :, k], cntsq[:, e + 1:e + 2],
                                  start=False, stop=(k == EDGES[-1]))
                m.then_inc(emb_done, 1)

            tiles(pe, body)


def attention_phase(nc, T, hs, h2):
    SCALE = DQ ** -0.5
    QKV = 3 * HEADS * DQ
    FRONT, BACK = 27, 14
    ATT, PROJ, X1T, FF1, FF2, RING = 0, 6, 9, 11, 17, 21
    PITCH = HEADS * REL + SEQ
    rel_d = nc.dram_tensor("rel_d", (4 * TILES * SEQ * (PITCH - 1) + PITCH,), F32, kind="Internal").ap()
    with ExitStack() as ctx:
        sb, ps, sem = names(ctx, nc)
        w_hi = sb("w_hi", [128, QKV], F32R)
        w_lo = sb("w_lo", [128, QKV], F32R)
        w_low = sb("w_low", [128, QKV], F32R)
        l1_hi = sb("l1_hi", [128, DFF], F32R)
        l1_lo = sb("l1_lo", [128, DFF], F32R)
        l1_low = sb("l1_low", [128, DFF], F32R)
        wo = sb("wo", [DQ, HEADS, D])
        lin2 = sb("lin2", [128, DFF // 128, D])
        rel = sb("rel", [DQ, HEADS, REL])
        l1b = sb("l1b", [128, DFF // 128])
        vecs = sb("vecs", [128, 5, D])
        ident = sb("ident", [128, 128])
        mhalf = sb("mhalf2", [128, TILES])
        h = sb("h", [128, TILES, D])
        hres = sb("hres", [128, TILES, D])
        src = sb("src", [128, TILES, 256])
        res = sb("res", [128, TILES, D])
        y = sb("y", [128, TILES, D])
        x1 = sb("x1", [128, TILES, 256])
        x1b = sb("x1b", [128, TILES, D])
        h2o = sb("h2o", [128, TILES, D])
        s_hi, s_lo, s_low, s_tail = [sb(n, [128, ROWS], F32R) for n in ("s_hi", "s_lo", "s_low", "s_tail")]
        x_hi, x_lo, x_low, x_tail = [sb(n, [128, ROWS], F32R) for n in ("x_hi", "x_lo", "x_low", "x_tail")]
        qk = sb("qk", [128, 2, HEADS, ROWS])
        relp = sb("relp", [128, TILES, HEADS, REL])
        pos = sb("pos", [128, TILES, HEADS, SEQ])
        logit = sb("logit", [128, TILES * HEADS, SEQ])
        prob = sb("prob", [128, TILES * HEADS, SEQ])
        bd = sb("bd", [128, TILES * HEADS, 128])
        v = sb("v", [128, TILES, HEADS * DQ])
        oT = sb("oT", [DQ, TILES, HEADS, 128])
        hT = sb("hT", [128, DFF // 128, ROWS])
        mx = sb("mx", [128, TILES * HEADS])
        sm = sb("sm", [128, TILES * HEADS])
        bn = sb("bn", [128, TILES, 6])
        mv = sb("mv", [128, TILES, 2])
        ve = sb("ve", [128, TILES])
        rstd = sb("rstd2", [128, TILES])
        fr = ps("fr", [128, 3, 512])
        bk = ps("bk", [128, 3, 512])
        lg = ps("lg", [128, 2, 512])
        (w_in, c_in, set_up, setup_steps, h_in, hres_in, h2_out, front_done, front_free, back_done,
         back_free, lg_done, lg_free, acc_done, acc_free, src_norm, src_rows, src_lo, x1_norm, x1_done, x1_lo,
         x1b_done, res_done, hb_done, max_done, sub_done, exp_done, inv_done, prob_done, bd_done, var_src, rstd_src,
         var_1, rstd_1, var_2, rstd_2, h2_done, tail_steps, ln1_steps, src_steps, ln2_steps) = [
            sem("a_" + n) for n in (
                "w_in c_in set_up setup_steps h_in hres_in h2_out front_done front_free back_done "
                "back_free lg_done lg_free acc_done acc_free src_norm src_rows src_lo x1_norm x1_done x1_lo "
                "x1b_done res_done hb_done max_done sub_done exp_done inv_done prob_done bd_done var_src rstd_src "
                "var_1 rstd_1 var_2 rstd_2 h2_done tail_steps ln1_steps src_steps ln2_steps").split()]
        passed = sem("a_passed")
        pool_set_up = sem("a_pool_set_up")
        rel_out = [sem(f"a_rel_out{t}") for t in range(TILES)]
        pos_in = [sem(f"a_pos_in{t}") for t in range(TILES)]
        block = ctx.enter_context(nc.Block())
        LN1G, LN1B, LN2G, LN2B, LIN2B = range(5)
        stage = qk[:, :, :, :].rearrange("p a h r -> p (a h r)")
        rows_of = lambda t, s: t[bass.ds(s * STEP_TOK, STEP_TOK)].rearrange("b t d -> (b t) d").rearrange(
            "(k p) d -> p k d", p=128)
        bcast = lambda vec: vecs[:, vec, :].unsqueeze(1).broadcast_to([128, TILES, D])

        def program(eng, step, first=None):
            if first:
                first()
            step(0, True, False, True)
            step(1, True, True, True)
            with eng.Fori(2, STEPS - 1) as i:
                step(i, True, True, True)
            step(STEPS - 1, True, True, False)
            step(STEPS, False, True, False)

        @block.sync
        def _(sp):
            sp.dma_start(stage[:, 0:QKV], T["wqkv_a"]).then_inc(w_in, 16)
            sp.dma_start(stage[:, QKV:2 * QKV], T["wqkv_b"]).then_inc(w_in, 16)
            sp.dma_start(stage[:, 2 * QKV:2 * QKV + DFF], T["lin1_a"]).then_inc(w_in, 16)
            sp.dma_start(stage[:, 2 * QKV + DFF:2 * QKV + 2 * DFF], T["lin1_b2"]).then_inc(w_in, 16)
            sp.dma_start(h[:, :, :], rows_of(hs, 0)).then_inc(h_in, 16)
            for dst, name in ((wo, "wo"), (lin2, "lin2"), (rel, "rel"), (ident, "ident"), (l1b, "lin1_bias")):
                sp.dma_start(dst[:], T[name]).then_inc(c_in, 16)
            for k in range(5):
                sp.dma_start(vecs[:, k, :], T["vecs"][k:k + 1, :].broadcast_to([128, D])).then_inc(c_in, 16)

            def step(i, front, back, nxt):
                j, n = i - 1, i + 1
                if nxt:
                    wait_alone(sp, src_rows, i + 1, passed)
                    sp.dma_start(h[:, :, :], rows_of(hs, n)).then_inc(h_in, 16)
                if back:
                    wait_alone(sp, h2_done, j, passed)
                    sp.dma_start(hres[:, :, :], rows_of(hs, j)).then_inc(hres_in, 16)
                if front:
                    for t in range(TILES):
                        wait_alone(sp, front_free, i * FRONT + 19 + t, passed)
                        wait_alone(sp, pos_in[t], i * 16, passed)
                        there = bass.AP(rel_d.tensor, t * 128 * (PITCH - 1),
                                        [[SEQ * (PITCH - 1), 4], [PITCH, SEQ], [1, HEADS * REL]])
                        sp.dma_start(there, relp[:, t, :, :].rearrange("p h m -> p (h m)")).then_inc(rel_out[t], 16)
                    wait_alone(sp, lg_free, i * 6, passed)
                    for t in range(TILES):
                        wait_alone(sp, rel_out[t], (i + 1) * 16, passed)
                        skew = bass.AP(rel_d.tensor, t * 128 * (PITCH - 1) + SEQ - 1,
                                       [[PITCH - 1, 128], [REL, HEADS], [1, SEQ]])
                        sp.dma_start(pos[:, t, :, :], skew).then_inc(pos_in[t], 16)
                if back:
                    wait_alone(sp, h2_done, j + 1, passed)
                    sp.dma_start(rows_of(h2, j), h2o[:, :, :]).then_inc(h2_out, 16)

            program(sp, step)
            sp.wait_ge(h2_out, 16 * STEPS)

        @block.tensor
        def _(pe):
            def ring_front(s, k):
                wait(pe, front_free, s * FRONT + k - 2)
                return fr[:, k % 3, :]

            def ring_back(s, k):
                before, p = (s, k - 3) if k >= 3 else (s - 1, k - 3 + RING)
                if p < PROJ:
                    wait(pe, back_free, before * BACK + p + 1)
                elif p < X1T:
                    wait(pe, acc_free, before * 6 + p - PROJ + 1)
                elif p < FF2:
                    wait(pe, back_free, before * BACK + 6 + p - X1T + 1)
                elif p < FF2 + TILES:
                    wait(pe, acc_free, before * 6 + 3 + p - FF2 + 1)
                return bk[:, k % 3, :]

            def five(out, lhs, rhs):
                for n, (a, b) in enumerate(zip(lhs, rhs)):
                    m = pe.matmul(out, a, b, start=(n == 0), stop=(n == 4))
                return m

            xs = lambda c: [s_hi[:, c], s_lo[:, c], s_hi[:, c], s_low[:, c], s_tail[:, c]]
            ws = lambda c: [w_hi[:, c], w_hi[:, c], w_lo[:, c], w_low[:, c], w_low[:, c]]
            xf = lambda c: [x_hi[:, c], x_lo[:, c], x_hi[:, c], x_low[:, c], x_tail[:, c]]
            wf = lambda c: [l1_hi[:, c], l1_hi[:, c], l1_lo[:, c], l1_low[:, c], l1_low[:, c]]
            tile = lambda t: slice(128 * t, 128 * t + 128)

            def src_t(s):
                pe.wait_ge(src_norm, s + 1)
                for k in range(2):
                    bank = ring_front(s, k)
                    for t in range(TILES):
                        m = pe.transpose(bank[:, tile(t)], src[:, t, 128 * k:128 * k + 128], ident[:, :])
                    m.then_inc(front_done, 1)

            def qk_proj(s):
                pe.wait_ge(front_free, s * FRONT + 2)
                pe.wait_ge(src_lo, s + 1)
                for k in range(2 * HEADS):
                    bank = ring_front(s, 2 + k)
                    col = (k % 2) * HEADS * DQ + (k // 2) * DQ
                    five(bank[0:DQ, 0:ROWS], ws(slice(col, col + DQ)), xs(slice(0, ROWS))).then_inc(front_done, 1)

            def rel_proj(s):
                pe.wait_ge(front_free, s * FRONT + 18)
                for t in range(TILES):
                    bank = ring_front(s, 18 + t)
                    for hd in range(HEADS):
                        m = pe.matmul(bank[:, 64 * hd:64 * hd + REL], qk[0:DQ, 0, hd, tile(t)], rel[:, hd, :],
                                      start=True, stop=True)
                    m.then_inc(front_done, 1)

            def attend(s):
                pe.wait_ge(bd_done, s + 1)
                pe.wait_ge(front_free, (s + 1) * FRONT)
                for k in range(6):
                    bank = ring_back(s, ATT + k)
                    for q in range(4):
                        hd = 4 * (k % 2) + q
                        m = pe.matmul(bank[0:DQ, tile(q)], v[:, k // 2, DQ * hd:DQ * hd + DQ],
                                      bd[:, k // 2 * HEADS + hd, :], start=True, stop=True)
                    m.then_inc(back_done, 1)

            def out_proj(s):
                for t in range(TILES):
                    pe.wait_ge(back_free, s * BACK + 2 * t + 2)
                    bank = ring_back(s, PROJ + t)
                    for hd in range(HEADS):
                        m = pe.matmul(bank[:, 0:D], oT[:, t, hd, :], wo[:, hd, :],
                                      start=(hd == 0), stop=(hd == HEADS - 1))
                    m.then_inc(acc_done, 1)

            def v_proj(s):
                for k in range(6):
                    bank = ring_front(s, 21 + k)
                    col = 2 * HEADS * DQ + (k % 2) * 384
                    five(bank[:, 0:384], xs(tile(k // 2)), ws(slice(col, col + 384))).then_inc(front_done, 1)

            def scores(s):
                for k in range(6):
                    wait(pe, lg_free, s * 6 + k - 1)
                    for q in range(4):
                        hd = 4 * (k % 2) + q
                        m = pe.matmul(lg[:, k % 2, tile(q)], qk[0:DQ, 0, hd, tile(k // 2)],
                                      qk[0:DQ, 1, hd, tile(k // 2)], start=True, stop=True)
                    m.then_inc(lg_done, 1)

            def x1_t(s):
                pe.wait_ge(x1_done, s + 1)
                for k in range(2):
                    bank = ring_back(s, X1T + k)
                    for t in range(TILES):
                        m = pe.transpose(bank[:, tile(t)], x1[:, t, 128 * k:128 * k + 128], ident[:, :])
                    m.then_inc(back_done, 1)

            def ffn1(s):
                pe.wait_ge(back_free, s * BACK + 8)
                pe.wait_ge(x1_lo, s + 1)
                for c in range(DFF // 128):
                    bank = ring_back(s, FF1 + c)
                    five(bank[:, 0:ROWS], wf(tile(c)), xf(slice(0, ROWS))).then_inc(back_done, 1)

            def ffn2(s):
                pe.wait_ge(back_free, s * BACK + BACK)
                for t in range(TILES):
                    bank = ring_back(s, FF2 + t)
                    for c in range(DFF // 128):
                        m = pe.matmul(bank[:, 0:D], hT[:, c, tile(t)], lin2[:, c, :],
                                      start=(c == 0), stop=(c == DFF // 128 - 1))
                    m.then_inc(acc_done, 1)

            def step(i, front, back, nxt):
                j, n = i - 1, i + 1
                if front:
                    qk_proj(i)
                    rel_proj(i)
                if back:
                    attend(j)
                    out_proj(j)
                if front:
                    v_proj(i)
                    scores(i)
                if back:
                    x1_t(j)
                    ffn1(j)
                if nxt:
                    src_t(n)
                if back:
                    ffn2(j)

            def first():
                pe.wait_ge(c_in, 160)
                src_t(0)

            program(pe, step, first)

        @block.scalar
        def _(act):
            def evac(s, k, out, inp, func=ACT.Copy, **kw):
                act.wait_ge(front_done, s * FRONT + k + 1)
                act.activation(out, inp, func, **kw).then_inc(front_free, 1)

            def evac_back(s, k, out, inp, func=ACT.Copy, **kw):
                act.wait_ge(back_done, s * BACK + k + 1)
                act.activation(out, inp, func, **kw).then_inc(back_free, 1)

            def src_hi(s):
                evac(s, 0, s_hi[:, :], fr[:, 0, 0:ROWS])
                evac(s, 1, s_low[:, :], fr[:, 1, 0:ROWS])

            def step(i, front, back, nxt):
                j, n = i - 1, i + 1
                if front:
                    for k in range(2 * HEADS):
                        evac(i, 2 + k, qk[0:DQ, k % 2, k // 2, :], fr[0:DQ, (2 + k) % 3, 0:ROWS])
                    for t in range(TILES):
                        wait(act, rel_out[t], i * 16)
                        evac(i, 18 + t, relp[:, t, :, :],
                             fr[:, (18 + t) % 3, :].rearrange("p (h m) -> p h m", m=64)[:, :, 0:REL])
                if back:
                    for k in range(6):
                        evac_back(j, k, oT[:, k // 2, 4 * (k % 2):4 * (k % 2) + 4, :],
                                  bk[0:DQ, (ATT + k) % 3, :].rearrange("p (h r) -> p h r", h=4))
                if front:
                    for k in range(6):
                        evac(i, 21 + k, v[:, k // 2, 384 * (k % 2):384 * (k % 2) + 384], fr[:, (21 + k) % 3, 0:384])
                if back:
                    evac_back(j, 6, x_hi[:, :], bk[:, X1T % 3, 0:ROWS])
                    evac_back(j, 7, x_low[:, :], bk[:, (X1T + 1) % 3, 0:ROWS])
                    for c in range(DFF // 128):
                        evac_back(j, 8 + c, hT[:, c, :], bk[:, (FF1 + c) % 3, 0:ROWS], ACT.Relu, bias=l1b[:, c:c + 1])
                if front:
                    act.wait_ge(sub_done, i + 1)
                    wait(act, bd_done, i)
                    act.activation(prob[:, :, :], logit[:, :, :], ACT.Exp).then_inc(exp_done, 1)
                if nxt:
                    src_hi(n)

            def first():
                act.wait_ge(w_in, 64)
                act.activation(w_hi[:, :], stage[:, 0:QKV], ACT.Copy).then_inc(setup_steps, 1)
                act.activation(w_low[:, :], stage[:, QKV:2 * QKV], ACT.Copy).then_inc(setup_steps, 1)
                act.activation(l1_hi[:, :], stage[:, 2 * QKV:2 * QKV + DFF], ACT.Copy).then_inc(setup_steps, 1)
                act.activation(l1_low[:, :], stage[:, 2 * QKV + DFF:2 * QKV + 2 * DFF],
                               ACT.Copy).then_inc(setup_steps, 1)
                act.wait_ge(c_in, 160)
                src_hi(0)
                act.wait_ge(set_up, 2)

            program(act, step, first)

        @block.gpsimd
        def _(pool):
            def power(s, var, rst):
                pool.wait_ge(var, s + 1)
                pool.tensor_tensor(rstd[:, :], ve[:, :], mhalf[:, :], ALU.pow).then_inc(rst, 1)

            def src_rows_of(s):
                power(s, var_src, rstd_src)
                pool.wait_ge(src_rows, s + 1)
                stand(pool, passed)
                pool.tensor_copy(src[:, :, 192:256], src[:, :, 128:192]).then_inc(src_norm, 1)

            def step(i, front, back, nxt):
                j, n = i - 1, i + 1
                if back:
                    pool.wait_ge(inv_done, j + 1)
                    pool.tensor_tensor(prob[:, :, :], prob[:, :, :],
                                       sm[:, :].unsqueeze(2).broadcast_to([128, TILES * HEADS, SEQ]),
                                       ALU.mult).then_inc(prob_done, 1)
                    power(j, var_1, rstd_1)
                    pool.wait_ge(x1_norm, j + 1)
                    stand(pool, passed)
                    pool.tensor_copy(x1[:, :, 192:256], x1[:, :, 128:192]).then_inc(x1_done, 1)
                    pool.tensor_tensor(x1b[:, :, :], x1[:, :, 0:D], bcast(LIN2B), ALU.add).then_inc(x1b_done, 1)
                if front:
                    wait(pool, acc_free, i * 6 - 3)
                    pool.wait_ge(src_rows, i + 1)
                    stand(pool, passed)
                    pool.tensor_copy(res[:, :, :], src[:, :, 0:D]).then_inc(res_done, 1)
                if back:
                    pool.wait_ge(hres_in, (j + 1) * 16)
                    pool.tensor_tensor(hres[:, :, :], hres[:, :, :], bcast(LN2B), ALU.add).then_inc(hb_done, 1)
                if front:
                    pool.wait_ge(max_done, i + 1)
                    pool.tensor_tensor(logit[:, :, :], logit[:, :, :],
                                       mx[:, :].unsqueeze(2).broadcast_to([128, TILES * HEADS, SEQ]),
                                       ALU.subtract).then_inc(sub_done, 1)
                if nxt:
                    src_rows_of(n)
                if back:
                    power(j, var_2, rstd_2)

            def first():
                pool.memset(mhalf[:, :], -0.5)
                pool.memset(bd[:, :, :], 0.0).then_inc(pool_set_up, 1)
                pool.wait_ge(pool_set_up, 1)
                pool.wait_ge(c_in, 160)
                src_rows_of(0)

            program(pool, step, first)

        @block.vector
        def _(dve):
            tail_c = Chain(dve, tail_steps, 1)
            ln1_c, src_c, ln2_c = Chain(dve, ln1_steps, 4), Chain(dve, src_steps, 2), Chain(dve, ln2_steps, 4)

            def moments(chain, rows, var, s):
                for t in range(TILES):
                    ins = dve.bn_stats(bn[:, t, :], rows(t))
                chain.link(ins)
                stand(dve, passed)
                for t in range(TILES):
                    ins = dve.bn_aggr(mv[:, t, :], bn[:, t, :])
                chain.link(ins)
                dve.tensor_scalar(ve[:, :], mv[:, :, 1], EPS, None, ALU.add).then_inc(var, 1)

            def src_norm_of(s):
                src_c.start(s)
                dve.wait_ge(h_in, (s + 1) * 16)
                moments(src_c, lambda t: h[:, t, :], var_src, s)
                src_c.end()
                dve.wait_ge(rstd_src, s + 1)
                wait(dve, res_done, s)
                for t in range(TILES):
                    ins = dve.tensor_scalar(src[:, t, 0:D], h[:, t, :], mv[:, t, 0:1], rstd[:, t:t + 1],
                                            ALU.subtract, ALU.mult)
                ins.then_inc(src_rows, 1)

            def src_lo_of(s):
                dve.wait_ge(front_free, s * FRONT + 2)
                dve.tensor_tensor(s_lo[:, :], fr[:, 0, 0:ROWS], s_hi[:, :].bitcast(F32), ALU.subtract)
                dve.tensor_tensor(s_tail[0:64, :], fr[0:64, 1, 0:ROWS], s_low[0:64, :].bitcast(F32),
                                  ALU.subtract).then_inc(src_lo, 1)

            def softmax_tail(s):
                tail_c.start(s)
                dve.wait_ge(exp_done, s + 1)
                tail_c.link(dve.tensor_reduce(sm[:, :], prob[:, :, :], AX.X, ALU.add))
                tail_c.end()
                dve.reciprocal(sm[:, :], sm[:, :]).then_inc(inv_done, 1)
                dve.wait_ge(prob_done, s + 1)
                wait(dve, back_done, s * BACK - 8)
                for g in range(4):
                    p = slice(32 * g, 32 * g + 32)
                    ins = dve.transpose(bd[p, :, 32 * g:32 * g + 32], prob[p, :, :])
                ins.then_inc(bd_done, 1)

            def add_norm(chain, s, base, use, other, ready, var, rst, gain, plus, out, done):
                chain.start(s)
                dve.wait_ge(ready, s + 1)
                for t in range(TILES):
                    dve.wait_ge(acc_done, s * 6 + base + t + 1)
                    ins = dve.tensor_tensor(y[:, t, :], bk[:, (use + t) % 3, 0:D], other(t), ALU.add)
                    ins.then_inc(acc_free, 1)
                dve.wait_ge(acc_free, s * 6 + base + 3)
                moments(chain, lambda t: y[:, t, :], var, s)
                for t in range(TILES):
                    ins = dve.scalar_tensor_tensor(y[:, t, :], y[:, t, :], mv[:, t, 0:1], vecs[:, gain, :],
                                                   ALU.subtract, ALU.mult)
                chain.link(ins)
                dve.wait_ge(rst, s + 1)
                for t in range(TILES):
                    ins = dve.scalar_tensor_tensor(out(t), y[:, t, :], rstd[:, t:t + 1], plus(t), ALU.mult, ALU.add)
                chain.link(ins)
                chain.end()
                dve.sem_inc(done, 1)

            def ln1(s):
                wait(dve, x1b_done, s)
                add_norm(ln1_c, s, 0, PROJ, lambda t: res[:, t, :], res_done, var_1, rstd_1, LN1G,
                         lambda t: vecs[:, LN1B, :], lambda t: x1[:, t, 0:D], x1_norm)

            def ln2(s):
                dve.wait_ge(hb_done, s + 1)
                wait(dve, h2_out, s * 16)
                add_norm(ln2_c, s, 3, FF2, lambda t: x1b[:, t, :], x1b_done, var_2, rstd_2, LN2G,
                         lambda t: hres[:, t, :], lambda t: h2o[:, t, :], h2_done)

            def extract(s):
                wait(dve, exp_done, s)
                for k in range(6):
                    dve.wait_ge(lg_done, s * 6 + k + 1)
                    t, h0 = k // 2, 4 * (k % 2)
                    dve.wait_ge(pos_in[t], (s + 1) * 16)
                    for g in range(4):
                        p = slice(32 * g, 32 * g + 32)
                        ins = dve.scalar_tensor_tensor(
                            logit[p, t * HEADS + h0:t * HEADS + h0 + 4, :],
                            lg[p, k % 2, :].rearrange("p (h c) -> p h c", h=4)[:, :, 32 * g:32 * g + 32], SCALE,
                            pos[p, t, h0:h0 + 4, :], ALU.mult, ALU.add)
                    ins.then_inc(lg_free, 1)

            def x1_lo_of(s):
                dve.wait_ge(back_free, s * BACK + 8)
                dve.tensor_tensor(x_lo[:, :], bk[:, X1T % 3, 0:ROWS], x_hi[:, :].bitcast(F32), ALU.subtract)
                dve.tensor_tensor(x_tail[0:64, :], bk[0:64, (X1T + 1) % 3, 0:ROWS], x_low[0:64, :].bitcast(F32),
                                  ALU.subtract).then_inc(x1_lo, 1)

            def step(i, front, back, nxt):
                j, n = i - 1, i + 1
                if back:
                    softmax_tail(j)
                    ln1(j)
                if front:
                    extract(i)
                if back:
                    x1_lo_of(j)
                if front:
                    dve.wait_ge(lg_free, (i + 1) * 6)
                    dve.tensor_reduce(mx[:, :], logit[:, :, :], AX.X, ALU.max).then_inc(max_done, 1)
                if nxt:
                    src_norm_of(n)
                    src_lo_of(n)
                if back:
                    ln2(j)

            def first():
                dve.memset(s_tail[64:128, :].bitcast(F32), 0.0)
                dve.memset(x_tail[64:128, :].bitcast(F32), 0.0).then_inc(set_up, 1)
                src_norm_of(0)
                for k, (hi, lo, low, at, n) in enumerate(((w_hi, w_lo, w_low, 0, QKV),
                                                          (l1_hi, l1_lo, l1_low, 2 * QKV, DFF))):
                    dve.wait_ge(setup_steps, 2 * k + 2)
                    dve.tensor_tensor(lo[:, :], stage[:, at:at + n], hi[:, :].bitcast(F32), ALU.subtract)
                    ins = dve.tensor_tensor(low[64:128, :], stage[64:128, at + n:at + 2 * n],
                                            low[64:128, :].bitcast(F32), ALU.subtract)
                ins.then_inc(set_up, 1)
                src_lo_of(0)
                dve.wait_ge(pool_set_up, 1)

            program(dve, step, first)


def experts_phase(nc, T, h2, out):
    NTILE, SLOTS = STEPS * TILES, 3
    WCOL = W13 + EXPERTS
    GROUP = 3
    USES = NEXP // GROUP * SLOTS + 1
    GW = INNER + 1
    ALPHA, LIMIT = 1.702, 7.0
    G2 = EXPERTS // GROUPS
    with ExitStack() as ctx:
        sb, ps, sem = names(ctx, nc)
        stage = sb("m_stage", [128, 3, WCOL])
        w_hi, w_lo, w_low, w_tail = [sb("m_" + n, [128, WCOL], F32R) for n in ("w_hi", "w_lo", "w_low", "w_tail")]
        w2 = sb("m_w2", [GW, NEXP, D])
        ident = sb("m_ident", [128, 128])
        lt4 = sb("m_lt4", [128, GROUPS, GROUPS])
        lt8 = sb("m_lt8", [128, EXPERTS, EXPERTS])
        gate_b = sb("m_gate_b", [128, EXPERTS])
        mhalf = sb("m_mhalf", [128, 1])
        h = sb("m_h", [128, SLOTS, D])
        hres = sb("m_hres", [128, SLOTS, D])
        z = sb("m_z", [128, SLOTS, 256])
        z_hi, z_lo_b, z_low, z_tail = [sb("m_" + n, [128, ROWS], F32R) for n in ("z_hi", "z_lo", "z_low", "z_tail")]
        h1 = sb("m_h1", [128, GROUP, GROUP, 2 * INNER])
        hh = sb("m_hh", [128, GROUP, GROUP, 2 * INNER])
        xg = sb("m_xg", [128, GROUP, GROUP, INNER])
        xl = sb("m_xl", [128, GROUP, GROUP, INNER])
        sg = sb("m_sg", [128, GROUP, GROUP, GW])
        g1 = sb("m_g1", [128, GROUP, GROUP, GW])
        sgw = sb("m_sgw", [128, GROUP, GROUP, GW])
        g = sb("m_g", [128, SLOTS, NEXP, GW])
        gT = sb("m_gT", [GW, NEXP, 128])
        ho = sb("m_ho", [128, SLOTS, D])
        bn, mv = sb("m_bn", [128, 6]), sb("m_mv", [128, 2])
        ve, rstd = sb("m_ve", [128, 1]), sb("m_rstd", [128, 1])
        lgt, score, s8, s8m = [sb("m_" + n, [128, TILES, EXPERTS]) for n in ("lgt", "score", "s8", "s8m")]
        w = sb("m_w", [128, TILES, NEXP])
        m1, gs, cnt4 = sb("m_m1", [128, TILES]), sb("m_gs", [128, TILES, GROUPS]), sb("m_cnt4", [128, TILES, GROUPS])
        cnt8 = sb("m_cnt8", [128, TILES, EXPERTS])
        gt4, ge4 = [sb("m_" + n, [128, TILES, GROUPS, GROUPS]) for n in ("gt4", "ge4")]
        gt8, ge8 = [sb("m_" + n, [128, TILES, EXPERTS, EXPERTS]) for n in ("gt8", "ge8")]
        gp = ps("m_gp", [128, 2, GROUP, 512])
        tr = ps("m_tr", [128, 512])
        acc = ps("m_acc", [128, 512])
        (w_in, c_in, hi_done, w_done, ones_done, pool_ready, tg_done, tg_free, tz_done, z_norm, z_rows, z_hi_done, z_lo_done,
         var_done, rstd_done, grp_done, grp_free, h1_done, hh_done, xg_done, xl_done, sg_done, wsg_done, g1_done,
         g_done, acc_done, add_done, gate_in, gate_exp, gate_w, gate_steps, ln_steps, passed) = [
            sem("m_" + n) for n in (
                "w_in c_in hi_done w_done ones_done pool_ready tg_done tg_free tz_done z_norm z_rows z_hi_done z_lo_done "
                "var_done rstd_done grp_done grp_free h1_done hh_done xg_done xl_done sg_done wsg_done g1_done "
                "g_done acc_done add_done gate_in gate_exp gate_w gate_steps ln_steps passed").split()]
        h_in, res_in, o_out = [[sem(f"m_{n}{t}") for t in range(SLOTS)] for n in ("h_in", "res_in", "o_out")]
        block = ctx.enter_context(nc.Block())
        tile = lambda t: slice(128 * t, 128 * t + 128)
        rows_of = lambda t, n: t[bass.ds(n * 4, 4)].rearrange("b t d -> (b t) d")

        def use(t, q):
            return (0, 2, 3)[q] if t == 0 else 1 + 3 * t + q

        def program(eng, tile_step, first, last):
            first()
            for t in range(SLOTS):
                tile_step(0, t, t, True)
            with eng.Fori(1, STEPS - 1) as s:
                for t in range(SLOTS):
                    tile_step(s, t, s * SLOTS + t, True)
            for t in range(SLOTS):
                tile_step(STEPS - 1, t, NTILE - SLOTS + t, False)
            last()

        @block.sync
        def _(sp):
            for k, name in enumerate(("w13_a", "w13_b")):
                sp.dma_start(stage[:, k, :], T[name]).then_inc(w_in, 16)
            for p in (64, 96):
                sp.dma_start(stage[p:p + 1, 2, :], T["b13"]).then_inc(w_in, 16)
            for dst, name in ((w2, "w2"), (ident, "ident"), (lt4, "lt4"), (lt8, "lt8")):
                sp.dma_start(dst[:], T[name]).then_inc(c_in, 16)
            sp.dma_start(gate_b[:, :], T["gate_b"].broadcast_to([128, EXPERTS])).then_inc(c_in, 16)
            for t in range(SLOTS):
                sp.dma_start(h[:, t, :], rows_of(h2, t)).then_inc(h_in[t], 16)

            def tile_step(s, t, n, nxt):
                if nxt:
                    wait_alone(sp, z_rows, n + 1, passed)
                    sp.dma_start(h[:, t, :], rows_of(h2, n + SLOTS)).then_inc(h_in[t], 16)
                wait_alone(sp, add_done, n - 2, passed)
                sp.dma_start(hres[:, t, :], rows_of(h2, n)).then_inc(res_in[t], 16)
                if not (isinstance(n, int) and n < 2):
                    store(n - 2, (t + 1) % SLOTS)

            def store(n, t, rows=4):
                wait_alone(sp, add_done, n + 1, passed)
                sp.dma_start(out[:, bass.ds(n * 4, rows), :].rearrange("t b d -> b t d"),
                             ho[0:32 * rows, t, :]).then_inc(o_out[t], 16)

            def last():
                store(NTILE - 2, (NTILE - 2) % SLOTS)
                store(NTILE - 1, (NTILE - 1) % SLOTS, NTOK - 4 * (NTILE - 1))
                for t in range(SLOTS):
                    sp.wait_ge(o_out[t], 16 * STEPS)

            program(sp, tile_step, lambda: None, last)

        @block.tensor
        def _(pe):
            def five(out, t, c):
                xs = [z_hi, z_lo_b, z_hi, z_low, z_tail]
                ws = [w_hi, w_hi, w_lo, w_low, w_tail]
                for k in range(5):
                    m = pe.matmul(out, xs[k][:, tile(t)], ws[k][:, c], start=(k == 0), stop=(k == 4))
                return m

            def group(s, t, n, q):
                wait(pe, grp_free, s * USES + use(t, q) - 1)
                for e in range(GROUP):
                    c = (q * GROUP + e) * EW
                    m = five(gp[:, use(t, q) % 2, e, 0:EW], t, slice(c, c + EW))
                m.then_inc(grp_done, 1)

            def gate(s):
                wait(pe, grp_free, s * USES)
                pe.wait_ge(z_lo_done, s * SLOTS + SLOTS)
                for t in range(TILES):
                    m = five(gp[:, 1, 0, EXPERTS * t:EXPERTS * t + EXPERTS], t, slice(W13, WCOL))
                m.then_inc(grp_done, 1)

            def g_turn(n, t, q):
                if q == 0:
                    pe.wait_ge(z_lo_done, n + 4 if nxt_of(n) else NTILE)
                else:
                    pe.wait_ge(tg_free, n * 3 + q)
                pe.wait_ge(g_done, n * 3 + q + 1)
                for e in range(GROUP):
                    m = pe.transpose(tr[0:GW, tile(e)], g[:, t, q * GROUP + e, :], ident[:, :])
                m.then_inc(tg_done, 1)

            def nxt_of(n):
                return not isinstance(n, int) or n + 4 <= NTILE

            def second(n, q):
                pe.wait_ge(tg_free, n * 3 + q + 1)
                if q == 0:
                    wait(pe, add_done, n)
                for e in range(q * GROUP, q * GROUP + GROUP):
                    m = pe.matmul(acc[:, 0:D], gT[:, e, :], w2[:, e, :], start=(e == 0), stop=(e == NEXP - 1))
                if q == 2:
                    m.then_inc(acc_done, 1)

            def z_turn(n, t):
                pe.wait_ge(z_norm, n + 1)
                if not (isinstance(n, int) and n < 4):
                    pe.wait_ge(tg_free, (n - 4) * 3 + 3)
                elif n:
                    pe.wait_ge(z_lo_done, n)
                for k in range(2):
                    m = pe.transpose(tr[:, tile(k)], z[:, t, 128 * k:128 * k + 128], ident[:, :])
                m.then_inc(tz_done, 1)

            def tile_step(s, t, n, nxt):
                p, pt = n - 1, (t + 2) % SLOTS
                prev = not (isinstance(n, int) and n == 0)
                pe.wait_ge(z_lo_done, n + 1)
                group(s, t, n, 0)
                if t == 0:
                    gate(s)
                group(s, t, n, 1)
                if prev:
                    g_turn(p, pt, 0)
                group(s, t, n, 2)
                if prev:
                    finish(p, pt)
                if nxt:
                    z_turn(n + 3, t)

            def finish(p, pt):
                g_turn(p, pt, 1)
                second(p, 0)
                g_turn(p, pt, 2)
                second(p, 1)
                second(p, 2)

            def first():
                pe.wait_ge(c_in, 80)
                for n in range(SLOTS):
                    z_turn(n, n)
                pe.wait_ge(w_done, 1)

            def last():
                g_turn(NTILE - 1, (NTILE - 1) % SLOTS, 0)
                finish(NTILE - 1, (NTILE - 1) % SLOTS)

            program(pe, tile_step, first, last)

        @block.scalar
        def _(act):
            def z_hi_of(n, t):
                act.wait_ge(tz_done, n + 1)
                act.activation(z_hi[:, tile(t)], tr[:, 0:128], ACT.Copy)
                act.activation(z_low[:, tile(t)], tr[:, 128:256], ACT.Copy).then_inc(z_hi_done, 1)

            def copy(s, t, n, q):
                act.wait_ge(grp_done, s * USES + use(t, q) + 1)
                act.activation(h1[:, q, :, :], gp[:, use(t, q) % 2, :, 0:2 * INNER], ACT.Copy).then_inc(h1_done, 1)

            def sigmoid(n, q):
                act.wait_ge(xg_done, n * 3 + q + 1)
                wait(act, wsg_done, n * 3 + q - 2)
                act.activation(sg[:, q, :, 0:INNER], xg[:, q, :, :], ACT.Sigmoid, scale=ALPHA).then_inc(sg_done, 1)

            def g_out(n, q):
                act.wait_ge(tg_done, n * 3 + q + 1)
                act.activation(gT[:, q * GROUP:q * GROUP + GROUP, :], tr[0:GW, 0:GROUP * 128], ACT.Copy).then_inc(
                    tg_free, 1)

            def tile_step(s, t, n, nxt):
                prev = not (isinstance(n, int) and n == 0)
                if not (isinstance(n, int) and (n == 0 or n + 3 > NTILE)):
                    z_hi_of(n + 2, (t + 2) % SLOTS)
                copy(s, t, n, 0)
                if prev:
                    sigmoid(n - 1, 2)
                copy(s, t, n, 1)
                if prev:
                    g_out(n - 1, 0)
                sigmoid(n, 0)
                if t == 0:
                    act.wait_ge(gate_in, s + 1)
                    act.activation(score[:, :, :], lgt[:, :, :], ACT.Exp).then_inc(gate_exp, 1)
                copy(s, t, n, 2)
                if prev:
                    g_out(n - 1, 1)
                sigmoid(n, 1)
                if prev:
                    g_out(n - 1, 2)

            def first():
                act.wait_ge(ones_done, 2)
                for n in range(SLOTS):
                    z_hi_of(n, n)
                act.wait_ge(w_in, 64)
                act.activation(w_hi[:, :], stage[:, 0, :], ACT.Copy).then_inc(hi_done, 1)
                act.activation(w_low[:, :], stage[:, 1, :], ACT.Copy).then_inc(hi_done, 1)
                act.activation(w_tail[0:64, :], stage[0:64, 1, :], ACT.Copy)
                act.activation(w_tail[64:65, :], stage[64:65, 2, :], ACT.Copy)
                act.activation(w_tail[96:97, :], stage[96:97, 2, :], ACT.Copy).then_inc(hi_done, 1)

            def last():
                n = NTILE - 1
                sigmoid(n, 2)
                for q in range(3):
                    g_out(n, q)

            program(act, tile_step, first, last)

        @block.gpsimd
        def _(pool):
            def clip(n, q):
                pool.wait_ge(hh_done, n * 3 + q + 1)
                stand(pool, passed)
                pool.tensor_scalar(xl[:, q, :, :], hh[:, q, :, INNER:], LIMIT, -LIMIT, ALU.min,
                                   ALU.max).then_inc(xl_done, 1)

            def weigh(s, t, n, q):
                pool.wait_ge(sg_done, n * 3 + q + 1)
                if t == 0 and q == 0:
                    pool.wait_ge(gate_w, s + 1)
                wq = w[:, t, q * GROUP:q * GROUP + GROUP].unsqueeze(2).broadcast_to([128, GROUP, GW])
                pool.tensor_tensor(sgw[:, q, :, :], sg[:, q, :, :], wq, ALU.mult).then_inc(wsg_done, 1)
                pool.wait_ge(wsg_done, n * 3 + q + 1)
                pool.wait_ge(g1_done, n * 3 + q + 1)
                if q == 0:
                    wait(pool, tg_done, n * 3 - 6)
                pool.tensor_tensor(g[:, t, q * GROUP:q * GROUP + GROUP, :], g1[:, q, :, :], sgw[:, q, :, :],
                                   ALU.mult).then_inc(g_done, 1)

            def power(n):
                pool.wait_ge(var_done, n + 1)
                pool.tensor_tensor(rstd[:, :], ve[:, :], mhalf[:, :], ALU.pow).then_inc(rstd_done, 1)

            def double(n, t):
                pool.wait_ge(z_rows, n + 1)
                stand(pool, passed)
                pool.tensor_copy(z[:, t, 192:256], z[:, t, 128:192]).then_inc(z_norm, 1)

            def tile_step(s, t, n, nxt):
                prev = not (isinstance(n, int) and n == 0)
                clip(n, 0)
                if prev:
                    weigh(s, (t + 2) % SLOTS, n - 1, 2)
                if nxt:
                    power(n + 3)
                clip(n, 1)
                weigh(s, t, n, 0)
                if nxt:
                    double(n + 3, t)
                clip(n, 2)
                weigh(s, t, n, 1)

            def first():
                pool.memset(mhalf[:, :], -0.5)
                pool.memset(sg[:, :, :, :], 1.0)
                pool.memset(g1[:, :, :, :], 1.0)
                pool.memset(w[:, :, :], 1.0).then_inc(pool_ready, 1)
                pool.wait_ge(pool_ready, 1)
                for n in range(SLOTS):
                    power(n)
                    double(n, n)

            def last():
                weigh(STEPS, (NTILE - 1) % SLOTS, NTILE - 1, 2)

            program(pool, tile_step, first, last)

        @block.vector
        def _(dve):
            ln_c, gate_c = Chain(dve, ln_steps, 2), Chain(dve, gate_steps, 16)

            def moments(n, t, k):
                ln_c.start(n)
                dve.wait_ge(h_in[t], (k + 1) * 16)
                ln_c.link(dve.bn_stats(bn[:, :], h[:, t, :]))
                stand(dve, passed)
                ln_c.link(dve.bn_aggr(mv[:, :], bn[:, :]))
                ln_c.end()
                dve.tensor_scalar(ve[:, :], mv[:, 1:2], EPS, None, ALU.add).then_inc(var_done, 1)

            def normalise(n, t):
                dve.wait_ge(rstd_done, n + 1)
                wait(dve, tz_done, n - 2)
                dve.tensor_scalar(z[:, t, 0:D], h[:, t, :], mv[:, 0:1], rstd[:, :], ALU.subtract,
                                  ALU.mult).then_inc(z_rows, 1)

            def z_lo_of(n, t):
                dve.wait_ge(z_hi_done, n + 1)
                dve.tensor_tensor(z_lo_b[:, tile(t)], tr[:, 0:128], z_hi[:, tile(t)].bitcast(F32), ALU.subtract)
                dve.tensor_tensor(z_tail[0:64, tile(t)], tr[0:64, 128:256], z_low[0:64, tile(t)].bitcast(F32),
                                  ALU.subtract).then_inc(z_lo_done, 1)

            def product(s, t, n, q):
                dve.wait_ge(h1_done, n * 3 + q + 1)
                dve.tensor_tensor(hh[:, q, :, :], h1[:, q, :, :], gp[:, use(t, q) % 2, :, 2 * INNER:EW],
                                  ALU.mult).then_inc(grp_free, 1)
                dve.wait_ge(grp_free, s * USES + use(t, q) + 1)
                dve.tensor_scalar(xg[:, q, :, :], hh[:, q, :, 0:INNER], LIMIT, None, ALU.min).then_inc(xg_done, 1)
                dve.sem_inc(hh_done, 1)

            def linear(n, q):
                dve.wait_ge(xl_done, n * 3 + q + 1)
                dve.wait_ge(xg_done, n * 3 + q + 1)
                wait(dve, g_done, n * 3 + q - 2)
                dve.scalar_tensor_tensor(g1[:, q, :, 0:INNER], xl[:, q, :, :], 1.0, xg[:, q, :, :], ALU.add,
                                         ALU.mult).then_inc(g1_done, 1)

            def residual(n, t, k):
                dve.wait_ge(acc_done, n + 1)
                dve.wait_ge(res_in[t], (k + 1) * 16)
                wait(dve, o_out[t], k * 16)
                dve.tensor_tensor(ho[:, t, :], acc[:, 0:D], hres[:, t, :], ALU.add).then_inc(add_done, 1)

            def before(a, count):
                shape = [128, TILES, count, count]
                return a.unsqueeze(2).broadcast_to(shape), a.unsqueeze(3).broadcast_to(shape)

            def rank(a, count, gt, ge, lt, cnt):
                aj, ai = before(a, count)
                dve.tensor_tensor(gt[:, :, :, :], aj, ai, ALU.is_gt)
                gate_c.link(dve.tensor_tensor(ge[:, :, :, :], aj, ai, ALU.is_ge))
                gate_c.link(dve.tensor_tensor(ge[:, :, :, :], ge[:, :, :, :], lt[:, :, :].unsqueeze(1).broadcast_to(
                    [128, TILES, count, count]), ALU.mult))
                gate_c.link(dve.tensor_tensor(gt[:, :, :, :], gt[:, :, :, :], ge[:, :, :, :], ALU.max))
                gate_c.link(dve.tensor_reduce(cnt[:, :, :], gt[:, :, :, :], AX.X, ALU.add))

            def gate_logits(s):
                gate_c.start(s)
                dve.wait_ge(grp_done, s * USES + 2)
                dve.tensor_copy(lgt[:, :, :], gp[:, 1, 0, 0:TILES * EXPERTS].rearrange(
                    "p (t e) -> p t e", t=TILES)).then_inc(grp_free, 1)
                dve.wait_ge(grp_free, s * USES + 2)
                gate_c.link(dve.tensor_reduce(m1[:, :], lgt[:, :, :], AX.X, ALU.max))
                dve.tensor_tensor(lgt[:, :, :], lgt[:, :, :], m1[:, :].unsqueeze(2).broadcast_to(
                    [128, TILES, EXPERTS]), ALU.subtract).then_inc(gate_in, 1)

            def gate_weights(s):
                wide = [128, TILES, EXPERTS]
                dve.wait_ge(gate_exp, s + 1)
                gate_c.link(dve.tensor_reduce(m1[:, :], score[:, :, :], AX.X, ALU.add))
                gate_c.link(dve.reciprocal(m1[:, :], m1[:, :]))
                gate_c.link(dve.tensor_tensor(score[:, :, :], score[:, :, :], m1[:, :].unsqueeze(2).broadcast_to(
                    wide), ALU.mult))
                gate_c.link(dve.tensor_tensor(s8[:, :, :], score[:, :, :], gate_b[:, :].unsqueeze(1).broadcast_to(
                    wide), ALU.add))
                gate_c.link(dve.tensor_reduce(gs[:, :, :], s8[:, :, :].rearrange("p t (g e) -> p t g e", e=G2),
                                              AX.X, ALU.add))
                rank(gs[:, :, :], GROUPS, gt4, ge4, lt4, cnt4)
                gate_c.link(dve.tensor_scalar(cnt4[:, :, :], cnt4[:, :, :], 2.0, -BIG, ALU.is_ge, ALU.mult))
                gate_c.link(dve.tensor_tensor(
                    s8m[:, :, :].rearrange("p t (g e) -> p t g e", e=G2),
                    s8[:, :, :].rearrange("p t (g e) -> p t g e", e=G2),
                    cnt4[:, :, :].unsqueeze(3).broadcast_to([128, TILES, GROUPS, G2]), ALU.add))
                rank(s8m[:, :, :], EXPERTS, gt8, ge8, lt8, cnt8)
                gate_c.end()
                wait(dve, wsg_done, s * 9)
                dve.scalar_tensor_tensor(w[:, :, 0:EXPERTS], cnt8[:, :, :], 2.0, score[:, :, :], ALU.is_lt,
                                         ALU.mult).then_inc(gate_w, 1)

            def tile_step(s, t, n, nxt):
                prev = not (isinstance(n, int) and n == 0)
                if not (isinstance(n, int) and (n == 0 or n + 3 > NTILE)):
                    z_lo_of(n + 2, (t + 2) % SLOTS)
                if not (isinstance(n, int) and n < 2):
                    residual(n - 2, (t + 1) % SLOTS, s if t == 2 else s - 1)
                product(s, t, n, 0)
                if t == 0:
                    gate_logits(s)
                if prev:
                    linear(n - 1, 2)
                if nxt:
                    moments(n + 3, t, s + 1)
                product(s, t, n, 1)
                if t == 0:
                    gate_weights(s)
                linear(n, 0)
                if nxt:
                    normalise(n + 3, t)
                product(s, t, n, 2)
                linear(n, 1)

            def first():
                dve.memset(w_tail[:, :].bitcast(F32), 0.0)
                dve.memset(z_tail[:, :].bitcast(F32), 0.0).then_inc(ones_done, 1)
                dve.wait_ge(ones_done, 1)
                dve.memset(z_tail[64:65, :].bitcast(F32), 1.0)
                dve.memset(z_tail[96:97, :].bitcast(F32), 1.0).then_inc(ones_done, 1)
                dve.wait_ge(ones_done, 2)
                dve.wait_ge(c_in, 80)
                for n in range(SLOTS):
                    moments(n, n, 0)
                    normalise(n, n)
                for n in range(SLOTS):
                    z_lo_of(n, n)
                dve.wait_ge(hi_done, 3)
                dve.tensor_tensor(w_lo[:, :], stage[:, 0, :], w_hi[:, :].bitcast(F32), ALU.subtract)
                dve.tensor_tensor(w_low[64:128, :], stage[64:128, 1, :], w_low[64:128, :].bitcast(F32), ALU.subtract)
                dve.tensor_tensor(w_tail[96:97, :], stage[96:97, 2, :], w_tail[96:97, :].bitcast(F32),
                                  ALU.subtract).then_inc(w_done, 1)
                dve.wait_ge(pool_ready, 1)

            def last():
                n = NTILE - 1
                residual(n - 1, (n - 1) % SLOTS, STEPS - 1)
                linear(n, 2)
                residual(n, n % SLOTS, STEPS - 1)

            program(dve, tile_step, first, last)


def build(nc, T, out):
    hs = nc.dram_tensor("hs", (PADTOK, SEQ, D), F32, kind="Internal").ap()
    h2 = nc.dram_tensor("h2", (PADTOK, SEQ, D), F32, kind="Internal").ap()
    embed_phase(nc, T, hs)
    attention_phase(nc, T, hs, h2)
    experts_phase(nc, T, h2, out)


def layouts(a):
    import numpy as np
    f = np.float32
    L = {}
    x = np.pad(a["x"], ((0, 0), (0, 0), (1, 1), (1, 1)))
    cols = PATCH * np.arange(GRID)[:, None] + np.arange(PATCH + 2)
    x = x[:, :, :, cols][:, :, cols]
    x = x.transpose(1, 3, 2, 4, 0, 5).reshape(3, PATCH + 2, NPATCH // 4, 128, 2, HALF)
    x = np.concatenate([x[:, 1:17].reshape(48, *x.shape[2:]), x[:, 0], x[:, 17]])
    L["xw"] = x.transpose(1, 3, 0, 2, 4).reshape(NPATCH // 4, 2 * WIN, 128 * HALF)
    full = np.concatenate([a["L0_tok_W"], a["L0_tok_ln_gamma"][:, None], a["L0_tok_ln_beta"][:, None]], axis=1)
    full = full.reshape(PATCH, PATCH, 5, 3, D + 2)
    sw = np.zeros((5, 3, PATCH + 2, PATCH + 2, D + 2), f)
    cw = np.zeros((3, PATCH + 2, PATCH + 2), f)
    for s, (dy, dx) in enumerate([(0, 0), (0, -1), (0, 1), (-1, 0), (1, 0)]):
        sw[s, :, 1 + dy:17 + dy, 1 + dx:17 + dx] = full[:, :, s].transpose(2, 0, 1, 3)
        cw[:, 1 + dy:17 + dy, 1 + dx:17 + dx] += 1
    def window(w):
        lead = w.shape[:-4]
        w = np.concatenate([w[..., :, 1:17, :, :].reshape(*lead, 48, 18, w.shape[-1]), w[..., :, 0, :, :],
                            w[..., :, 17, :, :]], axis=-3)
        gap = np.zeros((*lead, 10, HALF, w.shape[-1]), f)
        return np.concatenate([w[..., 0:HALF, :], gap, w[..., HALF:, :]], axis=-3)
    L["shift_w"] = window(sw)
    L["count_w"] = window(cw[..., None])[..., 0]
    row = L["count_w"][:, 4:5]
    L["count_sq"] = np.concatenate([row, L["count_w"][:, [0, 1, 7, 8]] - row], axis=1)
    L["tok_b"] = a["L0_tok_b"].reshape(1, D)
    L["txt"] = a["txt"]
    q = np.concatenate([a["L0_attn_" + n].transpose(1, 0, 2).reshape(D, HEADS * DQ) for n in ("w_q", "w_k", "w_v")], 1)
    two = lambda w: (w[0:128], np.concatenate([w[128:], w[128:]]))
    L["wqkv_a"], L["wqkv_b"] = two(q)
    L["lin1_a"], L["lin1_b2"] = two(a["L0_attn_lin1_w"].T)
    L["wo"] = a["L0_attn_w_o"].transpose(1, 0, 2)
    L["lin2"] = a["L0_attn_lin2_w"].T.reshape(DFF // 128, 128, D).transpose(1, 0, 2)
    mid = a["L0_attn_rel_emb"].shape[1] // 2
    L["rel"] = a["L0_attn_rel_emb"][:, mid - SEQ + 1:mid + SEQ, :, 0].transpose(2, 0, 1)
    L["ident"] = np.eye(128, dtype=f)
    L["lin1_bias"] = a["L0_attn_lin1_b"].reshape(DFF // 128, 128).T
    L["vecs"] = np.stack([a["L0_attn_" + n] for n in ("ln1_g", "ln1_b", "ln2_g", "ln2_b", "lin2_b")])
    F = {n: a["L0_ffn_" + n] for n in "gate_w gate_b W1 B1 W3 B3 W2 B2 Ws1 Bs1 Ws3 Bs3 Ws2 Bs2".split()}
    cat = lambda w, shared: np.concatenate([w, shared[None]])
    parts = lambda w: [w[..., 0::2], w[..., 1::2]]
    w13 = np.concatenate(parts(cat(F["W1"], F["Ws1"])) + parts(cat(F["W3"], F["Ws3"])), -1)
    w13 = np.concatenate([w13.transpose(1, 0, 2).reshape(D, W13), F["gate_w"].T], 1)
    L["w13_a"], L["w13_b"] = two(w13)
    b13 = np.concatenate(parts(cat(F["B1"], F["Bs1"])) + parts(cat(F["B3"], F["Bs3"])), -1)
    L["b13"] = np.concatenate([b13.reshape(W13), np.zeros(EXPERTS, f)])[None]
    L["w2"] = np.concatenate([cat(F["W2"], F["Ws2"]), cat(F["B2"], F["Bs2"])[:, None]], 1).transpose(1, 0, 2)
    L["gate_b"] = F["gate_b"][None]
    for n in (GROUPS, EXPERTS):
        L[f"lt{n}"] = np.broadcast_to(np.tril(np.ones((n, n), f), -1), (128, n, n))
    return L


def kernel(**inputs):
    import numpy as _np
    import concourse.bacc as _bacc
    from concourse.bass_utils import run_bass_kernel_spmd as _run

    nc = _bacc.Bacc("TRN2", target_bir_lowering=False, num_devices=1)
    arrays, T = {}, {}
    for name, a in layouts({k: _np.asarray(v) for k, v in inputs.items()}).items():
        a = _np.ascontiguousarray(a)
        arrays[f"in_{name}"] = a
        T[name] = nc.dram_tensor(f"in_{name}", a.shape, mybir.dt.from_np(a.dtype), kind="ExternalInput").ap()
    out = nc.dram_tensor("out", (SEQ, NTOK, D), F32, kind="ExternalOutput").ap()
    build(nc, T, out)
    r = _run(nc, [arrays], core_ids=[0])
    return r.results[0]["out"]
```

```python
from contextlib import ExitStack

import concourse.bass as bass
from concourse import mybir

F32 = mybir.dt.float32
F32R = mybir.dt.float32r
ALU = mybir.AluOpType
ACT = mybir.ActivationFunctionType
AX = mybir.AxisListType

SEQ, NPATCH, NTXT, D = 32, 196, 77, 192
NTOK = NPATCH + NTXT
HEADS, DQ, DFF = 8, 96, 768
EXPERTS, INNER, GROUPS = 8, 96, 4
EPS = 1e-5
IMG, PATCH, GRID = 224, 16, 14
ROW = IMG + 2
WIN = 54
HALF = 9
KWIN = 64 + WIN
NMEAN = 5 * 3 * PATCH * PATCH
TILES = 3
STEP_TOK = 4 * TILES
STEPS = -(-NTOK // STEP_TOK)
PADTOK = STEPS * STEP_TOK
ROWS = TILES * 128
QKV = 3 * HEADS * DQ
REL = 2 * SEQ - 1
NEXP = EXPERTS + 1
KSEL = 32 + NEXP
FT = -(-NEXP * INNER // 128)
W13 = FT * 4 * 128
WCOL = W13 + EXPERTS
BIG = 1e30


def wait(eng, sem, value):
    if not isinstance(value, int) or value > 0:
        eng.wait_ge(sem, value)


def stand(eng, passed):
    eng.sem_inc(passed, 1)


def wait_alone(eng, sem, value, passed):
    wait(eng, sem, value)
    if not isinstance(value, int):
        stand(eng, passed)


class Chain:

    def __init__(self, eng, sem, per):
        self.eng, self.sem, self.per, self.k, self.base = eng, sem, per, 0, 0

    def start(self, step, k=0):
        self.base, self.k = step * self.per, k

    def link(self, ins):
        self.k += 1
        ins.then_inc(self.sem, 1)
        self.eng.wait_ge(self.sem, self.base + self.k)

    def end(self):
        assert self.k == self.per, (self.k, self.per)


def names(ctx, nc):
    return (lambda n, s, d=F32: ctx.enter_context(nc.sbuf_tensor(n, s, d)),
            lambda n, s, d=F32: ctx.enter_context(nc.psum_tensor(n, s, d)),
            lambda n: ctx.enter_context(nc.semaphore(n)))


class Weights:
    pass


def attention_weights(sb, const):
    p = Weights()
    p.w_hi, p.w_lo, p.w_low = [sb(n, [128, QKV], F32R) for n in ("w_hi", "w_lo", "w_low")]
    p.l1_hi, p.l1_lo, p.l1_low = [sb(n, [128, DFF], F32R) for n in ("l1_hi", "l1_lo", "l1_low")]
    p.wo, p.lin2 = sb("wo", [DQ, HEADS, D]), sb("lin2", [128, DFF // 128, D])
    p.rel, p.l1b, p.vecs = sb("rel", [DQ, HEADS, REL]), sb("l1b", [128, DFF // 128]), sb("vecs", [128, 5, D])
    p.ident = const
    p.loads = [(p.wo[:], "wo"),
               (p.lin2[:], "lin2"), (p.rel[:], "rel"), (p.l1b[:], "lin1_bias"), (p.ident[:], "ident"),
               (p.vecs[:], "vecs")]
    return p


def expert_weights(sb, const):
    p = Weights()
    p.raw_a, p.raw_b = [sb("m_" + n, [128, WCOL]) for n in ("raw_a", "raw_b")]
    p.w2, p.sel = sb("m_w2", [128, FT, D]), sb("m_sel_f", [KSEL, FT, 128])
    p.b13, p.gate_b = sb("m_b13", [128, FT, 4]), sb("m_gate_b", [128, EXPERTS])
    p.lt4, p.lt8 = sb("m_lt4", [128, GROUPS, GROUPS]), sb("m_lt8", [128, EXPERTS, EXPERTS])
    p.ident = const
    p.loads = [(p.raw_a[:], "w13_a"), (p.raw_b[:], "w13_b"), (p.w2[:], "w2"),
               (p.sel[:], "sel"), (p.b13[:], "b13"), (p.lt4[:], "lt4"), (p.lt8[:], "lt8"), (p.gate_b[:], "gate_b")]
    return p


def embed_phase(nc, T, hs, att):
    NT, NW = NPATCH // 4, 5 * HALF
    EDGES = (0, 1, 7, 8)
    with ExitStack() as ctx:
        sb, ps, sem = names(ctx, nc)
        shifts = sb("shifts", [KWIN, 5, HALF, D + 2])
        wk = sb("wk", [KWIN, HALF, D + 1])
        cnt = sb("cnt", [KWIN, HALF])
        cntsq = sb("cntsq", [KWIN, 5])
        ones = sb("ones", [128, 128])
        xb = sb("xb", [KWIN, 2, 128, HALF])
        sq = sb("sq", [KWIN, 2, 128, HALF])
        rows = sb("rows", [KWIN, 2, 128])
        zero = sb("zero", [128, D])
        c0row = sb("c0row", [1, 2, D])
        c0 = sb("c0", [128, D])
        c1 = sb("c1", [128, D])
        mhalf = sb("mhalf", [128, 1])
        st = sb("st", [128, 4])
        rstd = sb("rstd", [128, 1])
        tmp = sb("tmp", [128, D])
        ho = sb("ho", [128, 2, D])
        raw_a, raw_b = [sb(n, [128, QKV + DFF]) for n in ("raw_a", "raw_b")]
        acc = ps("acc", [128, 2, 512])
        pc = ps("pc", [128, 2, 512])
        w_in, txt_in, x_zero, x_sq, win_done = [sem("e_" + n) for n in (
            "w_in", "txt_in", "x_zero", "x_sq", "win_done")]
        row_done, emb_done, mean_done, rstd_done, h_done = [sem("e_" + n) for n in (
            "row_done", "emb_done", "mean_done", "rstd_done", "h_done")]
        x_in = [sem(f"e_x_in{u}") for u in range(2)]
        h_out = [sem(f"e_h_out{u}") for u in range(2)]
        cst, cst_sb, beta_done, beta_sb, steps, psteps = [sem("e_" + n) for n in (
            "cst", "cst_sb", "beta_done", "beta_sb", "steps", "psteps")]
        att_in, att_hi = sem("e_att_in"), sem("e_att_hi")
        block = ctx.enter_context(nc.Block())
        chunks = [(att.w_hi, att.w_lo, att.w_low, slice(c, c + 384), slice(c, c + 384)) for c in range(0, QKV, 384)]
        chunks += [(att.l1_hi, att.l1_lo, att.l1_low, slice(c, c + 384), slice(QKV + c, QKV + c + 384))
                   for c in range(0, DFF, 384)]
        loads = [(raw_a[:, 0:QKV], "wqkv_a"), (raw_b[:, 0:QKV], "wqkv_b"), (raw_a[:, QKV:], "lin1_a"),
                 (raw_b[:, QKV:], "lin1_b2")] + att.loads

        def tiles(eng, body, after=None):
            for n in range(3):
                body(n, n % 2, n // 2)
                if after:
                    after(n)
            with eng.Fori(1, NT // 2) as i:
                body(i * 2 + 1, 1, i)
                body(i * 2 + 2, 0, i + 1)

        @block.sync
        def _(sp):
            sp.dma_start(shifts[:, :, :, :], T["shift_w"].rearrange("s p k d -> p s k d")).then_inc(w_in, 16)
            sp.dma_start(cnt[:, :], T["count_w"]).then_inc(w_in, 16)
            sp.dma_start(cntsq[:, :], T["count_sq"]).then_inc(w_in, 16)
            sp.dma_start(c0row[:, 1, :], T["tok_b"]).then_inc(w_in, 16)
            sp.dma_start(hs[NPATCH:NTOK].rearrange("b t d -> t b d"), T["txt"]).then_inc(txt_in, 16)
            sp.wait_ge(x_zero, 1)
            sp.dma_start(hs[NTOK:PADTOK].rearrange("b t d -> (b t) d"),
                         zero[0:(PADTOK - NTOK) * SEQ, :]).then_inc(txt_in, 16)
            sp.wait_ge(x_zero, 2)

            def body(n, u, v):
                wait(sp, emb_done, n - 1)
                wait(sp, x_sq, n - 1)
                src = T["xw"][bass.ds(n, 1)]
                for h in range(2):
                    sp.dma_start(xb[64 * h:64 * h + WIN, u, :, :], src[:, h * WIN:(h + 1) * WIN].rearrange(
                        "o p (r k) -> (o p) r k", k=HALF)).then_inc(x_in[u], 16)

            def load(n):
                if n == 0:
                    for dst, name in loads:
                        rows = T[name]
                        if name == "vecs":
                            rows = rows.broadcast_to([128, 5, D])
                        sp.dma_start(dst, rows).then_inc(att_in, 16)

            tiles(sp, body, load)
            sp.wait_ge(att_in, 16 * len(loads))

        @block.scalar
        def _(act):
            act.wait_ge(beta_done, 1)
            act.activation(c0row[:, 0, :], pc[0:1, 0, 0:D], ACT.Copy).then_inc(beta_sb, 1)

            def body(n, u, v):
                act.wait_ge(x_in[u], (v + 1) * 32)
                wait(act, emb_done, n - 1)
                act.activation(sq[:, u, :, :], xb[:, u, :, :], ACT.Square).then_inc(x_sq, 1)
                if isinstance(n, int) and n == 0:
                    return
                store(n - 1, 1 - u)

            def store(n, u):
                act.wait_ge(h_done, n + 1)
                act.dma_start(hs[bass.ds(n * 4, 4)].rearrange("b t d -> (b t) d"), ho[:, u, :]).then_inc(h_out[u], 16)

            def split(n):
                if n == 0:
                    act.wait_ge(att_in, 16 * len(loads))
                for k in range(3 * n, min(3 * n + 3, len(chunks))):
                    hi, lo, low, c, raw = chunks[k]
                    act.activation(hi[:, c], raw_a[:, raw], ACT.Copy)
                    act.activation(low[:, c], raw_b[:, raw], ACT.Copy).then_inc(att_hi, 1)

            tiles(act, body, split)
            store(NT - 1, 0)
            act.wait_ge(h_out[0], 16 * (NT // 2 + 1))
            act.wait_ge(h_out[1], 16 * (NT // 2))
            act.wait_ge(txt_in, 32)

        @block.gpsimd
        def _(pool):
            pool.memset(mhalf[:, :], -0.5).then_inc(psteps, 1)
            pool.wait_ge(psteps, 1)

            def body(n, u, v):
                pool.wait_ge(mean_done, n + 1)
                pool.tensor_tensor(rstd[:, :], st[:, 3:4], mhalf[:, :], ALU.pow).then_inc(rstd_done, 1)

            tiles(pool, body)

        @block.vector
        def _(dve):
            dve.memset(zero[:, :], 0.0).then_inc(x_zero, 1)
            dve.memset(ones[:, :], 1.0)
            dve.memset(xb[32:64, :, :, :], 0.0).then_inc(x_zero, 1)
            dve.wait_ge(w_in, 64)
            dve.tensor_copy(wk[:, :, D], cnt[:, :])
            done = 0
            for s in range(5):
                if s:
                    dve.wait_ge(steps, done)
                for k in range(HALF):
                    w, g = shifts[:, s, k, 0:D], shifts[:, s, k, D:D + 1]
                    if s == 0:
                        ins = dve.tensor_scalar(wk[:, k, 0:D], w, g, None, ALU.mult)
                    else:
                        ins = dve.scalar_tensor_tensor(wk[:, k, 0:D], w, g, wk[:, k, 0:D], ALU.mult, ALU.add)
                    ins.then_inc(steps, 1)
                    done += 1
            dve.wait_ge(steps, done)
            dve.wait_ge(beta_sb, 1)
            dve.tensor_tensor(c0row[:, 0, :], c0row[:, 0, :], c0row[:, 1, :], ALU.add).then_inc(win_done, 1)
            dve.wait_ge(cst, 1)
            dve.tensor_copy(c0[:, :], pc[:, 0, 0:D])
            dve.tensor_copy(c1[:, :], pc[:, 1, 0:D]).then_inc(cst_sb, 1)
            dve.wait_ge(cst_sb, 1)
            K = 5

            def body(n, u, v):
                dve.wait_ge(x_sq, n + 1)
                wait(dve, emb_done, n - 1)
                dve.tensor_reduce(rows[:, u, :], sq[:, u, :, :], AX.X, ALU.add).then_inc(row_done, 1)
                dve.wait_ge(emb_done, n + 1)
                b = done + n * K
                dve.tensor_scalar(st[:, 0:1], acc[:, u, D:D + 1], -1.0 / NMEAN, None, ALU.mult).then_inc(steps, 1)
                dve.tensor_scalar(st[:, 1:2], acc[:, u, D + 1:D + 2], 1.0 / NMEAN, None, ALU.mult).then_inc(steps, 1)
                dve.wait_ge(steps, b + 2)
                dve.tensor_tensor(st[:, 2:3], st[:, 0:1], st[:, 0:1], ALU.mult).then_inc(steps, 1)
                dve.wait_ge(steps, b + 3)
                dve.tensor_tensor(st[:, 2:3], st[:, 1:2], st[:, 2:3], ALU.subtract).then_inc(steps, 1)
                dve.wait_ge(steps, b + 4)
                wait(dve, rstd_done, n)
                dve.tensor_scalar(st[:, 3:4], st[:, 2:3], 0.0, EPS, ALU.max, ALU.add).then_inc(mean_done, 1)
                dve.scalar_tensor_tensor(tmp[:, :], c1[:, :], st[:, 0:1], acc[:, u, 0:D], ALU.mult,
                                         ALU.add).then_inc(steps, 1)
                dve.wait_ge(steps, b + 5)
                dve.wait_ge(rstd_done, n + 1)
                wait(dve, h_out[u], v * 16)
                dve.scalar_tensor_tensor(ho[:, u, :], tmp[:, :], rstd[:, :], c0[:, :], ALU.mult,
                                         ALU.add).then_inc(h_done, 1)

            def split(n):
                for k in range(3 * n, min(3 * n + 3, len(chunks))):
                    hi, lo, low, c, raw = chunks[k]
                    dve.wait_ge(att_hi, k + 1)
                    dve.tensor_tensor(lo[:, c], raw_a[:, raw], hi[:, c].bitcast(F32), ALU.subtract)
                    dve.tensor_tensor(low[64:128, c], raw_b[64:128, raw], low[64:128, c].bitcast(F32), ALU.subtract)

            tiles(dve, body, split)

        @block.tensor
        def _(pe):
            pe.wait_ge(w_in, 64)
            for s in range(5):
                for k in range(HALF):
                    m = pe.matmul(pc[0:1, 0, 0:D], shifts[:, s, k, D + 1:D + 2], shifts[:, s, k, 0:D],
                                  start=(s + k == 0), stop=(s * HALF + k == NW - 1))
            m.then_inc(beta_done, 1)
            pe.wait_ge(win_done, 1)
            pe.matmul(pc[:, 0, 0:D], ones[0:1, :], c0row[:, 0, :], start=True, stop=True)
            for k in range(HALF):
                m = pe.matmul(pc[:, 1, 0:D], ones[0:KWIN, :], wk[:, k, 0:D], start=(k == 0), stop=(k == HALF - 1))
            m.then_inc(cst, 1)

            def body(n, u, v):
                pe.wait_ge(x_in[u], (v + 1) * 32)
                wait(pe, h_done, n - 1)
                for k in range(HALF):
                    pe.matmul(acc[:, u, 0:D + 1], xb[:, u, :, k], wk[:, k, :], start=(k == 0), stop=(k == HALF - 1))
                pe.wait_ge(row_done, n + 1)
                m = pe.matmul(acc[:, u, D + 1:D + 2], rows[:, u, :], cntsq[:, 0:1], start=True, stop=False)
                for e, k in enumerate(EDGES):
                    m = pe.matmul(acc[:, u, D + 1:D + 2], sq[:, u, :, k], cntsq[:, e + 1:e + 2],
                                  start=False, stop=(k == EDGES[-1]))
                m.then_inc(emb_done, 1)

            tiles(pe, body)


def attention_phase(nc, T, hs, h2, pre, experts_pre):
    SCALE = DQ ** -0.5
    FRONT, BACK = 27, 14
    ATT, PROJ, X1T, FF1, FF2, RING = 0, 6, 9, 11, 17, 21
    PITCH = HEADS * REL + SEQ
    rel_d = nc.dram_tensor("rel_d", (4 * TILES * SEQ * (PITCH - 1) + PITCH,), F32, kind="Internal").ap()
    with ExitStack() as ctx:
        sb, ps, sem = names(ctx, nc)
        w_hi, w_lo, w_low, l1_hi, l1_lo, l1_low = pre.w_hi, pre.w_lo, pre.w_low, pre.l1_hi, pre.l1_lo, pre.l1_low
        wo, lin2, rel, l1b, vecs, ident = pre.wo, pre.lin2, pre.rel, pre.l1b, pre.vecs, pre.ident
        mhalf = sb("mhalf2", [128, TILES])
        h = sb("h", [128, TILES, D])
        hres = sb("hres", [128, TILES, D])
        src = sb("src", [128, TILES, 256])
        res = sb("res", [128, TILES, D])
        y = sb("y", [128, TILES, D])
        x1 = sb("x1", [128, TILES, 256])
        x1b = sb("x1b", [128, TILES, D])
        h2o = sb("h2o", [128, TILES, D])
        s_hi, s_lo, s_low, s_tail = [sb(n, [128, ROWS], F32R) for n in ("s_hi", "s_lo", "s_low", "s_tail")]
        x_hi, x_lo, x_low, x_tail = [sb(n, [128, ROWS], F32R) for n in ("x_hi", "x_lo", "x_low", "x_tail")]
        qk = sb("qk", [128, 2, HEADS, ROWS])
        relp = sb("relp", [128, TILES, HEADS, REL])
        pos = sb("pos", [128, TILES, HEADS, SEQ])
        logit = sb("logit", [128, TILES * HEADS, SEQ])
        prob = sb("prob", [128, TILES * HEADS, SEQ])
        bd = sb("bd", [128, TILES * HEADS, 128])
        v = sb("v", [128, TILES, HEADS * DQ])
        oT = sb("oT", [DQ, TILES, HEADS, 128])
        hT = sb("hT", [128, DFF // 128, ROWS])
        mx = sb("mx", [128, TILES * HEADS])
        sm = sb("sm", [128, TILES * HEADS])
        bn = sb("bn", [128, TILES, 6])
        mv = sb("mv", [128, TILES, 2])
        ve = sb("ve", [128, TILES])
        rstd = sb("rstd2", [128, TILES])
        src_mv = sb("src_mv", [128, TILES, 2])
        src_ve = sb("src_ve", [128, TILES])
        src_rstd = sb("src_rstd", [128, TILES])
        fr = ps("fr", [128, 3, 512])
        bk = ps("bk", [128, 3, 512])
        lg = ps("lg", [128, 2, 512])
        (pre_in, set_up, h_in, hres_in, h2_out, front_done, front_free, back_done,
         back_free, lg_done, lg_free, acc_done, acc_free, src_norm, src_rows, src_lo, x1_norm, x1_done, x1_lo,
         x1b_done, res_done, hb_done, max_done, sub_done, exp_done, inv_done, prob_done, bd_done, var_src, rstd_src,
         var_1, rstd_1, var_2, rstd_2, h2_done, tail_steps, ln1_steps, src_steps, ln2_steps) = [
            sem("a_" + n) for n in (
                "pre_in set_up h_in hres_in h2_out front_done front_free back_done "
                "back_free lg_done lg_free acc_done acc_free src_norm src_rows src_lo x1_norm x1_done x1_lo "
                "x1b_done res_done hb_done max_done sub_done exp_done inv_done prob_done bd_done var_src rstd_src "
                "var_1 rstd_1 var_2 rstd_2 h2_done tail_steps ln1_steps src_steps ln2_steps").split()]
        passed = sem("a_passed")
        pool_set_up = sem("a_pool_set_up")
        rel_out = [sem(f"a_rel_out{t}") for t in range(TILES)]
        pos_in = [sem(f"a_pos_in{t}") for t in range(TILES)]
        block = ctx.enter_context(nc.Block())
        LN1G, LN1B, LN2G, LN2B, LIN2B = range(5)
        rows_of = lambda t, s: t[bass.ds(s * STEP_TOK, STEP_TOK)].rearrange("b t d -> (b t) d").rearrange(
            "(k p) d -> p k d", p=128)
        bcast = lambda vec: vecs[:, vec, :].unsqueeze(1).broadcast_to([128, TILES, D])

        def program(eng, step, first=None):
            if first:
                first()
            step(0, True, False, True)
            step(1, True, True, True)
            with eng.Fori(2, STEPS - 1) as i:
                step(i, True, True, True)
            step(STEPS - 1, True, True, False)
            step(STEPS, False, True, False)

        @block.sync
        def _(sp):
            sp.dma_start(h[:, :, :], rows_of(hs, 0)).then_inc(h_in, 16)
            for dst, name in experts_pre.loads:
                rows = T[name]
                if name == "gate_b":
                    rows = rows.broadcast_to([128, EXPERTS])
                sp.dma_start(dst, rows).then_inc(pre_in, 16)

            def step(i, front, back, nxt):
                j, n = i - 1, i + 1
                if nxt:
                    wait_alone(sp, src_rows, i + 1, passed)
                    sp.dma_start(h[:, :, :], rows_of(hs, n)).then_inc(h_in, 16)
                if back:
                    wait_alone(sp, h2_done, j, passed)
                    sp.dma_start(hres[:, :, :], rows_of(hs, j)).then_inc(hres_in, 16)
                if front:
                    for t in range(TILES):
                        wait_alone(sp, front_free, i * FRONT + 19 + t, passed)
                        wait_alone(sp, pos_in[t], i * 16, passed)
                        there = bass.AP(rel_d.tensor, t * 128 * (PITCH - 1),
                                        [[SEQ * (PITCH - 1), 4], [PITCH, SEQ], [1, HEADS * REL]])
                        sp.dma_start(there, relp[:, t, :, :].rearrange("p h m -> p (h m)")).then_inc(rel_out[t], 16)
                    wait_alone(sp, lg_free, i * 6, passed)
                    for t in range(TILES):
                        wait_alone(sp, rel_out[t], (i + 1) * 16, passed)
                        skew = bass.AP(rel_d.tensor, t * 128 * (PITCH - 1) + SEQ - 1,
                                       [[PITCH - 1, 128], [REL, HEADS], [1, SEQ]])
                        sp.dma_start(pos[:, t, :, :], skew).then_inc(pos_in[t], 16)
                if back:
                    wait_alone(sp, h2_done, j + 1, passed)
                    sp.dma_start(rows_of(h2, j), h2o[:, :, :]).then_inc(h2_out, 16)

            program(sp, step)
            sp.wait_ge(h2_out, 16 * STEPS)
            sp.wait_ge(pre_in, 16 * len(experts_pre.loads))

        @block.tensor
        def _(pe):
            def ring_front(s, k):
                wait(pe, front_free, s * FRONT + k - 2)
                return fr[:, k % 3, :]

            def ring_back(s, k):
                before, p = (s, k - 3) if k >= 3 else (s - 1, k - 3 + RING)
                if p < PROJ:
                    wait(pe, back_free, before * BACK + p + 1)
                elif p < X1T:
                    wait(pe, acc_free, before * 6 + p - PROJ + 1)
                elif p < FF2:
                    wait(pe, back_free, before * BACK + 6 + p - X1T + 1)
                elif p < FF2 + TILES:
                    wait(pe, acc_free, before * 6 + 3 + p - FF2 + 1)
                return bk[:, k % 3, :]

            def five(out, lhs, rhs):
                for n, (a, b) in enumerate(zip(lhs, rhs)):
                    m = pe.matmul(out, a, b, start=(n == 0), stop=(n == 4))
                return m

            xs = lambda c: [s_hi[:, c], s_lo[:, c], s_hi[:, c], s_low[:, c], s_tail[:, c]]
            ws = lambda c: [w_hi[:, c], w_hi[:, c], w_lo[:, c], w_low[:, c], w_low[:, c]]
            xf = lambda c: [x_hi[:, c], x_lo[:, c], x_hi[:, c], x_low[:, c], x_tail[:, c]]
            wf = lambda c: [l1_hi[:, c], l1_hi[:, c], l1_lo[:, c], l1_low[:, c], l1_low[:, c]]
            tile = lambda t: slice(128 * t, 128 * t + 128)

            def src_t(s):
                pe.wait_ge(src_norm, s + 1)
                for k in range(2):
                    bank = ring_front(s, k)
                    for t in range(TILES):
                        m = pe.transpose(bank[:, tile(t)], src[:, t, 128 * k:128 * k + 128], ident[:, :])
                    m.then_inc(front_done, 1)

            def qk_proj(s):
                pe.wait_ge(front_free, s * FRONT + 2)
                pe.wait_ge(src_lo, s + 1)
                for k in range(2 * HEADS):
                    bank = ring_front(s, 2 + k)
                    col = (k % 2) * HEADS * DQ + (k // 2) * DQ
                    five(bank[0:DQ, 0:ROWS], ws(slice(col, col + DQ)), xs(slice(0, ROWS))).then_inc(front_done, 1)

            def rel_proj(s, t):
                if t == 0:
                    pe.wait_ge(front_free, s * FRONT + 18)
                bank = ring_front(s, 18 + t)
                for hd in range(HEADS):
                    m = pe.matmul(bank[:, 64 * hd:64 * hd + REL], qk[0:DQ, 0, hd, tile(t)], rel[:, hd, :],
                                  start=True, stop=True)
                m.then_inc(front_done, 1)

            def attend(s, t):
                if t == 0:
                    pe.wait_ge(bd_done, s + 1)
                    pe.wait_ge(front_free, (s + 1) * FRONT)
                for k in (2 * t, 2 * t + 1):
                    bank = ring_back(s, ATT + k)
                    for q in range(4):
                        hd = 4 * (k % 2) + q
                        m = pe.matmul(bank[0:DQ, tile(q)], v[:, k // 2, DQ * hd:DQ * hd + DQ],
                                      bd[:, k // 2 * HEADS + hd, :], start=True, stop=True)
                    m.then_inc(back_done, 1)

            def out_proj(s):
                for t in range(TILES):
                    pe.wait_ge(back_free, s * BACK + 2 * t + 2)
                    bank = ring_back(s, PROJ + t)
                    for hd in range(HEADS):
                        m = pe.matmul(bank[:, 0:D], oT[:, t, hd, :], wo[:, hd, :],
                                      start=(hd == 0), stop=(hd == HEADS - 1))
                    m.then_inc(acc_done, 1)

            def v_proj(s):
                for k in range(6):
                    bank = ring_front(s, 21 + k)
                    col = 2 * HEADS * DQ + (k % 2) * 384
                    five(bank[:, 0:384], xs(tile(k // 2)), ws(slice(col, col + 384))).then_inc(front_done, 1)

            def scores(s, ks):
                for k in ks:
                    wait(pe, lg_free, s * 6 + k - 1)
                    for q in range(4):
                        hd = 4 * (k % 2) + q
                        m = pe.matmul(lg[:, k % 2, tile(q)], qk[0:DQ, 0, hd, tile(k // 2)],
                                      qk[0:DQ, 1, hd, tile(k // 2)], start=True, stop=True)
                    m.then_inc(lg_done, 1)

            def x1_t(s):
                pe.wait_ge(x1_done, s + 1)
                for k in range(2):
                    bank = ring_back(s, X1T + k)
                    for t in range(TILES):
                        m = pe.transpose(bank[:, tile(t)], x1[:, t, 128 * k:128 * k + 128], ident[:, :])
                    m.then_inc(back_done, 1)

            def ffn1(s):
                pe.wait_ge(back_free, s * BACK + 8)
                pe.wait_ge(x1_lo, s + 1)
                for c in range(DFF // 128):
                    bank = ring_back(s, FF1 + c)
                    five(bank[:, 0:ROWS], wf(tile(c)), xf(slice(0, ROWS))).then_inc(back_done, 1)

            def ffn2(s):
                pe.wait_ge(back_free, s * BACK + BACK)
                for t in range(TILES):
                    bank = ring_back(s, FF2 + t)
                    for c in range(DFF // 128):
                        m = pe.matmul(bank[:, 0:D], hT[:, c, tile(t)], lin2[:, c, :],
                                      start=(c == 0), stop=(c == DFF // 128 - 1))
                    m.then_inc(acc_done, 1)

            def step(i, front, back, nxt):
                j, n = i - 1, i + 1
                if front:
                    qk_proj(i)
                for t in range(TILES):
                    if back:
                        attend(j, t)
                    if front:
                        rel_proj(i, t)
                if back:
                    out_proj(j)
                if front:
                    v_proj(i)
                    scores(i, (0, 1))
                if back:
                    x1_t(j)
                if front:
                    scores(i, (2, 3))
                if nxt:
                    src_t(n)
                if front:
                    scores(i, (4, 5))
                if back:
                    ffn1(j)
                    ffn2(j)

            def first():
                src_t(0)

            program(pe, step, first)

        @block.scalar
        def _(act):
            def evac(s, k, out, inp, func=ACT.Copy, **kw):
                act.wait_ge(front_done, s * FRONT + k + 1)
                act.activation(out, inp, func, **kw).then_inc(front_free, 1)

            def evac_back(s, k, out, inp, func=ACT.Copy, **kw):
                act.wait_ge(back_done, s * BACK + k + 1)
                act.activation(out, inp, func, **kw).then_inc(back_free, 1)

            def src_hi(s):
                evac(s, 0, s_hi[:, :], fr[:, 0, 0:ROWS])
                evac(s, 1, s_low[:, :], fr[:, 1, 0:ROWS])

            def step(i, front, back, nxt):
                j, n = i - 1, i + 1
                if front:
                    for k in range(2 * HEADS):
                        evac(i, 2 + k, qk[0:DQ, k % 2, k // 2, :], fr[0:DQ, (2 + k) % 3, 0:ROWS])
                for t in range(TILES):
                    if back:
                        for k in (2 * t, 2 * t + 1):
                            evac_back(j, k, oT[:, t, 4 * (k % 2):4 * (k % 2) + 4, :],
                                      bk[0:DQ, (ATT + k) % 3, :].rearrange("p (h r) -> p h r", h=4))
                    if front:
                        wait(act, rel_out[t], i * 16)
                        evac(i, 18 + t, relp[:, t, :, :],
                             fr[:, (18 + t) % 3, :].rearrange("p (h m) -> p h m", m=64)[:, :, 0:REL])
                if front:
                    for k in range(6):
                        evac(i, 21 + k, v[:, k // 2, 384 * (k % 2):384 * (k % 2) + 384], fr[:, (21 + k) % 3, 0:384])
                    wait(act, acc_free, i * 6 - 3)
                    act.wait_ge(src_rows, i + 1)
                    act.activation(res[:, :, :], src[:, :, 0:D], ACT.Copy).then_inc(res_done, 1)
                if back:
                    evac_back(j, 6, x_hi[:, :], bk[:, X1T % 3, 0:ROWS])
                    evac_back(j, 7, x_low[:, :], bk[:, (X1T + 1) % 3, 0:ROWS])
                if nxt:
                    src_hi(n)
                if back:
                    for c in range(DFF // 128):
                        evac_back(j, 8 + c, hT[:, c, :], bk[:, (FF1 + c) % 3, 0:ROWS], ACT.Relu, bias=l1b[:, c:c + 1])
                if front:
                    act.wait_ge(sub_done, i + 1)
                    wait(act, bd_done, i)
                    act.activation(prob[:, :, :], logit[:, :, :], ACT.Exp).then_inc(exp_done, 1)

            def first():
                src_hi(0)

            program(act, step, first)

        @block.gpsimd
        def _(pool):
            def power(s, var, rst, out=rstd, of=ve):
                pool.wait_ge(var, s + 1)
                pool.tensor_tensor(out[:, :], of[:, :], mhalf[:, :], ALU.pow).then_inc(rst, 1)

            def src_power(s):
                power(s, var_src, rstd_src, src_rstd, src_ve)

            def src_rows_of(s):
                pool.wait_ge(src_rows, s + 1)
                stand(pool, passed)
                pool.tensor_copy(src[:, :, 192:256], src[:, :, 128:192]).then_inc(src_norm, 1)

            def step(i, front, back, nxt):
                j, n = i - 1, i + 1
                if back:
                    pool.wait_ge(inv_done, j + 1)
                    pool.tensor_tensor(prob[:, :, :], prob[:, :, :],
                                       sm[:, :].unsqueeze(2).broadcast_to([128, TILES * HEADS, SEQ]),
                                       ALU.mult).then_inc(prob_done, 1)
                if nxt:
                    src_power(n)
                if back:
                    power(j, var_1, rstd_1)
                    pool.wait_ge(x1_norm, j + 1)
                    stand(pool, passed)
                    pool.tensor_copy(x1[:, :, 192:256], x1[:, :, 128:192]).then_inc(x1_done, 1)
                if nxt:
                    src_rows_of(n)
                if back:
                    pool.tensor_tensor(x1b[:, :, :], x1[:, :, 0:D], bcast(LIN2B), ALU.add).then_inc(x1b_done, 1)
                    pool.wait_ge(hres_in, (j + 1) * 16)
                    pool.tensor_tensor(hres[:, :, :], hres[:, :, :], bcast(LN2B), ALU.add).then_inc(hb_done, 1)
                if front:
                    pool.wait_ge(max_done, i + 1)
                    pool.tensor_tensor(logit[:, :, :], logit[:, :, :],
                                       mx[:, :].unsqueeze(2).broadcast_to([128, TILES * HEADS, SEQ]),
                                       ALU.subtract).then_inc(sub_done, 1)
                if back:
                    power(j, var_2, rstd_2)

            def first():
                pool.memset(mhalf[:, :], -0.5)
                pool.memset(bd[:, :, :], 0.0).then_inc(pool_set_up, 1)
                pool.wait_ge(pool_set_up, 1)
                src_power(0)
                src_rows_of(0)

            program(pool, step, first)

        @block.vector
        def _(dve):
            tail_c = Chain(dve, tail_steps, 1)
            ln1_c, src_c, ln2_c = Chain(dve, ln1_steps, 4), Chain(dve, src_steps, 2), Chain(dve, ln2_steps, 4)

            def moments(chain, rows, var, s, mv=mv, ve=ve):
                for t in range(TILES):
                    ins = dve.bn_stats(bn[:, t, :], rows(t))
                chain.link(ins)
                stand(dve, passed)
                for t in range(TILES):
                    ins = dve.bn_aggr(mv[:, t, :], bn[:, t, :])
                chain.link(ins)
                dve.tensor_scalar(ve[:, :], mv[:, :, 1], EPS, None, ALU.add).then_inc(var, 1)

            def src_moments(s):
                src_c.start(s)
                dve.wait_ge(h_in, (s + 1) * 16)
                moments(src_c, lambda t: h[:, t, :], var_src, s, src_mv, src_ve)
                src_c.end()

            def src_rows_of(s):
                dve.wait_ge(rstd_src, s + 1)
                wait(dve, res_done, s)
                for t in range(TILES):
                    ins = dve.tensor_scalar(src[:, t, 0:D], h[:, t, :], src_mv[:, t, 0:1], src_rstd[:, t:t + 1],
                                            ALU.subtract, ALU.mult)
                ins.then_inc(src_rows, 1)

            def src_lo_of(s):
                dve.wait_ge(front_free, s * FRONT + 2)
                dve.tensor_tensor(s_lo[:, :], fr[:, 0, 0:ROWS], s_hi[:, :].bitcast(F32), ALU.subtract)
                dve.tensor_tensor(s_tail[0:64, :], fr[0:64, 1, 0:ROWS], s_low[0:64, :].bitcast(F32),
                                  ALU.subtract).then_inc(src_lo, 1)

            def softmax_tail(s):
                tail_c.start(s)
                dve.wait_ge(exp_done, s + 1)
                tail_c.link(dve.tensor_reduce(sm[:, :], prob[:, :, :], AX.X, ALU.add))
                tail_c.end()
                dve.reciprocal(sm[:, :], sm[:, :]).then_inc(inv_done, 1)
                dve.wait_ge(prob_done, s + 1)
                wait(dve, back_done, s * BACK - 8)
                for g in range(4):
                    p = slice(32 * g, 32 * g + 32)
                    ins = dve.transpose(bd[p, :, 32 * g:32 * g + 32], prob[p, :, :])
                ins.then_inc(bd_done, 1)

            def add_norm(chain, s, base, use, other, ready, var, rst, gain, plus, out, done):
                chain.start(s)
                dve.wait_ge(ready, s + 1)
                for t in range(TILES):
                    dve.wait_ge(acc_done, s * 6 + base + t + 1)
                    ins = dve.tensor_tensor(y[:, t, :], bk[:, (use + t) % 3, 0:D], other(t), ALU.add)
                    ins.then_inc(acc_free, 1)
                dve.wait_ge(acc_free, s * 6 + base + 3)
                moments(chain, lambda t: y[:, t, :], var, s)
                for t in range(TILES):
                    ins = dve.scalar_tensor_tensor(y[:, t, :], y[:, t, :], mv[:, t, 0:1], vecs[:, gain, :],
                                                   ALU.subtract, ALU.mult)
                chain.link(ins)
                dve.wait_ge(rst, s + 1)
                for t in range(TILES):
                    ins = dve.scalar_tensor_tensor(out(t), y[:, t, :], rstd[:, t:t + 1], plus(t), ALU.mult, ALU.add)
                chain.link(ins)
                chain.end()
                dve.sem_inc(done, 1)

            def ln1(s):
                wait(dve, x1b_done, s)
                add_norm(ln1_c, s, 0, PROJ, lambda t: res[:, t, :], res_done, var_1, rstd_1, LN1G,
                         lambda t: vecs[:, LN1B, :], lambda t: x1[:, t, 0:D], x1_norm)

            def ln2(s):
                dve.wait_ge(hb_done, s + 1)
                wait(dve, h2_out, s * 16)
                add_norm(ln2_c, s, 3, FF2, lambda t: x1b[:, t, :], x1b_done, var_2, rstd_2, LN2G,
                         lambda t: hres[:, t, :], lambda t: h2o[:, t, :], h2_done)

            def extract(s, ks):
                if ks[0] == 0:
                    wait(dve, exp_done, s)
                for k in ks:
                    dve.wait_ge(lg_done, s * 6 + k + 1)
                    t, h0 = k // 2, 4 * (k % 2)
                    dve.wait_ge(pos_in[t], (s + 1) * 16)
                    for g in range(4):
                        p = slice(32 * g, 32 * g + 32)
                        ins = dve.scalar_tensor_tensor(
                            logit[p, t * HEADS + h0:t * HEADS + h0 + 4, :],
                            lg[p, k % 2, :].rearrange("p (h c) -> p h c", h=4)[:, :, 32 * g:32 * g + 32], SCALE,
                            pos[p, t, h0:h0 + 4, :], ALU.mult, ALU.add)
                    ins.then_inc(lg_free, 1)

            def x1_lo_of(s):
                dve.wait_ge(back_free, s * BACK + 8)
                dve.tensor_tensor(x_lo[:, :], bk[:, X1T % 3, 0:ROWS], x_hi[:, :].bitcast(F32), ALU.subtract)
                dve.tensor_tensor(x_tail[0:64, :], bk[0:64, (X1T + 1) % 3, 0:ROWS], x_low[0:64, :].bitcast(F32),
                                  ALU.subtract).then_inc(x1_lo, 1)

            def step(i, front, back, nxt):
                j, n = i - 1, i + 1
                if back:
                    softmax_tail(j)
                if nxt:
                    src_moments(n)
                if back:
                    ln1(j)
                if nxt:
                    src_rows_of(n)
                if front:
                    extract(i, (0, 1))
                if back:
                    x1_lo_of(j)
                if front:
                    extract(i, (2, 3))
                if nxt:
                    src_lo_of(n)
                if front:
                    extract(i, (4, 5))
                    dve.wait_ge(lg_free, (i + 1) * 6)
                    dve.tensor_reduce(mx[:, :], logit[:, :, :], AX.X, ALU.max).then_inc(max_done, 1)
                if back:
                    ln2(j)

            def first():
                dve.memset(s_tail[64:128, :].bitcast(F32), 0.0)
                dve.memset(x_tail[64:128, :].bitcast(F32), 0.0).then_inc(set_up, 1)
                src_moments(0)
                src_rows_of(0)
                src_lo_of(0)
                dve.wait_ge(set_up, 1)
                dve.wait_ge(pool_set_up, 1)

            program(dve, step, first)


def experts_phase(nc, T, h2, out, pre):
    LAG = 3
    ALPHA, LIMIT = 1.702, 7.0
    G2 = EXPERTS // GROUPS
    LAST = NEXP * INNER - (FT - 1) * 128
    with ExitStack() as ctx:
        sb, ps, sem = names(ctx, nc)
        w_hi, w_lo, w_low = [sb("m_" + n, [128, WCOL], F32R) for n in ("w_hi", "w_lo", "w_low")]
        w2, sel_f = pre.w2, pre.sel
        b13, gate_b, lt4, lt8, ident = pre.b13, pre.gate_b, pre.lt4, pre.lt8, pre.ident
        sel = sb("m_sel", [KSEL, FT, 128], F32R)
        mhalf = sb("m_mhalf", [128, TILES])
        h = sb("m_h", [128, TILES, D])
        hres = sb("m_hres", [128, TILES, D])
        z = sb("m_z", [128, TILES, 256])
        z_hi, z_lo_b, z_low, z_tail = [sb("m_" + n, [128, 2, ROWS], F32R) for n in ("z_hi", "z_lo", "z_low", "z_tail")]
        h1 = sb("m_h1", [128, 2, 2, ROWS])
        hx = sb("m_hx", [128, FT, 2, ROWS])
        sg = sb("m_sg", [128, FT, ROWS])
        gT = sb("m_gT", [128, FT, ROWS])
        wT = sb("m_wT", [64, ROWS], F32R)
        ho = sb("m_ho", [128, TILES, D])
        bn, mv = sb("m_bn", [128, TILES, 6]), sb("m_mv", [128, TILES, 2])
        ve, rstd = sb("m_ve", [128, TILES]), sb("m_rstd", [128, TILES])
        lgt, score, s8, s8m = [sb("m_" + n, [128, TILES, EXPERTS]) for n in ("lgt", "score", "s8", "s8m")]
        w = sb("m_w", [128, TILES, 128])
        m1, gs, cnt4 = sb("m_m1", [128, TILES]), sb("m_gs", [128, TILES, GROUPS]), sb("m_cnt4", [128, TILES, GROUPS])
        cnt8 = sb("m_cnt8", [128, TILES, EXPERTS])
        gt4, ge4 = [sb("m_" + n, [128, TILES, GROUPS, GROUPS]) for n in ("gt4", "ge4")]
        gt8, ge8 = [sb("m_" + n, [128, TILES, EXPERTS, EXPERTS]) for n in ("gt8", "ge8")]
        p1 = ps("m_p1", [128, 2, 512])
        p3 = ps("m_p3", [128, 2, 512])
        ring = ps("m_ring", [128, 4, 512])
        (hi_done, w_done, ready, pool_ready, h_in, res_in, z_rows, z_norm, z_hi_done, z_lo_done,
         var_done, rstd_done, h1_done, h1_copied, h3_done, hh_done, xg_done, xl_done, sg_done, g1_done, g_done,
         ring_done, ring_free, wt_hi, wt_done, b2_done, add_done, gate_in, gate_exp, gate_w, gate_steps,
         ln_steps, passed) = [
            sem("m_" + n) for n in (
                "hi_done w_done ready pool_ready h_in res_in z_rows z_norm z_hi_done z_lo_done "
                "var_done rstd_done h1_done h1_copied h3_done hh_done xg_done xl_done sg_done g1_done g_done "
                "ring_done ring_free wt_hi wt_done b2_done add_done gate_in gate_exp gate_w gate_steps "
                "ln_steps passed").split()]
        o_out = [sem(f"m_o_out{t}") for t in range(TILES)]
        block = ctx.enter_context(nc.Block())
        tile = lambda t: slice(128 * t, 128 * t + 128)
        chunk = lambda f: slice(512 * f, 512 * f + 512 if f < FT - 1 else WCOL)
        rows_of = lambda t, s: t[bass.ds(s * STEP_TOK, STEP_TOK)].rearrange("b t d -> (b t) d").rearrange(
            "(k p) d -> p k d", p=128)

        WB = [f"WB{f}" for f in range(FT)]
        OUT = [f"OUT{t}" for t in range(TILES)]
        ORDER = WB[0:3] + ["WT", WB[3], OUT[0], "Z0", "Z1", WB[4], OUT[1], "GATE", WB[5], OUT[2], WB[6]]
        USES = len(ORDER)
        NEXT = ("Z0", "Z1", "GATE")

        def uses_of(s):
            if s < 0:
                return NEXT
            lacks = (WB[0:LAG] + OUT if s == 0 else []) + (list(NEXT) if s == STEPS - 1 else [])
            return [k for k in ORDER if k not in lacks] if s < STEPS else WB[0:LAG] + OUT

        def use(s, k):
            if isinstance(s, int):
                return sum(len(uses_of(x)) for x in range(-1, s)) + list(uses_of(s)).index(k)
            return s * USES + use(1, k) - USES

        def bank(s, u, k):
            return (use(s, k) if isinstance(s, int) else use(2 - u, k)) % 4

        def weighting(s, f):
            return (True, f + FT - LAG) if f < LAG else (False, f - LAG)

        def program(eng, step, first, last):
            first()
            for s in range(3):
                step(s, s % 2)
            with eng.Fori(1, (STEPS - 3) // 2) as i:
                step(i * 2 + 1, 1)
                step(i * 2 + 2, 0)
            for s in range(1 + 2 * ((STEPS - 3) // 2), STEPS):
                step(s, s % 2)
            last()

        is_last = lambda s: isinstance(s, int) and s == STEPS - 1
        is_first = lambda s: isinstance(s, int) and s == 0

        @block.sync
        def _(sp):
            sp.dma_start(h[:, :, :], rows_of(h2, 0)).then_inc(h_in, 16)

            def step(s, u):
                if not (isinstance(s, int) and s >= STEPS - 2):
                    wait_alone(sp, z_rows, s + 2, passed)
                    sp.dma_start(h[:, :, :], rows_of(h2, s + 2)).then_inc(h_in, 16)
                if not is_first(s):
                    store(s - 1, 4)

            def store(s, rows):
                wait_alone(sp, add_done, s * TILES, passed)
                sp.dma_start(hres[:, :, :], rows_of(h2, s)).then_inc(res_in, 16)
                for t in range(TILES):
                    wait_alone(sp, add_done, s * TILES + t + 1, passed)
                    r = rows if t == TILES - 1 else 4
                    sp.dma_start(out[:, bass.ds(s * STEP_TOK + 4 * t, r), :].rearrange("t b d -> b t d"),
                                 ho[0:32 * r, t, :]).then_inc(o_out[t], 16)

            def last():
                store(STEPS - 1, NTOK - STEP_TOK * (STEPS - 1) - 4 * (TILES - 1))
                for t in range(TILES):
                    sp.wait_ge(o_out[t], 16 * STEPS)

            def first():
                sp.wait_ge(z_rows, 1)
                sp.dma_start(h[:, :, :], rows_of(h2, 1)).then_inc(h_in, 16)

            program(sp, step, first, last)

        @block.tensor
        def _(pe):
            xs = lambda u, c: [z_hi[:, u, c], z_lo_b[:, u, c], z_hi[:, u, c], z_low[:, u, c], z_tail[:, u, c]]
            ws = lambda c: [w_hi[:, c], w_hi[:, c], w_lo[:, c], w_low[:, c], w_low[:, c]]

            def five(out, lhs, rhs):
                for k, (a, b) in enumerate(zip(lhs, rhs)):
                    m = pe.matmul(out, a, b, start=(k == 0), stop=(k == 4))
                return m

            def free_bank(s, u, k):
                wait(pe, ring_free, use(s, k) - 3)
                return ring[:, bank(s, u, k), :]

            def unit(s, u, f):
                n = s * FT + f
                wait(pe, h1_copied, n)
                for half in range(2):
                    m = five(p1[:, half, 0:ROWS], ws(tile(4 * f + half)), xs(u, slice(0, ROWS)))
                m.then_inc(h1_done, 1)
                wait(pe, hh_done, n)
                for half in range(2):
                    m = five(p3[:, half, 0:ROWS], ws(tile(4 * f + 2 + half)), xs(u, slice(0, ROWS)))
                m.then_inc(h3_done, 1)

            def weight(s, u, f, k):
                b = free_bank(s, u, k)
                pe.matmul(b[:, 0:ROWS], sel[:, f, :], wT[0:KSEL, :], start=True, stop=True).then_inc(ring_done, 1)

            def turn_weights(s, u):
                pe.wait_ge(gate_w, s + 1)
                b = free_bank(s, u, "WT")
                for t in range(TILES):
                    m = pe.transpose(b[:, tile(t)], w[:, t, :], ident[:, :])
                m.then_inc(ring_done, 1)

            def turn_rows(s, u):
                pe.wait_ge(z_norm, s + 2)
                for k in range(2):
                    b = free_bank(s, u, f"Z{k}")
                    for t in range(TILES):
                        m = pe.transpose(b[:, tile(t)], z[:, t, 128 * k:128 * k + 128], ident[:, :])
                    m.then_inc(ring_done, 1)

            def gate(s, u):
                pe.wait_ge(z_lo_done, s + 2)
                b = free_bank(s, u, "GATE")
                for t in range(TILES):
                    m = five(b[:, EXPERTS * t:EXPERTS * t + EXPERTS], xs(1 - u, tile(t)), ws(slice(W13, WCOL)))
                m.then_inc(ring_done, 1)

            def second(s, u, t):
                if t == 0:
                    pe.wait_ge(g_done, s * FT)
                    pe.wait_ge(b2_done, s)
                b = free_bank(s, u, OUT[t])
                for f in range(FT):
                    k = 128 if f < FT - 1 else LAST + NEXP
                    m = pe.matmul(b[:, 0:D], gT[0:k, f, tile(t)], w2[0:k, f, :], start=(f == 0), stop=(f == FT - 1))
                m.then_inc(ring_done, 1)

            def step(s, u):
                for f in range(FT):
                    unit(s, u, f)
                    back, g = weighting(s, f)
                    if not (back and is_first(s)):
                        if f == LAG:
                            pe.wait_ge(wt_done, s + 1)
                        weight(s, u, g, WB[f])
                    if f == 2:
                        turn_weights(s, u)
                    if f >= 3 and f < 6 and not is_first(s):
                        second(s, u, f - 3)
                    if f == 3 and not is_last(s):
                        turn_rows(s, u)
                    if f == 4 and not is_last(s):
                        gate(s, u)

            def first():
                turn_rows(-1, 1)
                pe.wait_ge(w_done, FT)
                gate(-1, 1)

            def last():
                for f in range(LAG):
                    weight(STEPS, STEPS % 2, weighting(STEPS, f)[1], WB[f])
                for t in range(TILES):
                    second(STEPS, STEPS % 2, t)

            program(pe, step, first, last)

        @block.scalar
        def _(act):
            def z_hi_of(s, u):
                for k, dst in enumerate((z_hi, z_low)):
                    act.wait_ge(ring_done, use(s, f"Z{k}") + 1)
                    ins = act.activation(dst[:, 1 - u, :], ring[:, bank(s, u, f"Z{k}"), 0:ROWS], ACT.Copy)
                ins.then_inc(z_hi_done, 1)

            def copy(s, u, f):
                n = s * FT + f
                act.wait_ge(h1_done, n + 1)
                wait(act, hh_done, n - 1)
                for half in range(2):
                    ins = act.activation(h1[:, (FT * u + f) % 2, half, :], p1[:, half, 0:ROWS], ACT.Identity,
                                         bias=b13[:, f, half:half + 1])
                ins.then_inc(h1_copied, 1)

            def sigmoid(n, f):
                act.wait_ge(xg_done, n + 1)
                act.activation(sg[:, f, :], hx[:, f, 0, :], ACT.Sigmoid, scale=ALPHA).then_inc(sg_done, 1)

            def gate_exp_of(s):
                act.wait_ge(gate_in, s + 1)
                act.activation(score[:, :, :], lgt[:, :, :], ACT.Exp).then_inc(gate_exp, 1)

            def step(s, u):
                for f in range(FT):
                    copy(s, u, f)
                    if f == 5 and not is_last(s):
                        gate_exp_of(s + 1)
                    if f:
                        sigmoid(s * FT + f - 1, f - 1)
                    elif not is_first(s):
                        sigmoid(s * FT - 1, FT - 1)
                    if f == 2:
                        act.wait_ge(ring_done, use(s, "WT") + 1)
                        act.activation(wT[:, :], ring[0:64, bank(s, u, "WT"), 0:ROWS], ACT.Copy).then_inc(wt_hi, 1)
                    if f == 3 and not is_last(s):
                        z_hi_of(s, u)

            def first():
                z_hi_of(-1, 1)
                for f in range(FT):
                    c = chunk(f)
                    act.activation(w_hi[:, c], pre.raw_a[:, c], ACT.Copy)
                    act.activation(w_low[:, c], pre.raw_b[:, c], ACT.Copy).then_inc(hi_done, 1)
                act.activation(sel[:, :, :], sel_f[:, :, :], ACT.Copy).then_inc(hi_done, 1)
                gate_exp_of(0)

            def last():
                sigmoid(STEPS * FT - 1, FT - 1)

            program(act, step, first, last)

        @block.gpsimd
        def _(pool):
            def clip(n, f):
                pool.wait_ge(hh_done, n + 1)
                stand(pool, passed)
                pool.tensor_scalar(hx[:, f, 1, :], hx[:, f, 1, :], LIMIT, -LIMIT, ALU.min, ALU.max).then_inc(xl_done, 1)

            def product(n, f, s, k):
                p = 128 if f < FT - 1 else LAST
                pool.wait_ge(g1_done, n + 1)
                pool.wait_ge(ring_free, use(s, k) + 1)
                if f == 0 and not is_first(s):
                    pool.wait_ge(ring_done, use(s, OUT[TILES - 1]) + 1)
                pool.tensor_tensor(gT[0:p, f, :], hx[0:p, f, 1, :], sg[0:p, f, :], ALU.mult).then_inc(g_done, 1)

            def step(s, u):
                for f in range(FT):
                    clip(s * FT + f, f)
                    if f == 4 and not (isinstance(s, int) and s >= STEPS - 2):
                        power(s + 2)
                    back, g = weighting(s, f)
                    if not (back and is_first(s)):
                        product(s * FT + f - LAG, g, s, WB[f])
                    if f == 0 and not is_last(s):
                        double(s + 1)

            def power(s):
                pool.wait_ge(var_done, s + 1)
                pool.tensor_tensor(rstd[:, :], ve[:, :], mhalf[:, :], ALU.pow).then_inc(rstd_done, 1)

            def double(s):
                pool.wait_ge(z_rows, s + 1)
                stand(pool, passed)
                pool.tensor_copy(z[:, :, 192:256], z[:, :, 128:192]).then_inc(z_norm, 1)

            def first():
                pool.memset(mhalf[:, :], -0.5).then_inc(pool_ready, 1)
                pool.wait_ge(pool_ready, 1)
                power(0)
                double(0)
                power(1)

            def last():
                for f in range(LAG):
                    product(STEPS * FT + f - LAG, weighting(STEPS, f)[1], STEPS, WB[f])

            program(pool, step, first, last)

        @block.vector
        def _(dve):
            ln_c, gate_c = Chain(dve, ln_steps, 2), Chain(dve, gate_steps, 16)

            def moments(s):
                ln_c.start(s)
                dve.wait_ge(h_in, (s + 1) * 16)
                for t in range(TILES):
                    ins = dve.bn_stats(bn[:, t, :], h[:, t, :])
                ln_c.link(ins)
                stand(dve, passed)
                for t in range(TILES):
                    ins = dve.bn_aggr(mv[:, t, :], bn[:, t, :])
                ln_c.link(ins)
                ln_c.end()
                dve.tensor_scalar(ve[:, :], mv[:, :, 1], EPS, None, ALU.add).then_inc(var_done, 1)

            def normalise(s):
                dve.wait_ge(rstd_done, s + 1)
                if not is_first(s):
                    dve.wait_ge(z_lo_done, s)
                for t in range(TILES):
                    ins = dve.tensor_scalar(z[:, t, 0:D], h[:, t, :], mv[:, t, 0:1], rstd[:, t:t + 1],
                                            ALU.subtract, ALU.mult)
                ins.then_inc(z_rows, 1)

            def z_lo_of(s, u):
                dve.wait_ge(z_hi_done, s + 2)
                dve.tensor_tensor(z_lo_b[:, 1 - u, :], ring[:, bank(s, u, "Z0"), 0:ROWS],
                                  z_hi[:, 1 - u, :].bitcast(F32), ALU.subtract).then_inc(ring_free, 1)
                dve.tensor_tensor(z_tail[0:64, 1 - u, :], ring[0:64, bank(s, u, "Z1"), 0:ROWS],
                                  z_low[0:64, 1 - u, :].bitcast(F32), ALU.subtract).then_inc(ring_free, 1)
                dve.wait_ge(ring_free, use(s, "Z1") + 1)
                dve.sem_inc(z_lo_done, 1)

            def product(s, u, f):
                n = s * FT + f
                dve.wait_ge(h1_copied, n + 1)
                dve.wait_ge(h3_done, n + 1)
                wait(dve, g_done, n - FT + 1)
                for half in range(2):
                    ins = dve.scalar_tensor_tensor(hx[:, f, half, :], p3[:, half, 0:ROWS], b13[:, f, 2 + half:3 + half],
                                                   h1[:, (FT * u + f) % 2, half, :], ALU.add, ALU.mult)
                ins.then_inc(hh_done, 1)
                dve.wait_ge(hh_done, n + 1)
                dve.tensor_scalar(hx[:, f, 0, :], hx[:, f, 0, :], LIMIT, None, ALU.min).then_inc(xg_done, 1)

            def weigh(n, f, s, u, k):
                dve.wait_ge(xl_done, n + 1)
                dve.wait_ge(xg_done, n + 1)
                dve.scalar_tensor_tensor(hx[:, f, 1, :], hx[:, f, 1, :], 1.0, hx[:, f, 0, :], ALU.add,
                                         ALU.mult).then_inc(g1_done, 1)
                p, b = 128, ring[:, bank(s, u, k), :]
                dve.wait_ge(ring_done, use(s, k) + 1)
                if f == FT - 1:
                    p = LAST
                    dve.tensor_copy(gT[LAST:LAST + NEXP, f, :], b[LAST:LAST + NEXP, 0:ROWS]).then_inc(b2_done, 1)
                dve.wait_ge(sg_done, n + 1)
                dve.tensor_tensor(sg[0:p, f, :], sg[0:p, f, :], b[0:p, 0:ROWS], ALU.mult).then_inc(ring_free, 1)

            def residual(s, u, t):
                dve.wait_ge(res_in, s * 16)
                dve.wait_ge(ring_done, use(s, OUT[t]) + 1)
                wait(dve, o_out[t], (s - 1) * 16)
                dve.tensor_tensor(ho[:, t, :], ring[:, bank(s, u, OUT[t]), 0:D], hres[:, t, :], ALU.add).then_inc(
                    ring_free, 1)
                dve.wait_ge(ring_free, use(s, OUT[t]) + 1)
                dve.sem_inc(add_done, 1)

            def before(a, count):
                shape = [128, TILES, count, count]
                return a.unsqueeze(2).broadcast_to(shape), a.unsqueeze(3).broadcast_to(shape)

            def rank(a, count, gt, ge, lt, cnt, part=slice(0, 4)):
                aj, ai = before(a, count)
                earlier = lt[:, :, :].unsqueeze(1).broadcast_to([128, TILES, count, count])
                if part.start == 0:
                    dve.tensor_tensor(gt[:, :, :, :], aj, ai, ALU.is_gt)
                for link in (lambda: dve.tensor_tensor(ge[:, :, :, :], aj, ai, ALU.is_ge),
                             lambda: dve.tensor_tensor(ge[:, :, :, :], ge[:, :, :, :], earlier, ALU.mult),
                             lambda: dve.tensor_tensor(gt[:, :, :, :], gt[:, :, :, :], ge[:, :, :, :], ALU.max),
                             lambda: dve.tensor_reduce(cnt[:, :, :], gt[:, :, :, :], AX.X, ALU.add))[part]:
                    gate_c.link(link())

            def gate_logits(s, u):
                gate_c.start(s + 1)
                dve.wait_ge(ring_done, use(s, "GATE") + 1)
                dve.tensor_copy(lgt[:, :, :], ring[:, bank(s, u, "GATE"), 0:TILES * EXPERTS].rearrange(
                    "p (t e) -> p t e", t=TILES)).then_inc(ring_free, 1)
                dve.wait_ge(ring_free, use(s, "GATE") + 1)
                gate_c.link(dve.tensor_reduce(m1[:, :], lgt[:, :, :], AX.X, ALU.max))
                dve.tensor_tensor(lgt[:, :, :], lgt[:, :, :], m1[:, :].unsqueeze(2).broadcast_to(
                    [128, TILES, EXPERTS]), ALU.subtract).then_inc(gate_in, 1)

            def gate_groups(s):
                wide = [128, TILES, EXPERTS]
                gate_c.start(s, 1)
                dve.wait_ge(gate_exp, s + 1)
                gate_c.link(dve.tensor_reduce(m1[:, :], score[:, :, :], AX.X, ALU.add))
                gate_c.link(dve.reciprocal(m1[:, :], m1[:, :]))
                gate_c.link(dve.tensor_tensor(score[:, :, :], score[:, :, :], m1[:, :].unsqueeze(2).broadcast_to(
                    wide), ALU.mult))
                gate_c.link(dve.tensor_tensor(s8[:, :, :], score[:, :, :], gate_b[:, :].unsqueeze(1).broadcast_to(
                    wide), ALU.add))
                gate_c.link(dve.tensor_reduce(gs[:, :, :], s8[:, :, :].rearrange("p t (g e) -> p t g e", e=G2),
                                              AX.X, ALU.add))
                rank(gs[:, :, :], GROUPS, gt4, ge4, lt4, cnt4)
                gate_c.link(dve.tensor_scalar(cnt4[:, :, :], cnt4[:, :, :], 2.0, -BIG, ALU.is_ge, ALU.mult))
                gate_c.link(dve.tensor_tensor(
                    s8m[:, :, :].rearrange("p t (g e) -> p t g e", e=G2),
                    s8[:, :, :].rearrange("p t (g e) -> p t g e", e=G2),
                    cnt4[:, :, :].unsqueeze(3).broadcast_to([128, TILES, GROUPS, G2]), ALU.add))

            def gate_experts(s):
                gate_c.start(s, 12)
                rank(s8m[:, :, :], EXPERTS, gt8, ge8, lt8, cnt8, slice(0, 2))

            def gate_weights(s):
                gate_c.start(s, 14)
                rank(s8m[:, :, :], EXPERTS, gt8, ge8, lt8, cnt8, slice(2, 4))
                gate_c.end()
                wait(dve, wt_hi, s)
                for at in (0, 32):
                    ins = dve.scalar_tensor_tensor(w[:, :, at:at + EXPERTS], cnt8[:, :, :], 2.0, score[:, :, :],
                                                   ALU.is_lt, ALU.mult)
                ins.then_inc(gate_w, 1)

            def step(s, u):
                for f in range(FT):
                    product(s, u, f)
                    back, g = weighting(s, f)
                    if not (back and is_first(s)):
                        weigh(s * FT + f - LAG, g, s, u, WB[f])
                    if f == 2:
                        dve.wait_ge(wt_hi, s + 1)
                        dve.tensor_tensor(wT[32:64, :], ring[32:64, bank(s, u, "WT"), 0:ROWS],
                                          wT[32:64, :].bitcast(F32), ALU.subtract).then_inc(ring_free, 1)
                        dve.wait_ge(ring_free, use(s, "WT") + 1)
                        dve.sem_inc(wt_done, 1)
                    if f >= 3 and f < 6 and not is_first(s):
                        residual(s, u, f - 3)
                    if f == 1:
                        gate_weights(s)
                    if f == 4 and not (isinstance(s, int) and s >= STEPS - 2):
                        moments(s + 2)
                    if not is_last(s):
                        if f == 0:
                            normalise(s + 1)
                        if f == 3:
                            z_lo_of(s, u)
                        if f == 4:
                            gate_logits(s, u)
                        if f == 5:
                            gate_groups(s + 1)
                        if f == 6:
                            gate_experts(s + 1)

            def first():
                dve.memset(z_tail[64:128, :, :].bitcast(F32), 0.0)
                dve.memset(w[:, :, :], 0.0).then_inc(ready, 1)
                dve.wait_ge(ready, 1)
                for at in (EXPERTS, 32 + EXPERTS):
                    ins = dve.memset(w[:, :, at:at + 1], 1.0)
                ins.then_inc(ready, 1)
                moments(0)
                normalise(0)
                z_lo_of(-1, 1)
                for f in range(FT):
                    c = chunk(f)
                    dve.wait_ge(hi_done, f + 1)
                    dve.tensor_tensor(w_lo[:, c], pre.raw_a[:, c], w_hi[:, c].bitcast(F32), ALU.subtract)
                    dve.tensor_tensor(w_low[64:128, c], pre.raw_b[64:128, c], w_low[64:128, c].bitcast(F32),
                                      ALU.subtract).then_inc(w_done, 1)
                dve.wait_ge(ready, 2)
                moments(1)
                gate_logits(-1, 1)
                gate_groups(0)
                gate_experts(0)

            def last():
                for f in range(LAG):
                    weigh(STEPS * FT + f - LAG, weighting(STEPS, f)[1], STEPS, STEPS % 2, WB[f])
                for t in range(TILES):
                    residual(STEPS, STEPS % 2, t)

            program(dve, step, first, last)


def build(nc, T, out):
    hs = nc.dram_tensor("hs", (PADTOK, SEQ, D), F32, kind="Internal").ap()
    h2 = nc.dram_tensor("h2", (PADTOK, SEQ, D), F32, kind="Internal").ap()
    with ExitStack() as ctx:
        sb, _, _ = names(ctx, nc)
        ident = sb("ident", [128, 128])
        experts = expert_weights(sb, ident)
        with ExitStack() as inner:
            attention = attention_weights(names(inner, nc)[0], ident)
            embed_phase(nc, T, hs, attention)
            attention_phase(nc, T, hs, h2, attention, experts)
        experts_phase(nc, T, h2, out, experts)


def layouts(a):
    import numpy as np
    f = np.float32
    L = {}
    x = np.pad(a["x"], ((0, 0), (0, 0), (1, 1), (1, 1)))
    cols = PATCH * np.arange(GRID)[:, None] + np.arange(PATCH + 2)
    x = x[:, :, :, cols][:, :, cols]
    x = x.transpose(1, 3, 2, 4, 0, 5).reshape(3, PATCH + 2, NPATCH // 4, 128, 2, HALF)
    x = np.concatenate([x[:, 1:17].reshape(48, *x.shape[2:]), x[:, 0], x[:, 17]])
    L["xw"] = x.transpose(1, 3, 0, 2, 4).reshape(NPATCH // 4, 2 * WIN, 128 * HALF)
    full = np.concatenate([a["L0_tok_W"], a["L0_tok_ln_gamma"][:, None], a["L0_tok_ln_beta"][:, None]], axis=1)
    full = full.reshape(PATCH, PATCH, 5, 3, D + 2)
    sw = np.zeros((5, 3, PATCH + 2, PATCH + 2, D + 2), f)
    cw = np.zeros((3, PATCH + 2, PATCH + 2), f)
    for s, (dy, dx) in enumerate([(0, 0), (0, -1), (0, 1), (-1, 0), (1, 0)]):
        sw[s, :, 1 + dy:17 + dy, 1 + dx:17 + dx] = full[:, :, s].transpose(2, 0, 1, 3)
        cw[:, 1 + dy:17 + dy, 1 + dx:17 + dx] += 1
    def window(w):
        lead = w.shape[:-4]
        w = np.concatenate([w[..., :, 1:17, :, :].reshape(*lead, 48, 18, w.shape[-1]), w[..., :, 0, :, :],
                            w[..., :, 17, :, :]], axis=-3)
        gap = np.zeros((*lead, 10, HALF, w.shape[-1]), f)
        return np.concatenate([w[..., 0:HALF, :], gap, w[..., HALF:, :]], axis=-3)
    L["shift_w"] = window(sw)
    L["count_w"] = window(cw[..., None])[..., 0]
    row = L["count_w"][:, 4:5]
    L["count_sq"] = np.concatenate([row, L["count_w"][:, [0, 1, 7, 8]] - row], axis=1)
    L["tok_b"] = a["L0_tok_b"].reshape(1, D)
    L["txt"] = a["txt"]
    q = np.concatenate([a["L0_attn_" + n].transpose(1, 0, 2).reshape(D, HEADS * DQ) for n in ("w_q", "w_k", "w_v")], 1)
    two = lambda w: (w[0:128], np.concatenate([w[128:], w[128:]]))
    L["wqkv_a"], L["wqkv_b"] = two(q)
    L["lin1_a"], L["lin1_b2"] = two(a["L0_attn_lin1_w"].T)
    L["wo"] = a["L0_attn_w_o"].transpose(1, 0, 2)
    L["lin2"] = a["L0_attn_lin2_w"].T.reshape(DFF // 128, 128, D).transpose(1, 0, 2)
    mid = a["L0_attn_rel_emb"].shape[1] // 2
    L["rel"] = a["L0_attn_rel_emb"][:, mid - SEQ + 1:mid + SEQ, :, 0].transpose(2, 0, 1)
    L["ident"] = np.eye(128, dtype=f)
    L["lin1_bias"] = a["L0_attn_lin1_b"].reshape(DFF // 128, 128).T
    L["vecs"] = np.stack([a["L0_attn_" + n] for n in ("ln1_g", "ln1_b", "ln2_g", "ln2_b", "lin2_b")])[None]
    F = {n: a["L0_ffn_" + n] for n in "gate_w gate_b W1 B1 W3 B3 W2 B2 Ws1 Bs1 Ws3 Bs3 Ws2 Bs2".split()}
    cat = lambda w, shared: np.concatenate([w, shared[None]])
    def by_tiles(w):
        w = np.stack([w[..., 0::2], w[..., 1::2]])
        w = w.transpose(0, 2, 1, 3).reshape(2, w.shape[2], NEXP * INNER)
        return np.pad(w, ((0, 0), (0, 0), (0, FT * 128 - NEXP * INNER))).reshape(2, -1, FT, 128)
    def both(w1, w3):
        w = np.concatenate([by_tiles(w1), by_tiles(w3)])
        return w.transpose(1, 2, 0, 3).reshape(w.shape[1], W13)
    w13 = both(cat(F["W1"], F["Ws1"]), cat(F["W3"], F["Ws3"]))
    L["w13_a"], L["w13_b"] = two(np.concatenate([w13, F["gate_w"].T], 1))
    b13 = both(cat(F["B1"], F["Bs1"])[:, None], cat(F["B3"], F["Bs3"])[:, None])
    L["b13"] = b13.reshape(FT, 4, 128).transpose(2, 0, 1)
    w2 = np.concatenate([cat(F["W2"], F["Ws2"]).reshape(NEXP * INNER, D), cat(F["B2"], F["Bs2"])])
    L["w2"] = np.pad(w2, ((0, FT * 128 - len(w2)), (0, 0))).reshape(FT, 128, D).transpose(1, 0, 2)
    sel = np.zeros((32 + NEXP, FT * 128), f)
    for e in range(NEXP):
        for row in (e, 32 + e):
            sel[row, e * INNER:(e + 1) * INNER] = 1
            sel[row, NEXP * INNER + e] = 1
    L["sel"] = sel.reshape(-1, FT, 128)
    L["gate_b"] = F["gate_b"][None]
    for n in (GROUPS, EXPERTS):
        L[f"lt{n}"] = np.broadcast_to(np.tril(np.ones((n, n), f), -1), (128, n, n))
    return L


def kernel(**inputs):
    import numpy as _np
    import concourse.bacc as _bacc
    from concourse.bass_utils import run_bass_kernel_spmd as _run

    nc = _bacc.Bacc("TRN2", target_bir_lowering=False, num_devices=1)
    arrays, T = {}, {}
    for name, a in layouts({k: _np.asarray(v) for k, v in inputs.items()}).items():
        a = _np.ascontiguousarray(a)
        arrays[f"in_{name}"] = a
        T[name] = nc.dram_tensor(f"in_{name}", a.shape, mybir.dt.from_np(a.dtype), kind="ExternalInput").ap()
    out = nc.dram_tensor("out", (SEQ, NTOK, D), F32, kind="ExternalOutput").ap()
    build(nc, T, out)
    r = _run(nc, [arrays], core_ids=[0])
    return r.results[0]["out"]
```

```python
from contextlib import ExitStack

import concourse.bass as bass
from concourse import mybir

F32 = mybir.dt.float32
F32R = mybir.dt.float32r
ALU = mybir.AluOpType
ACT = mybir.ActivationFunctionType
AX = mybir.AxisListType

SEQ, NPATCH, NTXT, D = 32, 196, 77, 192
NTOK = NPATCH + NTXT
HEADS, DQ, DFF = 8, 96, 768
EXPERTS, INNER, GROUPS = 8, 96, 4
EPS = 1e-5
PATCH, GRID = 16, 14
WIN = 54
HALF = 9
KWIN = 64 + WIN
NMEAN = 5 * 3 * PATCH * PATCH
TILES = 3
STEP_TOK = 4 * TILES
STEPS = -(-NTOK // STEP_TOK)
PADTOK = STEPS * STEP_TOK
ROWS = TILES * 128
QKV = 3 * HEADS * DQ
REL = 2 * SEQ - 1
NEXP = EXPERTS + 1
KSEL = 32 + NEXP
FT = -(-NEXP * INNER // 128)
W13 = FT * 4 * 128
WCOL = W13 + EXPERTS
BIG = 1e30


def wait(eng, sem, value):
    if not isinstance(value, int) or value > 0:
        eng.wait_ge(sem, value)


def stand(eng, passed):
    eng.sem_inc(passed, 1)


def wait_alone(eng, sem, value, passed):
    wait(eng, sem, value)
    if not isinstance(value, int):
        stand(eng, passed)


class Chain:

    def __init__(self, eng, sem, per):
        self.eng, self.sem, self.per, self.k, self.base = eng, sem, per, 0, 0

    def start(self, step, k=0):
        self.base, self.k = step * self.per, k

    def link(self, ins):
        self.k += 1
        ins.then_inc(self.sem, 1)
        self.eng.wait_ge(self.sem, self.base + self.k)

    def end(self):
        assert self.k == self.per, (self.k, self.per)


def names(ctx, nc):
    return (lambda n, s, d=F32: ctx.enter_context(nc.sbuf_tensor(n, s, d)),
            lambda n, s, d=F32: ctx.enter_context(nc.psum_tensor(n, s, d)),
            lambda n: ctx.enter_context(nc.semaphore(n)))


class Weights:
    pass


def attention_weights(sb, ident):
    p = Weights()
    p.w_hi, p.w_lo, p.w_low = [sb(n, [128, QKV], F32R) for n in ("w_hi", "w_lo", "w_low")]
    p.l1_hi, p.l1_lo, p.l1_low = [sb(n, [128, DFF], F32R) for n in ("l1_hi", "l1_lo", "l1_low")]
    p.wo = sb("wo", [DQ, HEADS, 2 * D], F32R)
    p.lin2 = sb("lin2", [128, DFF // 128, D])
    p.rel, p.l1b, p.vecs = sb("rel", [DQ, HEADS, REL]), sb("l1b", [128, DFF // 128]), sb("vecs", [128, 5, D])
    p.ident = ident
    p.loads = [(p.lin2[:], "lin2"), (p.rel[:], "rel"), (p.l1b[:], "lin1_bias"), (p.ident[:], "ident"),
               (p.vecs[:], "vecs")]
    return p


def expert_weights(sb, ident):
    p = Weights()
    p.raw_a, p.raw_b = [sb("m_" + n, [128, WCOL]) for n in ("raw_a", "raw_b")]
    p.b13, p.gate_b = sb("m_b13", [128, FT, 4]), sb("m_gate_b", [128, EXPERTS])
    p.lt4, p.lt8 = sb("m_lt4", [128, GROUPS, GROUPS]), sb("m_lt8", [128, EXPERTS, EXPERTS])
    p.ident = ident
    p.loads = [(p.raw_a[:], "w13_a"), (p.raw_b[:], "w13_b"), (p.b13[:], "b13"), (p.lt4[:], "lt4"),
               (p.lt8[:], "lt8"), (p.gate_b[:], "gate_b")]
    return p


def embed_phase(nc, T, hs, att):
    NT, NW = NPATCH // 4, 5 * HALF
    NB = 4
    EDGES = (0, 1, 7, 8)
    with ExitStack() as ctx:
        sb, ps, sem = names(ctx, nc)
        shifts = sb("shifts", [KWIN, 5, HALF, D + 2])
        wk = sb("wk", [KWIN, HALF, D + 1])
        cnt = sb("cnt", [KWIN, HALF])
        cntrt = sb("cntrt", [KWIN, 5])
        ones = sb("ones", [128, 128])
        xb = sb("xb", [KWIN, NB, 128, HALF])
        sq = sb("sq", [KWIN, 2, 128, HALF])
        rows = sb("rows", [KWIN, NB, 128])
        zero = sb("zero", [128, D])
        c0row = sb("c0row", [1, 2, D])
        c0 = sb("c0", [128, D])
        c1 = sb("c1", [128, D])
        mhalf = sb("mhalf", [128, 1])
        st = sb("st", [128, 4])
        rstd = sb("rstd", [128, 1])
        tmp = sb("tmp", [128, D])
        ho = sb("ho", [128, NB, D])
        raw_a, raw_b = [sb(n, [128, QKV + DFF]) for n in ("raw_a", "raw_b")]
        raw_o = sb("raw_o", [DQ, HEADS, D])
        acc = ps("acc", [128, NB, 512])
        pc = ps("pc", [128, 2, 512])
        cnt_in, txt_in, x_zero, x_sq, win_done = [sem("e_" + n) for n in (
            "cnt_in", "txt_in", "x_zero", "x_sq", "win_done")]
        row_done, main_done, emb_done, mean_done, rstd_done, h_done = [sem("e_" + n) for n in (
            "row_done", "main_done", "emb_done", "mean_done", "rstd_done", "h_done")]
        w_in = [sem(f"e_w_in{k}") for k in range(5)]
        x_in = [sem(f"e_x_in{u}") for u in range(NB)]
        h_out = [sem(f"e_h_out{u}") for u in range(NB)]
        cst, cst_sb, beta_done, beta_sb, steps, psteps = [sem("e_" + n) for n in (
            "cst", "cst_sb", "beta_done", "beta_sb", "steps", "psteps")]
        att_in, att_hi = sem("e_att_in"), sem("e_att_hi")
        block = ctx.enter_context(nc.Block())
        chunks = [(att.w_hi, att.w_lo, att.w_low, slice(c, c + 384), slice(c, c + 384)) for c in range(0, QKV, 384)]
        chunks += [(att.l1_hi, att.l1_lo, att.l1_low, slice(c, c + 384), slice(QKV + c, QKV + c + 384))
                   for c in range(0, DFF, 384)]
        loads = [(raw_a[:, 0:QKV], "wqkv_a"), (raw_b[:, 0:QKV], "wqkv_b"), (raw_a[:, QKV:], "lin1_a"),
                 (raw_b[:, QKV:], "lin1_b2"), (raw_o[:, :, :], "wo")] + att.loads

        def tiles(eng, body, early=None, late=None):
            for n in range(2 * NB + 1):
                body(n, n % NB, n // NB)
                if early:
                    early(n)
            with eng.Fori(2, NT // NB - len(chunks) // NB) as i:
                for k in range(NB):
                    body(i * NB + 1 + k, (1 + k) % NB, i + (1 + k) // NB)
            for c, n in enumerate(range(NT - len(chunks), NT)):
                body(n, n % NB, n // NB)
                if late:
                    late(c)

        @block.sync
        def _(sp):
            sp.dma_start(cnt[:, :], T["count_w"]).then_inc(cnt_in, 16)
            sp.dma_start(cntrt[:, :], T["count_rt"]).then_inc(cnt_in, 16)
            sp.dma_start(c0row[:, 1, :], T["tok_b"]).then_inc(cnt_in, 16)
            for k in range(5):
                sp.dma_start(shifts[:, k, :, :], T["shift_w"][k]).then_inc(w_in[k], 16)

            def body(n, u, v):
                if isinstance(n, int) and n == 0:
                    sp.wait_ge(x_zero, 2)
                wait(sp, main_done, n - NB + 1)
                wait(sp, x_sq, n - NB + 1)
                src = T["xw"][bass.ds(n, 1)]
                for h in range(2):
                    sp.dma_start(xb[64 * h:64 * h + WIN, u, :, :], src[:, h * WIN:(h + 1) * WIN].rearrange(
                        "o p (r k) -> (o p) r k", k=HALF)).then_inc(x_in[u], 16)

            def early(n):
                if n == NB:
                    sp.dma_start(hs[NPATCH:NTOK].rearrange("b t d -> t b d"), T["txt"]).then_inc(txt_in, 16)
                    sp.dma_start(hs[NTOK:PADTOK].rearrange("b t d -> (b t) d"),
                                 zero[0:(PADTOK - NTOK) * SEQ, :]).then_inc(txt_in, 16)
                for dst, name in loads[2 * (n - NB + 1):2 * (n - NB + 2)] if n >= NB - 1 else []:
                    src = T[name]
                    if name == "vecs":
                        src = src.broadcast_to([128, 5, D])
                    sp.dma_start(dst, src).then_inc(att_in, 16)

            tiles(sp, body, early)
            sp.wait_ge(att_in, 16 * len(loads))
            sp.wait_ge(txt_in, 32)

        @block.scalar
        def _(act):
            act.wait_ge(beta_done, 1)
            act.activation(c0row[:, 0, :], pc[0:1, 0, 0:D], ACT.Copy).then_inc(beta_sb, 1)
            act.wait_ge(cnt_in, 48)

            def body(n, u, v):
                first = isinstance(n, int) and n == 0
                act.wait_ge(x_in[u], (v + 1) * 32)
                wait(act, row_done, n - 1)
                b = u % 2
                act.activation(sq[:, b, :, 2:7], xb[:, u, :, 2:7], ACT.Square, scale=cntrt[:, 0:1])
                for e, k in enumerate(EDGES):
                    ins = act.activation(sq[:, b, :, k], xb[:, u, :, k], ACT.Square, scale=cntrt[:, e + 1:e + 2])
                ins.then_inc(x_sq, 1)
                if not (first or isinstance(n, int) and n == 1):
                    store(n - 2, (u - 2) % NB)

            def store(n, u):
                act.wait_ge(h_done, n + 1)
                act.dma_start(hs[bass.ds(n * 4, 4)].rearrange("b t d -> (b t) d"), ho[:, u, :]).then_inc(h_out[u], 16)

            def split(k):
                if k == 0:
                    act.wait_ge(att_in, 16 * len(loads))
                hi, lo, low, c, raw = chunks[k]
                act.activation(hi[:, c], raw_a[:, raw], ACT.Copy)
                act.activation(low[:, c], raw_b[:, raw], ACT.Copy).then_inc(att_hi, 1)
                if k == len(chunks) - 1:
                    act.activation(att.wo[:, :, 0:D], raw_o[:, :, :], ACT.Copy).then_inc(att_hi, 1)

            tiles(act, body, None, split)
            store(NT - 2, (NT - 2) % NB)
            store(NT - 1, (NT - 1) % NB)
            for u in range(NB):
                act.wait_ge(h_out[u], 16 * len(range(u, NT, NB)))

        @block.gpsimd
        def _(pool):
            pool.memset(mhalf[:, :], -0.5).then_inc(psteps, 1)
            pool.wait_ge(psteps, 1)

            def body(n, u, v):
                pool.wait_ge(mean_done, n + 1)
                pool.tensor_tensor(rstd[:, :], st[:, 3:4], mhalf[:, :], ALU.pow).then_inc(rstd_done, 1)

            def split(k):
                hi, lo, low, c, raw = chunks[k]
                pool.wait_ge(att_hi, k + 1)
                pool.tensor_tensor(lo[:, c], raw_a[:, raw], hi[:, c].bitcast(F32), ALU.subtract).then_inc(psteps, 1)
                pool.wait_ge(psteps, 2 * k + 2)
                pool.tensor_tensor(low[64:128, c], raw_b[64:128, raw], low[64:128, c].bitcast(F32),
                                   ALU.subtract).then_inc(psteps, 1)
                pool.wait_ge(psteps, 2 * k + 3)

            tiles(pool, body, None, split)

        @block.vector
        def _(dve):
            dve.memset(zero[:, :], 0.0).then_inc(x_zero, 1)
            dve.memset(xb[32:64, :, :, :], 0.0).then_inc(x_zero, 1)
            dve.memset(ones[:, :], 1.0)
            dve.wait_ge(cnt_in, 48)
            dve.tensor_copy(wk[:, :, D], cnt[:, :])
            done = 0
            for s in range(5):
                if s:
                    dve.wait_ge(steps, done)
                dve.wait_ge(w_in[s], 16)
                for k in range(HALF):
                    w, g = shifts[:, s, k, 0:D], shifts[:, s, k, D:D + 1]
                    if s == 0:
                        ins = dve.tensor_scalar(wk[:, k, 0:D], w, g, None, ALU.mult)
                    else:
                        ins = dve.scalar_tensor_tensor(wk[:, k, 0:D], w, g, wk[:, k, 0:D], ALU.mult, ALU.add)
                    ins.then_inc(steps, 1)
                    done += 1
            dve.wait_ge(steps, done)
            dve.wait_ge(beta_sb, 1)
            dve.tensor_tensor(c0row[:, 0, :], c0row[:, 0, :], c0row[:, 1, :], ALU.add).then_inc(win_done, 1)
            dve.wait_ge(cst, 1)
            dve.tensor_copy(c0[:, :], pc[:, 0, 0:D])
            dve.tensor_copy(c1[:, :], pc[:, 1, 0:D]).then_inc(cst_sb, 1)
            dve.wait_ge(cst_sb, 1)
            K = 4

            def body(n, u, v):
                dve.wait_ge(x_sq, n + 1)
                wait(dve, emb_done, n - NB + 1)
                dve.tensor_reduce(rows[:, u, :], sq[:, u % 2, :, :], AX.X, ALU.add).then_inc(row_done, 1)
                if not (isinstance(n, int) and n == 0):
                    finish(n - 1, (u - 1) % NB, v if u else v - 1)

            def finish(n, u, v):
                dve.wait_ge(emb_done, n + 1)
                b = done + n * K
                dve.tensor_scalar(st[:, 0:1], acc[:, u, D:D + 1], -1.0 / NMEAN, None, ALU.mult).then_inc(steps, 1)
                dve.wait_ge(steps, b + 1)
                dve.tensor_tensor(st[:, 1:2], st[:, 0:1], st[:, 0:1], ALU.mult).then_inc(steps, 1)
                dve.wait_ge(steps, b + 2)
                dve.scalar_tensor_tensor(st[:, 2:3], acc[:, u, D + 1:D + 2], 1.0 / NMEAN, st[:, 1:2], ALU.mult,
                                         ALU.subtract).then_inc(steps, 1)
                dve.wait_ge(steps, b + 3)
                wait(dve, rstd_done, n)
                dve.tensor_scalar(st[:, 3:4], st[:, 2:3], 0.0, EPS, ALU.max, ALU.add).then_inc(mean_done, 1)
                dve.scalar_tensor_tensor(tmp[:, :], c1[:, :], st[:, 0:1], acc[:, u, 0:D], ALU.mult,
                                         ALU.add).then_inc(steps, 1)
                dve.wait_ge(steps, b + 4)
                dve.wait_ge(rstd_done, n + 1)
                wait(dve, h_out[u], v * 16)
                dve.scalar_tensor_tensor(ho[:, u, :], tmp[:, :], rstd[:, :], c0[:, :], ALU.mult,
                                         ALU.add).then_inc(h_done, 1)

            tiles(dve, body)
            finish(NT - 1, (NT - 1) % NB, (NT - 1) // NB)
            dve.wait_ge(att_hi, len(chunks) + 1)
            dve.tensor_tensor(att.wo[:, :, D:], raw_o[:, :, :], att.wo[:, :, 0:D].bitcast(F32), ALU.subtract)

        @block.tensor
        def _(pe):
            for s in range(5):
                pe.wait_ge(w_in[s], 16)
                for k in range(HALF):
                    m = pe.matmul(pc[0:1, 0, 0:D], shifts[:, s, k, D + 1:D + 2], shifts[:, s, k, 0:D],
                                  start=(s + k == 0), stop=(s * HALF + k == NW - 1))
            m.then_inc(beta_done, 1)
            pe.wait_ge(win_done, 1)
            pe.matmul(pc[:, 0, 0:D], ones[0:1, :], c0row[:, 0, :], start=True, stop=True)
            for k in range(HALF):
                m = pe.matmul(pc[:, 1, 0:D], ones[0:KWIN, :], wk[:, k, 0:D], start=(k == 0), stop=(k == HALF - 1))
            m.then_inc(cst, 1)

            def body(n, u, v):
                pe.wait_ge(x_in[u], (v + 1) * 32)
                wait(pe, h_done, n - NB + 1)
                for k in range(HALF):
                    m = pe.matmul(acc[:, u, 0:D + 1], xb[:, u, :, k], wk[:, k, :], start=(k == 0),
                                  stop=(k == HALF - 1))
                m.then_inc(main_done, 1)
                if not (isinstance(n, int) and n == 0):
                    squares(n - 1, (u - 1) % NB)

            def squares(n, u):
                pe.wait_ge(row_done, n + 1)
                pe.matmul(acc[:, u, D + 1:D + 2], rows[:, u, :], ones[0:KWIN, 0:1], start=True, stop=True).then_inc(
                    emb_done, 1)

            tiles(pe, body)
            squares(NT - 1, (NT - 1) % NB)


def attention_phase(nc, T, hs, h2, pre, experts_pre):
    SCALE = DQ ** -0.5
    FRONT, BACK = 27, 14
    ATT, PROJ, X1T, FF1, FF2, RING = 0, 6, 9, 11, 17, 21
    PITCH = HEADS * REL + SEQ
    rel_d = nc.dram_tensor("rel_d", (4 * TILES * SEQ * (PITCH - 1) + PITCH,), F32, kind="Internal").ap()
    with ExitStack() as ctx:
        sb, ps, sem = names(ctx, nc)
        w_hi, w_lo, w_low, l1_hi, l1_lo, l1_low = pre.w_hi, pre.w_lo, pre.w_low, pre.l1_hi, pre.l1_lo, pre.l1_low
        wo, lin2, rel, l1b, vecs, ident = pre.wo, pre.lin2, pre.rel, pre.l1b, pre.vecs, pre.ident
        mhalf = sb("mhalf2", [128, TILES])
        h = sb("h", [128, TILES, D])
        hres = sb("hres", [128, TILES, D])
        src = sb("src", [128, TILES, 256])
        res = sb("res", [128, TILES, D])
        y = sb("y", [128, TILES, D])
        x1 = sb("x1", [128, TILES, 256])
        x1b = sb("x1b", [128, TILES, D])
        s_hi, s_lo, s_low, s_tail = [sb(n, [128, ROWS], F32R) for n in ("s_hi", "s_lo", "s_low", "s_tail")]
        x_hi, x_lo, x_low, x_tail = [sb(n, [128, ROWS], F32R) for n in ("x_hi", "x_lo", "x_low", "x_tail")]
        qk = sb("qk", [128, 2, HEADS, ROWS])
        relp = sb("relp", [128, TILES, HEADS, REL])
        pos = sb("pos", [128, TILES, HEADS, SEQ])
        logit = sb("logit", [128, TILES * HEADS, SEQ])
        prob = logit
        bd = sb("bd", [128, TILES * HEADS, 128])
        v = sb("v", [128, TILES, HEADS * DQ])
        o_hi, o_lo = [sb(n, [DQ, TILES, HEADS, 128], F32R) for n in ("o_hi", "o_lo")]
        hT = sb("hT", [128, DFF // 128, ROWS])
        mx = sb("mx", [128, TILES * HEADS])
        sm = sb("sm", [128, TILES * HEADS])
        bn = sb("bn", [128, TILES, 6])
        mv = sb("mv", [128, TILES, 2])
        ve = sb("ve", [128, TILES])
        rstd = sb("rstd2", [128, TILES])
        src_mv = sb("src_mv", [128, TILES, 2])
        src_ve = sb("src_ve", [128, TILES])
        src_rstd = sb("src_rstd", [128, TILES])
        fr = ps("fr", [128, 3, 512])
        bk = ps("bk", [128, 3, 512])
        lg = ps("lg", [128, 2, 512])
        (pre_in, set_up, h_in, hres_in, h2_out, front_done, front_free, back_done,
         back_free, o_done, half_done, lg_done, lg_free, acc_done, acc_free, src_rows, src_lo, x1_norm, x1_lo,
         x1b_done, res_done, hb_done, max_done, sub_done, exp_done, inv_done, prob_done, bd_done, var_src, rstd_src,
         var_1, rstd_1, var_2, rstd_2, h2_done, tail_steps, ln1_steps, src_steps, ln2_steps) = [
            sem("a_" + n) for n in (
                "pre_in set_up h_in hres_in h2_out front_done front_free back_done "
                "back_free o_done half_done lg_done lg_free acc_done acc_free src_rows src_lo x1_norm x1_lo "
                "x1b_done res_done hb_done max_done sub_done exp_done inv_done prob_done bd_done var_src rstd_src "
                "var_1 rstd_1 var_2 rstd_2 h2_done tail_steps ln1_steps src_steps ln2_steps").split()]
        passed = sem("a_passed")
        pool_set_up = sem("a_pool_set_up")
        rel_out = [sem(f"a_rel_out{t}") for t in range(TILES)]
        pos_in = [sem(f"a_pos_in{t}") for t in range(TILES)]
        block = ctx.enter_context(nc.Block())
        LN1G, LN1B, LN2G, LN2B, LIN2B = range(5)
        rows_of = lambda t, s: t[bass.ds(s * STEP_TOK, STEP_TOK)].rearrange("b t d -> (b t) d").rearrange(
            "(k p) d -> p k d", p=128)
        bcast = lambda vec: vecs[:, vec, :].unsqueeze(1).broadcast_to([128, TILES, D])

        def program(eng, step, first=None):
            if first:
                first()
            step(0, True, False, True)
            step(1, True, True, True)
            with eng.Fori(2, STEPS - 1) as i:
                step(i, True, True, True)
            step(STEPS - 1, True, True, False)
            step(STEPS, False, True, False)

        @block.sync
        def _(sp):
            sp.dma_start(h[:, :, :], rows_of(hs, 0)).then_inc(h_in, 16)
            for dst, name in experts_pre.loads:
                rows = T[name]
                if name == "gate_b":
                    rows = rows.broadcast_to([128, EXPERTS])
                sp.dma_start(dst, rows).then_inc(pre_in, 16)

            def step(i, front, back, nxt):
                j, n = i - 1, i + 1
                if nxt:
                    wait_alone(sp, src_rows, i + 1, passed)
                    sp.dma_start(h[:, :, :], rows_of(hs, n)).then_inc(h_in, 16)
                if back:
                    wait_alone(sp, h2_out, j * 16, passed)
                    sp.dma_start(hres[:, :, :], rows_of(hs, j)).then_inc(hres_in, 16)
                if front:
                    for t in range(TILES):
                        wait_alone(sp, front_free, i * FRONT + 19 + t, passed)
                        wait_alone(sp, pos_in[t], i * 16, passed)
                        there = bass.AP(rel_d.tensor, t * 128 * (PITCH - 1),
                                        [[SEQ * (PITCH - 1), 4], [PITCH, SEQ], [1, HEADS * REL]])
                        sp.dma_start(there, relp[:, t, :, :].rearrange("p h m -> p (h m)")).then_inc(rel_out[t], 16)
                    wait_alone(sp, lg_free, i * 6, passed)
                    for t in range(TILES):
                        wait_alone(sp, rel_out[t], (i + 1) * 16, passed)
                        skew = bass.AP(rel_d.tensor, t * 128 * (PITCH - 1) + SEQ - 1,
                                       [[PITCH - 1, 128], [REL, HEADS], [1, SEQ]])
                        sp.dma_start(pos[:, t, :, :], skew).then_inc(pos_in[t], 16)
                if back:
                    wait_alone(sp, h2_done, j + 1, passed)
                    sp.dma_start(rows_of(h2, j), hres[:, :, :]).then_inc(h2_out, 16)

            program(sp, step)
            sp.wait_ge(h2_out, 16 * STEPS)
            sp.wait_ge(pre_in, 16 * len(experts_pre.loads))

        @block.tensor
        def _(pe):
            def ring_front(s, k):
                wait(pe, front_free, s * FRONT + k - 2)
                return fr[:, k % 3, :]

            def ring_back(s, k):
                before, p = (s, k - 3) if k >= 3 else (s - 1, k - 3 + RING)
                if p < PROJ:
                    wait(pe, o_done, before * 6 + p + 1)
                elif p < X1T:
                    wait(pe, acc_free, before * 6 + p - PROJ + 1)
                elif p < FF2:
                    wait(pe, back_free, before * BACK + 6 + p - X1T + 1)
                elif p < FF2 + TILES:
                    wait(pe, acc_free, before * 6 + 3 + p - FF2 + 1)
                return bk[:, k % 3, :]

            def five(out, lhs, rhs):
                for n, (a, b) in enumerate(zip(lhs, rhs)):
                    m = pe.matmul(out, a, b, start=(n == 0), stop=(n == 4))
                return m

            xs = lambda c: [s_hi[:, c], s_lo[:, c], s_hi[:, c], s_low[:, c], s_tail[:, c]]
            ws = lambda c: [w_hi[:, c], w_hi[:, c], w_lo[:, c], w_low[:, c], w_low[:, c]]
            xf = lambda c: [x_hi[:, c], x_lo[:, c], x_hi[:, c], x_low[:, c], x_tail[:, c]]
            wf = lambda c: [l1_hi[:, c], l1_hi[:, c], l1_lo[:, c], l1_low[:, c], l1_low[:, c]]
            tile = lambda t: slice(128 * t, 128 * t + 128)

            def src_t(s):
                pe.wait_ge(src_rows, s + 1)
                for k in range(2):
                    bank = ring_front(s, k)
                    for t in range(TILES):
                        m = pe.transpose(bank[:, tile(t)], src[:, t, 128 * k:128 * k + 128], ident[:, :])
                    m.then_inc(front_done, 1)

            def qk_proj(s):
                pe.wait_ge(front_free, s * FRONT + 2)
                pe.wait_ge(src_lo, s + 1)
                for k in range(2 * HEADS):
                    bank = ring_front(s, 2 + k)
                    col = (k % 2) * HEADS * DQ + (k // 2) * DQ
                    five(bank[0:DQ, 0:ROWS], ws(slice(col, col + DQ)), xs(slice(0, ROWS))).then_inc(front_done, 1)

            def rel_proj(s, t):
                if t == 0:
                    pe.wait_ge(front_free, s * FRONT + 18)
                bank = ring_front(s, 18 + t)
                for hd in range(HEADS):
                    m = pe.matmul(bank[:, 64 * hd:64 * hd + REL], qk[0:DQ, 0, hd, tile(t)], rel[:, hd, :],
                                  start=True, stop=True)
                m.then_inc(front_done, 1)

            def attend(s, t):
                if t == 0:
                    pe.wait_ge(bd_done, s + 1)
                    pe.wait_ge(front_free, (s + 1) * FRONT)
                for k in (2 * t, 2 * t + 1):
                    bank = ring_back(s, ATT + k)
                    for q in range(4):
                        hd = 4 * (k % 2) + q
                        m = pe.matmul(bank[0:DQ, tile(q)], v[:, k // 2, DQ * hd:DQ * hd + DQ],
                                      bd[:, k // 2 * HEADS + hd, :], start=True, stop=True)
                    m.then_inc(back_done, 1)

            def out_proj(s):
                for t in range(TILES):
                    pe.wait_ge(o_done, s * 6 + 2 * t + 2)
                    bank = ring_back(s, PROJ + t)
                    pe.matmul(bank[:, 0:2 * D], o_hi[:, t, 0, :], wo[:, 0, :], start=True, stop=False)
                    pe.matmul(bank[:, 0:D], o_lo[:, t, 0, :], wo[:, 0, 0:D], start=False, stop=False)
                    for hd in range(1, HEADS):
                        pe.matmul(bank[:, 0:D], o_lo[:, t, hd, :], wo[:, hd, 0:D], start=False, stop=False)
                        m = pe.matmul(bank[:, 0:2 * D], o_hi[:, t, hd, :], wo[:, hd, :], start=False,
                                      stop=(hd == HEADS - 1))
                    m.then_inc(acc_done, 1)

            def v_proj(s):
                for k in range(6):
                    bank = ring_front(s, 21 + k)
                    col = 2 * HEADS * DQ + (k % 2) * 384
                    five(bank[:, 0:384], xs(tile(k // 2)), ws(slice(col, col + 384))).then_inc(front_done, 1)

            def scores(s, ks):
                for k in ks:
                    wait(pe, lg_free, s * 6 + k - 1)
                    for q in range(4):
                        hd = 4 * (k % 2) + q
                        m = pe.matmul(lg[:, k % 2, tile(q)], qk[0:DQ, 0, hd, tile(k // 2)],
                                      qk[0:DQ, 1, hd, tile(k // 2)], start=True, stop=True)
                    m.then_inc(lg_done, 1)

            def x1_t(s):
                pe.wait_ge(x1_norm, s + 1)
                for k in range(2):
                    bank = ring_back(s, X1T + k)
                    for t in range(TILES):
                        m = pe.transpose(bank[:, tile(t)], x1[:, t, 128 * k:128 * k + 128], ident[:, :])
                    m.then_inc(back_done, 1)

            def ffn1(s):
                pe.wait_ge(back_free, s * BACK + 8)
                pe.wait_ge(x1_lo, s + 1)
                for c in range(DFF // 128):
                    bank = ring_back(s, FF1 + c)
                    five(bank[:, 0:ROWS], wf(tile(c)), xf(slice(0, ROWS))).then_inc(back_done, 1)

            def ffn2(s):
                pe.wait_ge(back_free, s * BACK + BACK)
                for t in range(TILES):
                    bank = ring_back(s, FF2 + t)
                    for c in range(DFF // 128):
                        m = pe.matmul(bank[:, 0:D], hT[:, c, tile(t)], lin2[:, c, :],
                                      start=(c == 0), stop=(c == DFF // 128 - 1))
                    m.then_inc(acc_done, 1)

            def step(i, front, back, nxt):
                j, n = i - 1, i + 1
                if front:
                    qk_proj(i)
                for t in range(TILES):
                    if back:
                        attend(j, t)
                    if front:
                        rel_proj(i, t)
                if back:
                    out_proj(j)
                if front:
                    v_proj(i)
                    scores(i, (0, 1))
                if back:
                    x1_t(j)
                if nxt:
                    src_t(n)
                if front:
                    scores(i, (2, 3))
                if back:
                    ffn1(j)
                if front:
                    scores(i, (4, 5))
                if back:
                    ffn2(j)

            def first():
                src_t(0)

            program(pe, step, first)

        @block.scalar
        def _(act):
            def evac(s, k, out, inp, func=ACT.Copy, **kw):
                act.wait_ge(front_done, s * FRONT + k + 1)
                act.activation(out, inp, func, **kw).then_inc(front_free, 1)

            def evac_back(s, k, out, inp, func=ACT.Copy, **kw):
                act.wait_ge(back_done, s * BACK + k + 1)
                act.activation(out, inp, func, **kw).then_inc(back_free, 1)

            def src_hi(s):
                evac(s, 0, s_hi[:, :], fr[:, 0, 0:ROWS])
                evac(s, 1, s_low[:, :], fr[:, 1, 0:ROWS])

            def step(i, front, back, nxt):
                j, n = i - 1, i + 1
                if front:
                    for k in range(2 * HEADS):
                        evac(i, 2 + k, qk[0:DQ, k % 2, k // 2, :], fr[0:DQ, (2 + k) % 3, 0:ROWS])
                for t in range(TILES):
                    if back:
                        for k in (2 * t, 2 * t + 1):
                            evac_back(j, k, o_hi[:, t, 4 * (k % 2):4 * (k % 2) + 4, :],
                                      bk[0:DQ, (ATT + k) % 3, :].rearrange("p (h r) -> p h r", h=4))
                    if front:
                        wait(act, rel_out[t], i * 16)
                        evac(i, 18 + t, relp[:, t, :, :],
                             fr[:, (18 + t) % 3, :].rearrange("p (h m) -> p h m", m=64)[:, :, 0:REL])
                if front:
                    for k in range(6):
                        evac(i, 21 + k, v[:, k // 2, 384 * (k % 2):384 * (k % 2) + 384], fr[:, (21 + k) % 3, 0:384])
                        if k == 2:
                            wait(act, acc_free, i * 6 - 3)
                            act.wait_ge(src_rows, i + 1)
                            act.activation(res[:, :, :], src[:, :, 0:D], ACT.Copy).then_inc(res_done, 1)
                if back:
                    evac_back(j, 6, x_hi[:, :], bk[:, X1T % 3, 0:ROWS])
                    evac_back(j, 7, x_low[:, :], bk[:, (X1T + 1) % 3, 0:ROWS])
                if nxt:
                    src_hi(n)
                if back:
                    for c in range(DFF // 128):
                        evac_back(j, 8 + c, hT[:, c, :], bk[:, (FF1 + c) % 3, 0:ROWS], ACT.Relu, bias=l1b[:, c:c + 1])
                if front:
                    act.wait_ge(sub_done, i + 1)
                    wait(act, bd_done, i)
                    act.activation(prob[:, :, :], logit[:, :, :], ACT.Exp).then_inc(exp_done, 1)

            def first():
                src_hi(0)

            program(act, step, first)

        @block.gpsimd
        def _(pool):
            def power(s, var, rst, out=rstd, of=ve):
                pool.wait_ge(var, s + 1)
                pool.tensor_tensor(out[:, :], of[:, :], mhalf[:, :], ALU.pow).then_inc(rst, 1)

            def src_power(s):
                power(s, var_src, rstd_src, src_rstd, src_ve)

            def step(i, front, back, nxt):
                j, n = i - 1, i + 1
                if back:
                    pool.wait_ge(inv_done, j + 1)
                    pool.tensor_tensor(prob[:, :, :], prob[:, :, :],
                                       sm[:, :].unsqueeze(2).broadcast_to([128, TILES * HEADS, SEQ]),
                                       ALU.mult).then_inc(prob_done, 1)
                if nxt:
                    src_power(n)
                if back:
                    power(j, var_1, rstd_1)
                    pool.wait_ge(x1_norm, j + 1)
                    pool.tensor_tensor(x1b[:, :, :], x1[:, :, 0:D], bcast(LIN2B), ALU.add).then_inc(x1b_done, 1)
                    pool.wait_ge(hres_in, (j + 1) * 16)
                    pool.tensor_tensor(hres[:, :, :], hres[:, :, :], bcast(LN2B), ALU.add).then_inc(hb_done, 1)
                if front:
                    pool.wait_ge(max_done, i + 1)
                    pool.tensor_tensor(logit[:, :, :], logit[:, :, :],
                                       mx[:, :].unsqueeze(2).broadcast_to([128, TILES * HEADS, SEQ]),
                                       ALU.subtract).then_inc(sub_done, 1)
                if back:
                    power(j, var_2, rstd_2)

            def first():
                pool.memset(mhalf[:, :], -0.5)
                pool.memset(bd[:, :, :], 0.0).then_inc(pool_set_up, 1)
                pool.wait_ge(pool_set_up, 1)
                src_power(0)

            program(pool, step, first)

        @block.vector
        def _(dve):
            tail_c = Chain(dve, tail_steps, 1)
            ln1_c, src_c, ln2_c = Chain(dve, ln1_steps, 4), Chain(dve, src_steps, 2), Chain(dve, ln2_steps, 4)

            def moments(chain, rows, var, s, mv=mv, ve=ve):
                for t in range(TILES):
                    ins = dve.bn_stats(bn[:, t, :], rows(t))
                chain.link(ins)
                stand(dve, passed)
                for t in range(TILES):
                    ins = dve.bn_aggr(mv[:, t, :], bn[:, t, :])
                chain.link(ins)
                dve.tensor_scalar(ve[:, :], mv[:, :, 1], EPS, None, ALU.add).then_inc(var, 1)

            def src_moments(s):
                src_c.start(s)
                dve.wait_ge(h_in, (s + 1) * 16)
                moments(src_c, lambda t: h[:, t, :], var_src, s, src_mv, src_ve)
                src_c.end()

            def src_rows_of(s):
                dve.wait_ge(rstd_src, s + 1)
                wait(dve, res_done, s)
                for t in range(TILES):
                    for to, of in ((slice(0, D), slice(0, D)), (slice(D, 256), slice(128, D))):
                        ins = dve.tensor_scalar(src[:, t, to], h[:, t, of], src_mv[:, t, 0:1], src_rstd[:, t:t + 1],
                                                ALU.subtract, ALU.mult)
                ins.then_inc(src_rows, 1)

            def src_lo_of(s):
                dve.wait_ge(front_free, s * FRONT + 2)
                dve.tensor_tensor(s_lo[:, :], fr[:, 0, 0:ROWS], s_hi[:, :].bitcast(F32), ALU.subtract)
                dve.tensor_tensor(s_tail[0:64, :], fr[0:64, 1, 0:ROWS], s_low[0:64, :].bitcast(F32),
                                  ALU.subtract).then_inc(src_lo, 1)

            def softmax_tail(s):
                tail_c.start(s)
                dve.wait_ge(exp_done, s + 1)
                tail_c.link(dve.tensor_reduce(sm[:, :], prob[:, :, :], AX.X, ALU.add))
                tail_c.end()
                dve.reciprocal(sm[:, :], sm[:, :]).then_inc(inv_done, 1)
                dve.wait_ge(prob_done, s + 1)
                wait(dve, back_done, s * BACK - 8)
                for g in range(4):
                    p = slice(32 * g, 32 * g + 32)
                    ins = dve.transpose(bd[p, :, 32 * g:32 * g + 32], prob[p, :, :])
                ins.then_inc(bd_done, 1)

            def add_norm(chain, s, base, use, other, ready, var, rst, gain, plus, out, done, twice=None):
                chain.start(s)
                dve.wait_ge(ready, s + 1)
                for t in range(TILES):
                    bank = bk[:, (use + t) % 3, :]
                    dve.wait_ge(acc_done, s * 6 + base + t + 1)
                    if use == PROJ:
                        dve.tensor_tensor(y[:, t, :], bank[:, D:2 * D], other(t), ALU.add).then_inc(half_done, 1)
                        dve.wait_ge(half_done, s * TILES + t + 1)
                        ins = dve.tensor_tensor(y[:, t, :], bank[:, 0:D], y[:, t, :], ALU.add)
                    else:
                        ins = dve.tensor_tensor(y[:, t, :], bank[:, 0:D], other(t), ALU.add)
                    ins.then_inc(acc_free, 1)
                dve.wait_ge(acc_free, s * 6 + base + 3)
                moments(chain, lambda t: y[:, t, :], var, s)
                for t in range(TILES):
                    ins = dve.scalar_tensor_tensor(y[:, t, :], y[:, t, :], mv[:, t, 0:1], vecs[:, gain, :],
                                                   ALU.subtract, ALU.mult)
                chain.link(ins)
                dve.wait_ge(rst, s + 1)
                for t in range(TILES):
                    ins = dve.scalar_tensor_tensor(out(t), y[:, t, :], rstd[:, t:t + 1], plus(t), ALU.mult, ALU.add)
                    if twice is not None:
                        ins = dve.scalar_tensor_tensor(twice[:, t, D:256], y[:, t, 128:D], rstd[:, t:t + 1],
                                                       plus(t)[:, 128:D], ALU.mult, ALU.add)
                chain.link(ins)
                chain.end()
                dve.sem_inc(done, 1)

            def ln1(s):
                wait(dve, x1b_done, s)
                add_norm(ln1_c, s, 0, PROJ, lambda t: res[:, t, :], res_done, var_1, rstd_1, LN1G,
                         lambda t: vecs[:, LN1B, :], lambda t: x1[:, t, 0:D], x1_norm, x1)

            def ln2(s):
                dve.wait_ge(hb_done, s + 1)
                wait(dve, h2_out, s * 16)
                add_norm(ln2_c, s, 3, FF2, lambda t: x1b[:, t, :], x1b_done, var_2, rstd_2, LN2G,
                         lambda t: hres[:, t, :], lambda t: hres[:, t, :], h2_done)

            def o_lo_of(s):
                for k in range(6):
                    dve.wait_ge(back_free, s * BACK + k + 1)
                    h4 = slice(4 * (k % 2), 4 * (k % 2) + 4)
                    dve.tensor_tensor(o_lo[:, k // 2, h4, :],
                                      bk[0:DQ, (ATT + k) % 3, :].rearrange("p (h r) -> p h r", h=4),
                                      o_hi[:, k // 2, h4, :].bitcast(F32), ALU.subtract).then_inc(o_done, 1)

            def extract(s, ks):
                if ks[0] == 0:
                    wait(dve, exp_done, s)
                for k in ks:
                    dve.wait_ge(lg_done, s * 6 + k + 1)
                    t, h0 = k // 2, 4 * (k % 2)
                    dve.wait_ge(pos_in[t], (s + 1) * 16)
                    for g in range(4):
                        p = slice(32 * g, 32 * g + 32)
                        ins = dve.scalar_tensor_tensor(
                            logit[p, t * HEADS + h0:t * HEADS + h0 + 4, :],
                            lg[p, k % 2, :].rearrange("p (h c) -> p h c", h=4)[:, :, 32 * g:32 * g + 32], SCALE,
                            pos[p, t, h0:h0 + 4, :], ALU.mult, ALU.add)
                    ins.then_inc(lg_free, 1)

            def x1_lo_of(s):
                dve.wait_ge(back_free, s * BACK + 8)
                dve.tensor_tensor(x_lo[:, :], bk[:, X1T % 3, 0:ROWS], x_hi[:, :].bitcast(F32), ALU.subtract)
                dve.tensor_tensor(x_tail[0:64, :], bk[0:64, (X1T + 1) % 3, 0:ROWS], x_low[0:64, :].bitcast(F32),
                                  ALU.subtract).then_inc(x1_lo, 1)

            def step(i, front, back, nxt):
                j, n = i - 1, i + 1
                if back:
                    softmax_tail(j)
                if nxt:
                    src_moments(n)
                if back:
                    o_lo_of(j)
                    ln1(j)
                if nxt:
                    src_rows_of(n)
                if front:
                    extract(i, (0, 1))
                if back:
                    x1_lo_of(j)
                if nxt:
                    src_lo_of(n)
                if front:
                    extract(i, (2, 3, 4, 5))
                    dve.wait_ge(lg_free, (i + 1) * 6)
                    dve.tensor_reduce(mx[:, :], logit[:, :, :], AX.X, ALU.max).then_inc(max_done, 1)
                if back:
                    ln2(j)

            def first():
                dve.memset(s_tail[64:128, :].bitcast(F32), 0.0)
                dve.memset(x_tail[64:128, :].bitcast(F32), 0.0).then_inc(set_up, 1)
                src_moments(0)
                src_rows_of(0)
                src_lo_of(0)
                dve.wait_ge(set_up, 1)
                dve.wait_ge(pool_set_up, 1)

            program(dve, step, first)


def experts_phase(nc, T, h2, out, pre):
    LAG = 3
    ALPHA, LIMIT = 1.702, 7.0
    G2 = EXPERTS // GROUPS
    LAST = NEXP * INNER - (FT - 1) * 128
    with ExitStack() as ctx:
        sb, ps, sem = names(ctx, nc)
        w_hi, w_lo, w_low = [sb("m_" + n, [128, WCOL], F32R) for n in ("w_hi", "w_lo", "w_low")]
        w2, sel_f = sb("m_w2", [128, FT, D]), sb("m_sel_f", [KSEL, FT, 128])
        b13, gate_b, lt4, lt8, ident = pre.b13, pre.gate_b, pre.lt4, pre.lt8, pre.ident
        sel = sb("m_sel", [KSEL, FT, 128], F32R)
        mhalf = sb("m_mhalf", [128, TILES])
        h = sb("m_h", [128, TILES, D])
        hres = sb("m_hres", [128, TILES, D])
        z = sb("m_z", [128, TILES, 256])
        z_hi, z_lo_b, z_low, z_tail = [sb("m_" + n, [128, 2, ROWS], F32R) for n in ("z_hi", "z_lo", "z_low", "z_tail")]
        h1 = sb("m_h1", [128, 2, 2, ROWS])
        hx = sb("m_hx", [128, FT, 2, ROWS])
        sg = sb("m_sg", [128, FT, ROWS])
        gT = sb("m_gT", [128, 2, FT, ROWS])
        wT = sb("m_wT", [64, ROWS], F32R)
        ho = sb("m_ho", [128, TILES, D])
        bn, mv = sb("m_bn", [128, TILES, 6]), sb("m_mv", [128, TILES, 2])
        ve, rstd = sb("m_ve", [128, TILES]), sb("m_rstd", [128, TILES])
        lgt, score, s8, s8m = [sb("m_" + n, [128, TILES, EXPERTS]) for n in ("lgt", "score", "s8", "s8m")]
        w = sb("m_w", [128, TILES, 128])
        m1, gs, cnt4 = sb("m_m1", [128, TILES]), sb("m_gs", [128, TILES, GROUPS]), sb("m_cnt4", [128, TILES, GROUPS])
        cnt8 = sb("m_cnt8", [128, TILES, EXPERTS])
        gt4, ge4 = [sb("m_" + n, [128, TILES, GROUPS, GROUPS]) for n in ("gt4", "ge4")]
        gt8, ge8 = [sb("m_" + n, [128, TILES, EXPERTS, EXPERTS]) for n in ("gt8", "ge8")]
        p1 = ps("m_p1", [128, 2, 512])
        p3 = ps("m_p3", [128, 2, 512])
        ring = ps("m_ring", [128, 4, 512])
        (c_in, hi_done, w_done, ready, pool_ready, h_in, res_in, z_rows, z_norm, z_hi_done, z_lo_done,
         var_done, rstd_done, h1_done, h1_copied, h3_done, hh_done, xg_done, xl_done, sg_done, g1_done, g_done,
         ring_done, ring_free, wt_hi, wt_done, b2_done, add_done, gate_in, gate_exp, gate_w, gate_steps,
         ln_steps, passed) = [
            sem("m_" + n) for n in (
                "c_in hi_done w_done ready pool_ready h_in res_in z_rows z_norm z_hi_done z_lo_done "
                "var_done rstd_done h1_done h1_copied h3_done hh_done xg_done xl_done sg_done g1_done g_done "
                "ring_done ring_free wt_hi wt_done b2_done add_done gate_in gate_exp gate_w gate_steps "
                "ln_steps passed").split()]
        o_out = [sem(f"m_o_out{t}") for t in range(TILES)]
        block = ctx.enter_context(nc.Block())
        tile = lambda t: slice(128 * t, 128 * t + 128)
        chunk = lambda f: slice(512 * f, 512 * f + 512 if f < FT - 1 else WCOL)
        CHUNKS = [FT - 1] + list(range(FT - 1))
        rows_of = lambda t, s: t[bass.ds(s * STEP_TOK, STEP_TOK)].rearrange("b t d -> (b t) d").rearrange(
            "(k p) d -> p k d", p=128)

        WB = [f"WB{f}" for f in range(FT)]
        OUT = [f"OUT{t}" for t in range(TILES)]
        ORDER = WB[0:3] + ["WT", WB[3], "Z0", "Z1", OUT[0], WB[4], "GATE", WB[5], OUT[1], WB[6], OUT[2]]
        OUT_SLOT = (3, 5, 6)
        USES = len(ORDER)
        NEXT = ("Z0", "Z1", "GATE")

        def uses_of(s):
            if s < 0:
                return NEXT
            lacks = (WB[0:LAG] + OUT if s == 0 else []) + (list(NEXT) if s == STEPS - 1 else [])
            return [k for k in ORDER if k not in lacks] if s < STEPS else WB[0:LAG] + OUT

        def use(s, k):
            if isinstance(s, int):
                return sum(len(uses_of(x)) for x in range(-1, s)) + list(uses_of(s)).index(k)
            return s * USES + use(1, k) - USES

        def bank(s, u, k):
            return (use(s, k) if isinstance(s, int) else use(2 - u, k)) % 4

        def weighting(s, f):
            return (True, f + FT - LAG) if f < LAG else (False, f - LAG)

        def program(eng, step, first, last):
            first()
            for s in range(3):
                step(s, s % 2)
            with eng.Fori(1, (STEPS - 3) // 2) as i:
                step(i * 2 + 1, 1)
                step(i * 2 + 2, 0)
            for s in range(1 + 2 * ((STEPS - 3) // 2), STEPS):
                step(s, s % 2)
            last()

        is_last = lambda s: isinstance(s, int) and s == STEPS - 1
        is_first = lambda s: isinstance(s, int) and s == 0

        @block.sync
        def _(sp):
            sp.dma_start(h[:, :, :], rows_of(h2, 0)).then_inc(h_in, 16)
            sp.dma_start(sel_f[:, :, :], T["sel"]).then_inc(c_in, 16)
            sp.dma_start(w2[:, :, :], T["w2"]).then_inc(c_in, 16)

            def step(s, u):
                if not (isinstance(s, int) and s >= STEPS - 2):
                    wait_alone(sp, z_rows, s + 2, passed)
                    sp.dma_start(h[:, :, :], rows_of(h2, s + 2)).then_inc(h_in, 16)
                if not is_first(s):
                    store(s - 1, 4)

            def store(s, rows):
                wait_alone(sp, add_done, s * TILES, passed)
                sp.dma_start(hres[:, :, :], rows_of(h2, s)).then_inc(res_in, 16)
                for t in range(TILES):
                    wait_alone(sp, add_done, s * TILES + t + 1, passed)
                    r = rows if t == TILES - 1 else 4
                    sp.dma_start(out[:, bass.ds(s * STEP_TOK + 4 * t, r), :].rearrange("t b d -> b t d"),
                                 ho[0:32 * r, t, :]).then_inc(o_out[t], 16)

            def last():
                store(STEPS - 1, NTOK - STEP_TOK * (STEPS - 1) - 4 * (TILES - 1))
                for t in range(TILES):
                    sp.wait_ge(o_out[t], 16 * STEPS)

            def first():
                sp.wait_ge(z_rows, 1)
                sp.dma_start(h[:, :, :], rows_of(h2, 1)).then_inc(h_in, 16)

            program(sp, step, first, last)

        @block.tensor
        def _(pe):
            xs = lambda u, c: [z_hi[:, u, c], z_lo_b[:, u, c], z_hi[:, u, c], z_low[:, u, c], z_tail[:, u, c]]
            ws = lambda c: [w_hi[:, c], w_hi[:, c], w_lo[:, c], w_low[:, c], w_low[:, c]]

            def five(out, lhs, rhs):
                for k, (a, b) in enumerate(zip(lhs, rhs)):
                    m = pe.matmul(out, a, b, start=(k == 0), stop=(k == 4))
                return m

            def free_bank(s, u, k):
                wait(pe, ring_free, use(s, k) - 3)
                return ring[:, bank(s, u, k), :]

            def unit(s, u, f):
                n = s * FT + f
                wait(pe, h1_copied, n)
                for half in range(2):
                    m = five(p1[:, half, 0:ROWS], ws(tile(4 * f + half)), xs(u, slice(0, ROWS)))
                m.then_inc(h1_done, 1)
                wait(pe, hh_done, n)
                for half in range(2):
                    m = five(p3[:, half, 0:ROWS], ws(tile(4 * f + 2 + half)), xs(u, slice(0, ROWS)))
                m.then_inc(h3_done, 1)

            def weight(s, u, f, k):
                b = free_bank(s, u, k)
                pe.matmul(b[:, 0:ROWS], sel[:, f, :], wT[0:KSEL, :], start=True, stop=True).then_inc(ring_done, 1)

            def turn_weights(s, u):
                pe.wait_ge(gate_w, s + 1)
                b = free_bank(s, u, "WT")
                for t in range(TILES):
                    m = pe.transpose(b[:, tile(t)], w[:, t, :], ident[:, :])
                m.then_inc(ring_done, 1)

            def turn_rows(s, u):
                pe.wait_ge(z_norm, s + 2)
                for k in range(2):
                    b = free_bank(s, u, f"Z{k}")
                    for t in range(TILES):
                        m = pe.transpose(b[:, tile(t)], z[:, t, 128 * k:128 * k + 128], ident[:, :])
                    m.then_inc(ring_done, 1)

            def gate(s, u):
                pe.wait_ge(z_lo_done, s + 2)
                b = free_bank(s, u, "GATE")
                for t in range(TILES):
                    m = five(b[:, EXPERTS * t:EXPERTS * t + EXPERTS], xs(1 - u, tile(t)), ws(slice(W13, WCOL)))
                m.then_inc(ring_done, 1)

            def second(s, u, t):
                if t == 0:
                    pe.wait_ge(g_done, s * FT)
                    pe.wait_ge(b2_done, s)
                b = free_bank(s, u, OUT[t])
                for f in range(FT):
                    k = 128 if f < FT - 1 else LAST + NEXP
                    m = pe.matmul(b[:, 0:D], gT[0:k, 1 - u, f, tile(t)], w2[0:k, f, :], start=(f == 0),
                                  stop=(f == FT - 1))
                m.then_inc(ring_done, 1)

            def step(s, u):
                for f in range(FT):
                    if is_first(s):
                        pe.wait_ge(w_done, min(f + 2, FT))
                    unit(s, u, f)
                    back, g = weighting(s, f)
                    if not (back and is_first(s)):
                        if f == LAG:
                            pe.wait_ge(wt_done, s + 1)
                        weight(s, u, g, WB[f])
                    if f == 2:
                        turn_weights(s, u)
                    if f == 3 and not is_last(s):
                        turn_rows(s, u)
                    if f in OUT_SLOT and not is_first(s):
                        second(s, u, OUT_SLOT.index(f))
                    if f == 4 and not is_last(s):
                        gate(s, u)

            def first():
                turn_rows(-1, 1)
                pe.wait_ge(c_in, 32)
                pe.wait_ge(w_done, 1)
                gate(-1, 1)

            def last():
                for f in range(LAG):
                    weight(STEPS, STEPS % 2, weighting(STEPS, f)[1], WB[f])
                for t in range(TILES):
                    second(STEPS, STEPS % 2, t)

            program(pe, step, first, last)

        @block.scalar
        def _(act):
            def z_hi_of(s, u):
                for k, dst in enumerate((z_hi, z_low)):
                    act.wait_ge(ring_done, use(s, f"Z{k}") + 1)
                    ins = act.activation(dst[:, 1 - u, :], ring[:, bank(s, u, f"Z{k}"), 0:ROWS], ACT.Copy)
                ins.then_inc(z_hi_done, 1)

            def copy(s, u, f):
                n = s * FT + f
                act.wait_ge(h1_done, n + 1)
                wait(act, hh_done, n - 1)
                for half in range(2):
                    ins = act.activation(h1[:, (FT * u + f) % 2, half, :], p1[:, half, 0:ROWS], ACT.Identity,
                                         bias=b13[:, f, half:half + 1])
                ins.then_inc(h1_copied, 1)

            def sigmoid(n, f):
                act.wait_ge(xg_done, n + 1)
                act.activation(sg[:, f, :], hx[:, f, 0, :], ACT.Sigmoid, scale=ALPHA).then_inc(sg_done, 1)

            def weights_of(s, u):
                act.wait_ge(ring_done, use(s, WB[2]) + 1)
                behind = slice(LAST, LAST + NEXP)
                act.activation(gT[behind, 1 - u, FT - 1, :], ring[behind, bank(s, u, WB[2]), 0:ROWS],
                               ACT.Copy).then_inc(b2_done, 1)

            def gate_exp_of(s):
                act.wait_ge(gate_in, s + 1)
                act.activation(score[:, :, :], lgt[:, :, :], ACT.Exp).then_inc(gate_exp, 1)

            def step(s, u):
                for f in range(FT):
                    copy(s, u, f)
                    if f == 2 and not is_first(s):
                        weights_of(s, u)
                    if f == 5 and not is_last(s):
                        gate_exp_of(s + 1)
                    if f:
                        sigmoid(s * FT + f - 1, f - 1)
                    elif not is_first(s):
                        sigmoid(s * FT - 1, FT - 1)
                    if f == 2:
                        act.wait_ge(ring_done, use(s, "WT") + 1)
                        act.activation(wT[:, :], ring[0:64, bank(s, u, "WT"), 0:ROWS], ACT.Copy).then_inc(wt_hi, 1)
                    if f == 3 and not is_last(s):
                        z_hi_of(s, u)

            def first():
                for f in CHUNKS:
                    c = chunk(f)
                    act.activation(w_hi[:, c], pre.raw_a[:, c], ACT.Copy)
                    act.activation(w_low[:, c], pre.raw_b[:, c], ACT.Copy).then_inc(hi_done, 1)
                z_hi_of(-1, 1)
                act.wait_ge(c_in, 32)
                act.activation(sel[:, :, :], sel_f[:, :, :], ACT.Copy).then_inc(hi_done, 1)
                gate_exp_of(0)

            def last():
                sigmoid(STEPS * FT - 1, FT - 1)
                weights_of(STEPS, STEPS % 2)

            program(act, step, first, last)

        @block.gpsimd
        def _(pool):
            def clip(n, f):
                pool.wait_ge(hh_done, n + 1)
                stand(pool, passed)
                pool.tensor_scalar(hx[:, f, 1, :], hx[:, f, 1, :], LIMIT, -LIMIT, ALU.min, ALU.max).then_inc(xl_done, 1)

            def product(n, f, s, u, k):
                p = 128 if f < FT - 1 else LAST
                pool.wait_ge(g1_done, n + 1)
                pool.wait_ge(ring_free, use(s, k) + 1)
                if f == 0 and not (isinstance(s, int) and s < 2):
                    pool.wait_ge(ring_done, use(s - 1, OUT[TILES - 1]) + 1)
                pool.tensor_tensor(gT[0:p, u, f, :], hx[0:p, f, 1, :], sg[0:p, f, :], ALU.mult).then_inc(g_done, 1)

            def step(s, u):
                for f in range(FT):
                    clip(s * FT + f, f)
                    if f == 4 and not (isinstance(s, int) and s >= STEPS - 2):
                        power(s + 2)
                    back, g = weighting(s, f)
                    if not (back and is_first(s)):
                        product(s * FT + f - LAG, g, s, 1 - u if back else u, WB[f])
                    if f == 0 and not is_last(s):
                        double(s + 1)

            def power(s):
                pool.wait_ge(var_done, s + 1)
                pool.tensor_tensor(rstd[:, :], ve[:, :], mhalf[:, :], ALU.pow).then_inc(rstd_done, 1)

            def double(s):
                pool.wait_ge(z_rows, s + 1)
                stand(pool, passed)
                pool.tensor_copy(z[:, :, 192:256], z[:, :, 128:192]).then_inc(z_norm, 1)

            def first():
                pool.memset(mhalf[:, :], -0.5).then_inc(pool_ready, 1)
                pool.wait_ge(pool_ready, 1)
                power(0)
                double(0)
                power(1)

            def last():
                for f in range(LAG):
                    product(STEPS * FT + f - LAG, weighting(STEPS, f)[1], STEPS, (STEPS - 1) % 2, WB[f])

            program(pool, step, first, last)

        @block.vector
        def _(dve):
            ln_c, gate_c = Chain(dve, ln_steps, 2), Chain(dve, gate_steps, 16)

            def moments(s):
                ln_c.start(s)
                dve.wait_ge(h_in, (s + 1) * 16)
                for t in range(TILES):
                    ins = dve.bn_stats(bn[:, t, :], h[:, t, :])
                ln_c.link(ins)
                stand(dve, passed)
                for t in range(TILES):
                    ins = dve.bn_aggr(mv[:, t, :], bn[:, t, :])
                ln_c.link(ins)
                ln_c.end()
                dve.tensor_scalar(ve[:, :], mv[:, :, 1], EPS, None, ALU.add).then_inc(var_done, 1)

            def normalise(s):
                dve.wait_ge(rstd_done, s + 1)
                if not is_first(s):
                    dve.wait_ge(z_lo_done, s)
                for t in range(TILES):
                    ins = dve.tensor_scalar(z[:, t, 0:D], h[:, t, :], mv[:, t, 0:1], rstd[:, t:t + 1],
                                            ALU.subtract, ALU.mult)
                ins.then_inc(z_rows, 1)

            def z_lo_of(s, u):
                dve.wait_ge(z_hi_done, s + 2)
                dve.tensor_tensor(z_lo_b[:, 1 - u, :], ring[:, bank(s, u, "Z0"), 0:ROWS],
                                  z_hi[:, 1 - u, :].bitcast(F32), ALU.subtract).then_inc(ring_free, 1)
                dve.tensor_tensor(z_tail[0:64, 1 - u, :], ring[0:64, bank(s, u, "Z1"), 0:ROWS],
                                  z_low[0:64, 1 - u, :].bitcast(F32), ALU.subtract).then_inc(ring_free, 1)
                dve.wait_ge(ring_free, use(s, "Z1") + 1)
                dve.sem_inc(z_lo_done, 1)

            def product(s, u, f):
                n = s * FT + f
                dve.wait_ge(h1_copied, n + 1)
                dve.wait_ge(h3_done, n + 1)
                wait(dve, g_done, n - FT + 1)
                for half in range(2):
                    ins = dve.scalar_tensor_tensor(hx[:, f, half, :], p3[:, half, 0:ROWS], b13[:, f, 2 + half:3 + half],
                                                   h1[:, (FT * u + f) % 2, half, :], ALU.add, ALU.mult)
                ins.then_inc(hh_done, 1)
                dve.wait_ge(hh_done, n + 1)
                dve.tensor_scalar(hx[:, f, 0, :], hx[:, f, 0, :], LIMIT, None, ALU.min).then_inc(xg_done, 1)

            def weigh(n, f, s, u, k):
                dve.wait_ge(xl_done, n + 1)
                dve.wait_ge(xg_done, n + 1)
                dve.scalar_tensor_tensor(hx[:, f, 1, :], hx[:, f, 1, :], 1.0, hx[:, f, 0, :], ALU.add,
                                         ALU.mult).then_inc(g1_done, 1)
                p, b = 128, ring[:, bank(s, u, k), :]
                dve.wait_ge(ring_done, use(s, k) + 1)
                if f == FT - 1:
                    p = LAST
                    dve.wait_ge(b2_done, s)
                dve.wait_ge(sg_done, n + 1)
                dve.tensor_tensor(sg[0:p, f, :], sg[0:p, f, :], b[0:p, 0:ROWS], ALU.mult).then_inc(ring_free, 1)

            def residual(s, u, t):
                dve.wait_ge(res_in, s * 16)
                dve.wait_ge(ring_done, use(s, OUT[t]) + 1)
                wait(dve, o_out[t], (s - 1) * 16)
                dve.tensor_tensor(ho[:, t, :], ring[:, bank(s, u, OUT[t]), 0:D], hres[:, t, :], ALU.add).then_inc(
                    ring_free, 1)
                dve.wait_ge(ring_free, use(s, OUT[t]) + 1)
                dve.sem_inc(add_done, 1)

            def before(a, count):
                shape = [128, TILES, count, count]
                return a.unsqueeze(2).broadcast_to(shape), a.unsqueeze(3).broadcast_to(shape)

            def rank(a, count, gt, ge, lt, cnt):
                aj, ai = before(a, count)
                dve.tensor_tensor(gt[:, :, :, :], aj, ai, ALU.is_gt)
                gate_c.link(dve.tensor_tensor(ge[:, :, :, :], aj, ai, ALU.is_ge))
                gate_c.link(dve.tensor_tensor(ge[:, :, :, :], ge[:, :, :, :], lt[:, :, :].unsqueeze(1).broadcast_to(
                    [128, TILES, count, count]), ALU.mult))
                gate_c.link(dve.tensor_tensor(gt[:, :, :, :], gt[:, :, :, :], ge[:, :, :, :], ALU.max))
                gate_c.link(dve.tensor_reduce(cnt[:, :, :], gt[:, :, :, :], AX.X, ALU.add))

            def gate_logits(s, u):
                gate_c.start(s + 1)
                dve.wait_ge(ring_done, use(s, "GATE") + 1)
                dve.tensor_copy(lgt[:, :, :], ring[:, bank(s, u, "GATE"), 0:TILES * EXPERTS].rearrange(
                    "p (t e) -> p t e", t=TILES)).then_inc(ring_free, 1)
                dve.wait_ge(ring_free, use(s, "GATE") + 1)
                gate_c.link(dve.tensor_reduce(m1[:, :], lgt[:, :, :], AX.X, ALU.max))
                dve.tensor_tensor(lgt[:, :, :], lgt[:, :, :], m1[:, :].unsqueeze(2).broadcast_to(
                    [128, TILES, EXPERTS]), ALU.subtract).then_inc(gate_in, 1)

            def gate_groups(s):
                wide = [128, TILES, EXPERTS]
                gate_c.start(s, 1)
                dve.wait_ge(gate_exp, s + 1)
                gate_c.link(dve.tensor_reduce(m1[:, :], score[:, :, :], AX.X, ALU.add))
                gate_c.link(dve.reciprocal(m1[:, :], m1[:, :]))
                gate_c.link(dve.tensor_tensor(score[:, :, :], score[:, :, :], m1[:, :].unsqueeze(2).broadcast_to(
                    wide), ALU.mult))
                gate_c.link(dve.tensor_tensor(s8[:, :, :], score[:, :, :], gate_b[:, :].unsqueeze(1).broadcast_to(
                    wide), ALU.add))
                gate_c.link(dve.tensor_reduce(gs[:, :, :], s8[:, :, :].rearrange("p t (g e) -> p t g e", e=G2),
                                              AX.X, ALU.add))
                rank(gs[:, :, :], GROUPS, gt4, ge4, lt4, cnt4)
                gate_c.link(dve.tensor_scalar(cnt4[:, :, :], cnt4[:, :, :], 2.0, -BIG, ALU.is_ge, ALU.mult))
                gate_c.link(dve.tensor_tensor(
                    s8m[:, :, :].rearrange("p t (g e) -> p t g e", e=G2),
                    s8[:, :, :].rearrange("p t (g e) -> p t g e", e=G2),
                    cnt4[:, :, :].unsqueeze(3).broadcast_to([128, TILES, GROUPS, G2]), ALU.add))

            def gate_experts(s):
                gate_c.start(s, 12)
                rank(s8m[:, :, :], EXPERTS, gt8, ge8, lt8, cnt8)
                gate_c.end()
                wait(dve, wt_hi, s)
                for at in (0, 32):
                    ins = dve.scalar_tensor_tensor(w[:, :, at:at + EXPERTS], cnt8[:, :, :], 2.0, score[:, :, :],
                                                   ALU.is_lt, ALU.mult)
                ins.then_inc(gate_w, 1)

            def step(s, u):
                for f in range(FT):
                    product(s, u, f)
                    back, g = weighting(s, f)
                    if not (back and is_first(s)):
                        weigh(s * FT + f - LAG, g, s, u, WB[f])
                    if f == 2:
                        dve.wait_ge(wt_hi, s + 1)
                        dve.tensor_tensor(wT[32:64, :], ring[32:64, bank(s, u, "WT"), 0:ROWS],
                                          wT[32:64, :].bitcast(F32), ALU.subtract).then_inc(ring_free, 1)
                        dve.wait_ge(ring_free, use(s, "WT") + 1)
                        dve.sem_inc(wt_done, 1)
                    if f == 3 and not is_last(s):
                        z_lo_of(s, u)
                    if f in OUT_SLOT and not is_first(s):
                        residual(s, u, OUT_SLOT.index(f))
                    if f == 4 and not (isinstance(s, int) and s >= STEPS - 2):
                        moments(s + 2)
                    if not is_last(s):
                        if f == 0:
                            normalise(s + 1)
                        if f == 4:
                            gate_logits(s, u)
                        if f == 5:
                            gate_groups(s + 1)
                        if f == 6:
                            gate_experts(s + 1)

            def first():
                dve.memset(z_tail[64:128, :, :].bitcast(F32), 0.0)
                dve.memset(w[:, :, :], 0.0).then_inc(ready, 1)
                dve.wait_ge(ready, 1)
                for at in (EXPERTS, 32 + EXPERTS):
                    ins = dve.memset(w[:, :, at:at + 1], 1.0)
                ins.then_inc(ready, 1)

                def split(ns):
                    for n in ns:
                        c = chunk(CHUNKS[n])
                        dve.wait_ge(hi_done, n + 1)
                        dve.tensor_tensor(w_lo[:, c], pre.raw_a[:, c], w_hi[:, c].bitcast(F32), ALU.subtract)
                        dve.tensor_tensor(w_low[64:128, c], pre.raw_b[64:128, c], w_low[64:128, c].bitcast(F32),
                                          ALU.subtract).then_inc(w_done, 1)

                split((0,))
                moments(0)
                split((1,))
                normalise(0)
                split((2, 3, 4))
                z_lo_of(-1, 1)
                split(range(5, FT))
                dve.wait_ge(ready, 2)
                moments(1)
                gate_logits(-1, 1)
                gate_groups(0)
                gate_experts(0)

            def last():
                for f in range(LAG):
                    weigh(STEPS * FT + f - LAG, weighting(STEPS, f)[1], STEPS, STEPS % 2, WB[f])
                for t in range(TILES):
                    residual(STEPS, STEPS % 2, t)

            program(dve, step, first, last)


def build(nc, T, out):
    hs = nc.dram_tensor("hs", (PADTOK, SEQ, D), F32, kind="Internal").ap()
    h2 = nc.dram_tensor("h2", (PADTOK, SEQ, D), F32, kind="Internal").ap()
    with ExitStack() as ctx:
        sb, _, _ = names(ctx, nc)
        ident = sb("ident", [128, 128])
        experts = expert_weights(sb, ident)
        with ExitStack() as inner:
            attention = attention_weights(names(inner, nc)[0], ident)
            embed_phase(nc, T, hs, attention)
            attention_phase(nc, T, hs, h2, attention, experts)
        experts_phase(nc, T, h2, out, experts)


def layouts(a):
    import numpy as np
    f = np.float32
    L = {}
    x = np.pad(a["x"], ((0, 0), (0, 0), (1, 1), (1, 1)))
    cols = PATCH * np.arange(GRID)[:, None] + np.arange(PATCH + 2)
    x = x[:, :, :, cols][:, :, cols]
    x = x.transpose(1, 3, 2, 4, 0, 5).reshape(3, PATCH + 2, NPATCH // 4, 128, 2, HALF)
    x = np.concatenate([x[:, 1:17].reshape(48, *x.shape[2:]), x[:, 0], x[:, 17]])
    L["xw"] = x.transpose(1, 3, 0, 2, 4).reshape(NPATCH // 4, 2 * WIN, 128 * HALF)
    full = np.concatenate([a["L0_tok_W"], a["L0_tok_ln_gamma"][:, None], a["L0_tok_ln_beta"][:, None]], axis=1)
    full = full.reshape(PATCH, PATCH, 5, 3, D + 2)
    sw = np.zeros((5, 3, PATCH + 2, PATCH + 2, D + 2), f)
    cw = np.zeros((3, PATCH + 2, PATCH + 2), f)
    for s, (dy, dx) in enumerate([(0, 0), (0, -1), (0, 1), (-1, 0), (1, 0)]):
        sw[s, :, 1 + dy:17 + dy, 1 + dx:17 + dx] = full[:, :, s].transpose(2, 0, 1, 3)
        cw[:, 1 + dy:17 + dy, 1 + dx:17 + dx] += 1
    def window(w):
        lead = w.shape[:-4]
        w = np.concatenate([w[..., :, 1:17, :, :].reshape(*lead, 48, 18, w.shape[-1]), w[..., :, 0, :, :],
                            w[..., :, 17, :, :]], axis=-3)
        gap = np.zeros((*lead, 10, HALF, w.shape[-1]), f)
        return np.concatenate([w[..., 0:HALF, :], gap, w[..., HALF:, :]], axis=-3)
    L["shift_w"] = window(sw)
    L["count_w"] = window(cw[..., None])[..., 0]
    L["count_rt"] = np.sqrt(L["count_w"][:, [4, 0, 1, 7, 8]])
    L["tok_b"] = a["L0_tok_b"].reshape(1, D)
    L["txt"] = a["txt"]
    q = np.concatenate([a["L0_attn_" + n].transpose(1, 0, 2).reshape(D, HEADS * DQ) for n in ("w_q", "w_k", "w_v")], 1)
    two = lambda w: (w[0:128], np.concatenate([w[128:], w[128:]]))
    L["wqkv_a"], L["wqkv_b"] = two(q)
    L["lin1_a"], L["lin1_b2"] = two(a["L0_attn_lin1_w"].T)
    L["wo"] = a["L0_attn_w_o"].transpose(1, 0, 2)
    L["lin2"] = a["L0_attn_lin2_w"].T.reshape(DFF // 128, 128, D).transpose(1, 0, 2)
    mid = a["L0_attn_rel_emb"].shape[1] // 2
    L["rel"] = a["L0_attn_rel_emb"][:, mid - SEQ + 1:mid + SEQ, :, 0].transpose(2, 0, 1)
    L["ident"] = np.eye(128, dtype=f)
    L["lin1_bias"] = a["L0_attn_lin1_b"].reshape(DFF // 128, 128).T
    L["vecs"] = np.stack([a["L0_attn_" + n] for n in ("ln1_g", "ln1_b", "ln2_g", "ln2_b", "lin2_b")])[None]
    F = {n: a["L0_ffn_" + n] for n in "gate_w gate_b W1 B1 W3 B3 W2 B2 Ws1 Bs1 Ws3 Bs3 Ws2 Bs2".split()}
    cat = lambda w, shared: np.concatenate([w, shared[None]])
    def by_tiles(w):
        w = np.stack([w[..., 0::2], w[..., 1::2]])
        w = w.transpose(0, 2, 1, 3).reshape(2, w.shape[2], NEXP * INNER)
        return np.pad(w, ((0, 0), (0, 0), (0, FT * 128 - NEXP * INNER))).reshape(2, -1, FT, 128)
    def both(w1, w3):
        w = np.concatenate([by_tiles(w1), by_tiles(w3)])
        return w.transpose(1, 2, 0, 3).reshape(w.shape[1], W13)
    w13 = both(cat(F["W1"], F["Ws1"]), cat(F["W3"], F["Ws3"]))
    L["w13_a"], L["w13_b"] = two(np.concatenate([w13, F["gate_w"].T], 1))
    b13 = both(cat(F["B1"], F["Bs1"])[:, None], cat(F["B3"], F["Bs3"])[:, None])
    L["b13"] = b13.reshape(FT, 4, 128).transpose(2, 0, 1)
    w2 = np.concatenate([cat(F["W2"], F["Ws2"]).reshape(NEXP * INNER, D), cat(F["B2"], F["Bs2"])])
    L["w2"] = np.pad(w2, ((0, FT * 128 - len(w2)), (0, 0))).reshape(FT, 128, D).transpose(1, 0, 2)
    sel = np.zeros((32 + NEXP, FT * 128), f)
    for e in range(NEXP):
        for row in (e, 32 + e):
            sel[row, e * INNER:(e + 1) * INNER] = 1
            sel[row, NEXP * INNER + e] = 1
    L["sel"] = sel.reshape(-1, FT, 128)
    L["gate_b"] = F["gate_b"][None]
    for n in (GROUPS, EXPERTS):
        L[f"lt{n}"] = np.broadcast_to(np.tril(np.ones((n, n), f), -1), (128, n, n))
    return L


def kernel(**inputs):
    import numpy as _np
    import concourse.bacc as _bacc
    from concourse.bass_utils import run_bass_kernel_spmd as _run

    nc = _bacc.Bacc("TRN2", target_bir_lowering=False, num_devices=1)
    arrays, T = {}, {}
    for name, a in layouts({k: _np.asarray(v) for k, v in inputs.items()}).items():
        a = _np.ascontiguousarray(a)
        arrays[f"in_{name}"] = a
        T[name] = nc.dram_tensor(f"in_{name}", a.shape, mybir.dt.from_np(a.dtype), kind="ExternalInput").ap()
    out = nc.dram_tensor("out", (SEQ, NTOK, D), F32, kind="ExternalOutput").ap()
    build(nc, T, out)
    r = _run(nc, [arrays], core_ids=[0])
    return r.results[0]["out"]
```
